# Optimizing a Trainium2 kernel written in Bass

```python
import numpy as np
import jax
import jax.numpy as jnp

def _softmax(x, axis=-1):
    return jax.nn.softmax(x, axis=axis)

def _gelu(x):
    return jax.nn.gelu(x, approximate=True)

def _silu(x):
    return jax.nn.silu(x)

def _sigmoid(x):
    return jax.nn.sigmoid(x)

def _layernorm(x, axis=-1, eps=1e-05):
    m = jnp.mean(x, axis=axis, keepdims=True)
    v = jnp.var(x, axis=axis, keepdims=True)
    return (x - m) / jnp.sqrt(v + eps)

def _scatter_add(tgt, idx, src, axis=0):
    return tgt.at[idx].add(src)

def _segment_sum(src, seg, n):
    return jax.ops.segment_sum(src, seg, n)
kernel_name = 'mk_flamingo_gated_d2_seqx_r4_a59817'

def setup_inputs(seed: int=0):
    np.random.seed(seed)
    _w = jnp.asarray

    def _rec_inputs():
        import jax
        import jax.numpy as jnp
        _rk = jax.random.key(seed)
        x = 7.22e-05 + 1 * jax.random.normal(jax.random.fold_in(_rk, 1), (8, 512, 256), jnp.float32)
        _lenS = 512 - jax.random.randint(jax.random.fold_in(_rk, 7), (8,), 0, max(1, 512 // 4) + 1, jnp.int32)
        _lenS2 = 512 - jax.random.randint(jax.random.fold_in(_rk, 8), (8,), 0, max(1, 512 // 4) + 1, jnp.int32)
        _ctx_1024P = jax.random.normal(jax.random.fold_in(_rk, 11), (8, 16, 256), jnp.float32)
        _ctx_1024c = jax.random.dirichlet(jax.random.fold_in(_rk, 511), 0.3 * jnp.ones((16,), jnp.float32), (8, 512))
        _ctx_1024t = jnp.einsum('bsk,bkd->bsd', _ctx_1024c, _ctx_1024P)
        _ctx_1024t = _ctx_1024t * jax.lax.rsqrt(jnp.mean(jnp.square(_ctx_1024t)) + 1e-12) * 0.953939
        ctx_1024 = 4.13588e-05 + 0.999923 * (_ctx_1024t + 0.3 * jax.random.normal(jax.random.fold_in(_rk, 611), (8, 512, 256), jnp.float32))
        _validS = jnp.arange(512)[None, :] < _lenS[:, None]
        _validS2 = jnp.arange(512)[None, :] < _lenS2[:, None]
        _causal = jnp.tril(jnp.ones((512, 512), dtype=bool))
        mask_BxS2_ff0 = jnp.where(jnp.ones((8, 512), dtype=bool), 0.0, -1000000000.0).astype(jnp.float32)
        mask_Bx1xS_if1 = jnp.where(jnp.ones((8, 1, 512), dtype=bool), 1, 0).astype(jnp.int32)
        _g = jax.random.normal(jax.random.fold_in(_rk, 9001), (2, 2), jnp.float32)
        _g = jnp.sign(_g) * jnp.maximum(jnp.abs(_g), 1.0) + (_g == 0) * 1.0
        g_xattn = _g[0]
        g_ffn = _g[1]
        return (x, ctx_1024, mask_BxS2_ff0, mask_Bx1xS_if1, g_xattn, g_ffn)
    x, ctx_1024, mask_BxS2_ff0, mask_Bx1xS_if1, g_xattn, g_ffn = _rec_inputs()

    def _L0_xattn_setup():
        import jax, jax.numpy as jnp
        import numpy as np
        D_MODEL = 256
        N_HEAD = 16
        HEAD_DIM = D_MODEL // N_HEAD
        key = jax.random.key(seed)
        ks = jax.random.split(key, 12)
        B, S, D = (4, 512, D_MODEL)
        scale = 1.0 / np.sqrt(D)
        inp = {'q': jax.random.normal(ks[0], (B, S, D), jnp.float32), 'k': jax.random.normal(ks[1], (B, S, D), jnp.float32), 'v': jax.random.normal(ks[2], (B, S, D), jnp.float32), 'attention_mask': jnp.zeros((B, S), jnp.float32), 'Wq': jax.random.normal(ks[3], (D, D), jnp.float32) * scale, 'bq': jnp.zeros((D,), jnp.float32), 'Wk': jax.random.normal(ks[4], (D, D), jnp.float32) * scale, 'bk': jnp.zeros((D,), jnp.float32), 'Wv': jax.random.normal(ks[5], (D, D), jnp.float32) * scale, 'bv': jnp.zeros((D,), jnp.float32), 'Wp': jax.random.normal(ks[6], (D, D), jnp.float32) * scale, 'bp': jnp.zeros((D,), jnp.float32)}
        return inp
    _L0_xattn_all = _L0_xattn_setup()
    _L0_xattn_in = {k: v for k, v in _L0_xattn_all.items() if k in ('Wq', 'bq', 'Wk', 'bk', 'Wv', 'bv', 'Wp', 'bp')}
    del _L0_xattn_all

    def _L0_ffn_setup():
        import jax, jax.numpy as jnp
        import numpy as np
        TOP_K = 8
        NUM_EXPERTS = 32
        CAPACITY = 256
        key = jax.random.key(seed)
        k1, k2, k3, k4 = jax.random.split(key, 4)
        B, S, H, E, F = (2, 256, 256, NUM_EXPERTS, 192)
        return {'hidden_states': jax.random.normal(k1, (B, S, H), dtype=jnp.float32), 'gate_weight': jax.random.normal(k2, (E, H), dtype=jnp.float32) * 0.02, 'gate_up_proj': jax.random.normal(k3, (E, 2 * F, H), dtype=jnp.float32) * 0.02, 'down_proj': jax.random.normal(k4, (E, H, F), dtype=jnp.float32) * 0.02}
    _L0_ffn_all = _L0_ffn_setup()
    _L0_ffn_in = {k: v for k, v in _L0_ffn_all.items() if k in ('gate_weight', 'gate_up_proj', 'down_proj')}
    del _L0_ffn_all

    def _L1_xattn_setup():
        import math
        import jax, jax.numpy as jnp
        import numpy as np
        B, S, E, H = (2, 512, 256, 16)
        D = E // H
        key = jax.random.key(seed)
        ks = jax.random.split(key, 12)
        sc = 1.0 / math.sqrt(E)
        inp = {'q': jax.random.normal(ks[0], (B, S, E), jnp.float32), 'k': jax.random.normal(ks[1], (B, S, E), jnp.float32), 'v': jax.random.normal(ks[2], (B, S, E), jnp.float32), 'mask': jnp.ones((B, 1, S), jnp.int32), 'Wq': jax.random.normal(ks[3], (E, E), jnp.float32) * sc, 'bq': jnp.zeros((E,), jnp.float32), 'Wk': jax.random.normal(ks[4], (E, E), jnp.float32) * sc, 'bk': jnp.zeros((E,), jnp.float32), 'Wv': jax.random.normal(ks[5], (E, E), jnp.float32) * sc, 'bv': jnp.zeros((E,), jnp.float32), 'Wo': jax.random.normal(ks[6], (E, E), jnp.float32) * sc, 'bo': jnp.zeros((E,), jnp.float32)}
        return inp
    _L1_xattn_all = _L1_xattn_setup()
    _L1_xattn_in = {k: v for k, v in _L1_xattn_all.items() if k in ('Wq', 'bq', 'Wk', 'bk', 'Wv', 'bv', 'Wo', 'bo')}
    del _L1_xattn_all

    def _L1_ffn_setup():
        import jax, jax.numpy as jnp
        import numpy as np
        B, S, D = (2, 512, 256)
        E, K, H = (8, 2, 1024)
        CAP_FACTOR = 1.0

        def _moe_forward(x, wg, w1, b1, w2, b2):
            Bb, Ss, Dd = x.shape
            T = Bb * Ss
            cap = int(K * CAP_FACTOR * ((T + E - 1) // E))
            xt = x.reshape(T, Dd)
            logits = xt @ wg
            scores = jax.nn.softmax(logits, axis=-1)
            gates_k, idx_k = jax.lax.top_k(scores, K)
            gates_k = gates_k / jnp.sum(gates_k, axis=-1, keepdims=True)
            masks = jax.nn.one_hot(idx_k, E, dtype=jnp.int32)
            m = jnp.transpose(masks, (1, 0, 2)).reshape(K * T, E)
            locs_full = jnp.cumsum(m, axis=0) - 1
            loc = jnp.sum(locs_full * m, axis=-1)
            loc = loc.reshape(K, T).T
            valid = (loc < cap).astype(xt.dtype)
            loc_c = jnp.clip(loc, 0, cap - 1)
            contrib = (xt[:, None, :] * valid[:, :, None]).reshape(T * K, Dd)
            disp = jnp.zeros((E, cap, Dd), xt.dtype)
            disp = disp.at[idx_k.reshape(-1), loc_c.reshape(-1)].add(contrib)
            h = jax.nn.relu(jnp.einsum('ecd,edh->ech', disp, w1) + b1[:, None, :])
            out = jnp.einsum('ech,ehd->ecd', h, w2) + b2[:, None, :]
            gathered = out[idx_k, loc_c]
            y = jnp.einsum('tk,tkd->td', gates_k * valid, gathered)
            return y.reshape(Bb, Ss, Dd)
        key = jax.random.key(seed)
        ks = jax.random.split(key, 6)
        scale_in = 1.0 / np.sqrt(D)
        scale_h = 1.0 / np.sqrt(H)
        return {'x': jax.random.normal(ks[0], (B, S, D), jnp.float32), 'wg': jax.random.normal(ks[1], (D, E), jnp.float32) * scale_in, 'w1': jax.random.normal(ks[2], (E, D, H), jnp.float32) * scale_in, 'b1': jnp.zeros((E, H), jnp.float32), 'w2': jax.random.normal(ks[3], (E, H, D), jnp.float32) * scale_h, 'b2': jnp.zeros((E, D), jnp.float32)}
    _L1_ffn_all = _L1_ffn_setup()
    _L1_ffn_in = {k: v for k, v in _L1_ffn_all.items() if k in ('wg', 'w1', 'b1', 'w2', 'b2')}
    del _L1_ffn_all
    return {'x': x, 'ctx_1024': ctx_1024, 'mask_BxS2_ff0': mask_BxS2_ff0, 'mask_Bx1xS_if1': mask_Bx1xS_if1, 'g_xattn': g_xattn, 'g_ffn': g_ffn, 'L0_xattn_Wq': _L0_xattn_in['Wq'], 'L0_xattn_bq': _L0_xattn_in['bq'], 'L0_xattn_Wk': _L0_xattn_in['Wk'], 'L0_xattn_bk': _L0_xattn_in['bk'], 'L0_xattn_Wv': _L0_xattn_in['Wv'], 'L0_xattn_bv': _L0_xattn_in['bv'], 'L0_xattn_Wp': _L0_xattn_in['Wp'], 'L0_xattn_bp': _L0_xattn_in['bp'], 'L0_ffn_gate_weight': _L0_ffn_in['gate_weight'], 'L0_ffn_gate_up_proj': _L0_ffn_in['gate_up_proj'], 'L0_ffn_down_proj': _L0_ffn_in['down_proj'], 'L1_xattn_Wq': _L1_xattn_in['Wq'], 'L1_xattn_bq': _L1_xattn_in['bq'], 'L1_xattn_Wk': _L1_xattn_in['Wk'], 'L1_xattn_bk': _L1_xattn_in['bk'], 'L1_xattn_Wv': _L1_xattn_in['Wv'], 'L1_xattn_bv': _L1_xattn_in['bv'], 'L1_xattn_Wo': _L1_xattn_in['Wo'], 'L1_xattn_bo': _L1_xattn_in['bo'], 'L1_ffn_wg': _L1_ffn_in['wg'], 'L1_ffn_w1': _L1_ffn_in['w1'], 'L1_ffn_b1': _L1_ffn_in['b1'], 'L1_ffn_w2': _L1_ffn_in['w2'], 'L1_ffn_b2': _L1_ffn_in['b2']}

def reference(x, ctx_1024, mask_BxS2_ff0, mask_Bx1xS_if1, g_xattn, g_ffn, L0_xattn_Wq, L0_xattn_bq, L0_xattn_Wk, L0_xattn_bk, L0_xattn_Wv, L0_xattn_bv, L0_xattn_Wp, L0_xattn_bp, L0_ffn_gate_weight, L0_ffn_gate_up_proj, L0_ffn_down_proj, L1_xattn_Wq, L1_xattn_bq, L1_xattn_Wk, L1_xattn_bk, L1_xattn_Wv, L1_xattn_bv, L1_xattn_Wo, L1_xattn_bo, L1_ffn_wg, L1_ffn_w1, L1_ffn_b1, L1_ffn_w2, L1_ffn_b2):
    import jax
    import jax.numpy as jnp

    def _L0_xattn_ref(q, k, v, attention_mask, Wq, bq, Wk, bk, Wv, bv, Wp, bp):
        import jax, jax.numpy as jnp
        import numpy as np
        D_MODEL = 256
        N_HEAD = 16
        HEAD_DIM = D_MODEL // N_HEAD
        B, S, D = q.shape
        H, Dh = (N_HEAD, HEAD_DIM)
        wq = (q @ Wq + bq).reshape(B, S, H, Dh).transpose(0, 2, 1, 3)
        wk = (k @ Wk + bk).reshape(B, S, H, Dh).transpose(0, 2, 1, 3)
        wv = (v @ Wv + bv).reshape(B, S, H, Dh).transpose(0, 2, 1, 3)
        scores = jnp.einsum('bhqd,bhkd->bhqk', wq, wk) / jnp.sqrt(jnp.asarray(Dh, wq.dtype))
        causal = jnp.tril(jnp.ones((S, S), bool))[None, None]
        mask_value = jnp.finfo(scores.dtype).min
        scores = jnp.where(causal, scores, mask_value)
        scores = scores + attention_mask[:, None, None, :]
        att = jax.nn.softmax(scores, axis=-1)
        out = jnp.einsum('bhqk,bhkd->bhqd', att, wv)
        out = out.transpose(0, 2, 1, 3).reshape(B, S, H * Dh)
        return out @ Wp + bp

    def _L0_ffn_ref(hidden_states, gate_weight, gate_up_proj, down_proj):
        import jax, jax.numpy as jnp
        import numpy as np
        TOP_K = 8
        NUM_EXPERTS = 32
        CAPACITY = 256
        B, S, H = hidden_states.shape
        E = gate_weight.shape[0]
        N = B * S
        x = hidden_states.reshape(N, H)
        logits = x @ gate_weight.T
        probs = jax.nn.softmax(logits.astype(jnp.float32), axis=-1)
        topw, topi = jax.lax.top_k(probs, TOP_K)
        topw = topw / topw.sum(-1, keepdims=True)
        topw = topw.astype(x.dtype)
        flat_e = topi.reshape(-1)
        flat_w = topw.reshape(-1)
        flat_x = jnp.repeat(x, TOP_K, axis=0)
        oh = jax.nn.one_hot(flat_e, E, dtype=jnp.int32)
        pos = (jnp.cumsum(oh, axis=0) * oh).sum(-1) - 1
        buf = jnp.zeros((E, CAPACITY, H), x.dtype).at[flat_e, pos].set(flat_x, mode='drop')
        gu = jnp.einsum('ech,efh->ecf', buf, gate_up_proj)
        gate, up = jnp.split(gu, 2, axis=-1)
        h = jax.nn.silu(gate) * up
        eo = jnp.einsum('ecf,ehf->ech', h, down_proj)
        tok_out = eo.at[flat_e, pos].get(mode='fill', fill_value=0)
        out = (tok_out * flat_w[:, None]).reshape(N, TOP_K, H).sum(1)
        return out.reshape(B, S, H)

    def _L1_xattn_ref(q, k, v, mask, Wq, bq, Wk, bk, Wv, bv, Wo, bo):
        import math
        import jax, jax.numpy as jnp
        import numpy as np
        B, S, E, H = (2, 512, 256, 16)
        D = E // H
        b = q.shape[0]

        def proj(x, W, bias):
            return (x @ W.T + bias).reshape(b, -1, H, D).transpose(0, 2, 1, 3)
        qh, kh, vh = (proj(q, Wq, bq), proj(k, Wk, bk), proj(v, Wv, bv))
        scores = jnp.einsum('bhqd,bhkd->bhqk', qh, kh) / math.sqrt(D)
        scores = jnp.where(mask[:, :, :, None] == 0, jnp.float32(-1000000000.0), scores)
        attn = jax.nn.softmax(scores, axis=-1)
        out = jnp.einsum('bhqk,bhkd->bhqd', attn, vh)
        concat = out.transpose(0, 2, 1, 3).reshape(b, -1, E)
        return concat @ Wo.T + bo

    def _L1_ffn_ref(x, wg, w1, b1, w2, b2):
        import jax, jax.numpy as jnp
        import numpy as np
        B, S, D = (2, 512, 256)
        E, K, H = (8, 2, 1024)
        CAP_FACTOR = 1.0

        def _moe_forward(x, wg, w1, b1, w2, b2):
            Bb, Ss, Dd = x.shape
            T = Bb * Ss
            cap = int(K * CAP_FACTOR * ((T + E - 1) // E))
            xt = x.reshape(T, Dd)
            logits = xt @ wg
            scores = jax.nn.softmax(logits, axis=-1)
            gates_k, idx_k = jax.lax.top_k(scores, K)
            gates_k = gates_k / jnp.sum(gates_k, axis=-1, keepdims=True)
            masks = jax.nn.one_hot(idx_k, E, dtype=jnp.int32)
            m = jnp.transpose(masks, (1, 0, 2)).reshape(K * T, E)
            locs_full = jnp.cumsum(m, axis=0) - 1
            loc = jnp.sum(locs_full * m, axis=-1)
            loc = loc.reshape(K, T).T
            valid = (loc < cap).astype(xt.dtype)
            loc_c = jnp.clip(loc, 0, cap - 1)
            contrib = (xt[:, None, :] * valid[:, :, None]).reshape(T * K, Dd)
            disp = jnp.zeros((E, cap, Dd), xt.dtype)
            disp = disp.at[idx_k.reshape(-1), loc_c.reshape(-1)].add(contrib)
            h = jax.nn.relu(jnp.einsum('ecd,edh->ech', disp, w1) + b1[:, None, :])
            out = jnp.einsum('ech,ehd->ecd', h, w2) + b2[:, None, :]
            gathered = out[idx_k, loc_c]
            y = jnp.einsum('tk,tkd->td', gates_k * valid, gathered)
            return y.reshape(Bb, Ss, Dd)
        return _moe_forward(x, wg, w1, b1, w2, b2)
    x = x + jnp.tanh(g_xattn[0]) * _L0_xattn_ref(_layernorm(x, axis=-1), ctx_1024, ctx_1024, mask_BxS2_ff0, L0_xattn_Wq, L0_xattn_bq, L0_xattn_Wk, L0_xattn_bk, L0_xattn_Wv, L0_xattn_bv, L0_xattn_Wp, L0_xattn_bp)
    x = x + jnp.tanh(g_ffn[0]) * _L0_ffn_ref(_layernorm(x, axis=-1), L0_ffn_gate_weight, L0_ffn_gate_up_proj, L0_ffn_down_proj)
    x = x + jnp.tanh(g_xattn[1]) * _L1_xattn_ref(_layernorm(x, axis=-1), ctx_1024, ctx_1024, mask_Bx1xS_if1, L1_xattn_Wq, L1_xattn_bq, L1_xattn_Wk, L1_xattn_bk, L1_xattn_Wv, L1_xattn_bv, L1_xattn_Wo, L1_xattn_bo)
    x = x + jnp.tanh(g_ffn[1]) * _L1_ffn_ref(_layernorm(x, axis=-1), L1_ffn_wg, L1_ffn_w1, L1_ffn_b1, L1_ffn_w2, L1_ffn_b2)
    return x

_drawn_inputs = setup_inputs


def setup_inputs(seed=0):
    import zlib

    import numpy as np

    out = dict(_drawn_inputs(seed))
    spreads = {'g_ffn': (-1.0, 0.6),
     'L0_xattn_bq': (0.0, 0.1),
     'L0_xattn_bk': (0.0, 2.0),
     'L0_xattn_bv': (0.0, 0.1),
     'L0_xattn_bp': (0.0, 0.1),
     'L1_xattn_bq': (0.0, 0.1),
     'L1_xattn_bk': (0.0, 2.0),
     'L1_xattn_bv': (0.0, 0.1),
     'L1_xattn_bo': (0.0, 0.1),
     'L1_ffn_b1': (0.0, 0.267),
     'L1_ffn_b2': (0.0, 0.1)}
    factors = {'L0_ffn_gate_weight': 8.0, 'L0_ffn_gate_up_proj': 6.075, 'L0_ffn_down_proj': 5.719}
    for name, (base, spread) in spreads.items():
        noise = np.random.default_rng([zlib.crc32(name.encode()), seed]).standard_normal(out[name].shape)
        drawn = base * np.exp(spread * noise) if base else spread * noise
        out[name] = jnp.asarray(drawn.astype(out[name].dtype))
    for name, factor in factors.items():
        out[name] = (out[name] * factor).astype(out[name].dtype)
    return out
```

```python
from contextlib import ExitStack

import concourse.bass as bass
from concourse import mybir
from concourse.alu_op_type import AluOpType as ALU

F32 = mybir.dt.float32
BF16 = mybir.dt.bfloat16
U32 = mybir.dt.uint32
I32 = mybir.dt.int32
ACT = mybir.ActivationFunctionType
AX = mybir.AxisListType

P = 128
B, S, D = 8, 512, 256
T = B * S
HEADS, DH = 16, 16
NT = S // P
NC = D // P
GROUPS = HEADS // 4
EPS = 1e-5
SCALE = DH ** -0.5
HIDDEN = -float(2 ** 100)

Q_TERM = (0, 0, 1, 1, 0, 2)
K_TERM = (0, 1, 0, 1, 2, 0)
STACK = DH * len(Q_TERM)
ROW_MASK = STACK
ROW_SHIFT = STACK + 3
ROWS = STACK + 6

E0, CAP0, F0, K0 = 32, 256, 192, 8
E1, CAP1, F1, K1 = 8, 1024, 1024, 2
W0 = D + 1 + E0
W1 = D + 1 + E1
SLOTS = E0 * CAP0
SPARE = CAP1
NOWHERE0 = 16384.0
NOWHERE1 = 32768.0

N_PREP = 10
N_POST = 6


class Chip:

    def __init__(self, nc, ctx):
        self.nc, self.ctx = nc, ctx


def sb(c, ctx, name, shape, dt=F32):
    return ctx.enter_context(c.nc.sbuf_tensor(name, shape, dt))


def count(per, half, par, extra=0):
    return half * (2 * per) + (per * par + extra)


def wait(eng, sem, value):
    if isinstance(value, int) and value <= 0:
        return
    eng.wait_ge(sem, value)


def wait_apart(eng, sem, value, passed):
    wait(eng, sem, value)
    if not isinstance(value, int):
        eng.sem_inc(passed, 1)


def pipeline(eng, n_items, prologue, iteration):
    prologue((0, 0))
    iteration((0, 0), (0, 1))
    with eng.Fori(1, n_items // 2) as it:
        iteration((it - 1, 1), (it, 0))
        iteration((it, 0), (it, 1))
    iteration((n_items // 2 - 1, 1), None)


def constants(c, g_xattn, g_ffn, rows0, rows1, x1, x3):
    nc, ctx = c.nc, c.ctx
    c.ident = sb(c, ctx, "ident", [P, P])
    c.identb = sb(c, ctx, "identb", [P, P], BF16)
    c.before = sb(c, ctx, "before", [P, P], BF16)
    c.onesb = sb(c, ctx, "onesb", [P, P], BF16)
    c.hide_st = sb(c, ctx, "hide_st", [P, P], BF16)
    c.hide_max = sb(c, ctx, "hide_max", [P, P], BF16)
    c.gates = sb(c, ctx, "gates", [P, 4])
    c.mhalf = sb(c, ctx, "mhalf", [P, NT])
    c.tok0 = sb(c, ctx, "tok0", [P, NT])
    c.key0 = sb(c, ctx, "key0", [P, E0])
    c.key1 = sb(c, ctx, "key1", [P, 2, E1])
    c.eid = sb(c, ctx, "eid", [P, E1])
    c.slot_in = sb(c, ctx, "slot_in", [P, E1, CAP1 // P])
    c.slot_at = sb(c, ctx, "slot_at", [P, E1, CAP1 // P])
    with ExitStack() as tmp:
        ii = sb(c, tmp, "ii", [P, 256], I32)
        empty = sb(c, tmp, "empty", [P, SPARE // P, W0])
        sem = lambda n: tmp.enter_context(nc.semaphore(n))
        gate_in, tables, empty_set, empty_out, iota_s, made = (
            sem(n) for n in ("gate_in", "tables", "empty_set", "empty_out", "iota_s", "made"))
        block = tmp.enter_context(nc.Block())

        @block.sync
        def _(sp):
            sp.dma_start(c.gates[:, 0:2], g_xattn.partition_broadcast(P)).then_inc(gate_in, 16)
            sp.dma_start(c.gates[:, 2:4], g_ffn.partition_broadcast(P)).then_inc(gate_in, 16)
            sp.wait_ge(empty_set, 2)
            for rows, n_rows, width in ((rows0, SLOTS, W0), (rows1, 2 * SLOTS, W1)):
                for at in range(0, n_rows, SPARE):
                    sp.dma_start(rows[at:at + SPARE, :].rearrange("(t p) w -> p t w", p=P),
                                 empty[:, :, 0:width]).then_inc(empty_out, 16)
            for x in (x1, x3):
                sp.dma_start(x[T:T + SPARE, :].rearrange("(t p) d -> p t d", p=P), empty[:, :, 0:D]).then_inc(empty_out, 16)
            sp.wait_ge(empty_out, 16 * (3 * SLOTS // SPARE + 2))

        @block.scalar
        def _(act):
            act.wait_ge(gate_in, 32)
            act.activation(c.gates[:, :], c.gates[:, :], ACT.Tanh).then_inc(made, 1)

        @block.vector
        def _(dve):
            dve.memset(empty[:, :, :], 0.0).then_inc(made, 1)
            dve.wait_ge(made, 2)
            dve.wait_ge(iota_s, 1)
            dve.tensor_copy(empty[:, :, D:D + 1], ii[:, 200:200 + SPARE // P].unsqueeze(2)).then_inc(empty_set, 1)
            dve.memset(c.onesb[:, :], 1.0)
            dve.memset(c.mhalf[:, :], -0.5).then_inc(empty_set, 1)
            dve.wait_ge(iota_s, 2)
            dve.tensor_copy(c.tok0[:, :], ii[:, 1:1 + NT])
            dve.tensor_copy(c.key0[:, :], ii[:, 8:8 + E0])
            dve.tensor_copy(c.key1[:, :, :], ii[:, 40:56].rearrange("p (k e) -> p k e", k=2))
            dve.tensor_copy(c.eid[:, :], ii[:, 56:64])
            n = E1 * (CAP1 // P)
            dve.tensor_copy(c.slot_in[:, :, :], ii[:, 64:64 + n].rearrange("p (e s) -> p e s", e=E1))
            dve.tensor_copy(c.slot_at[:, :, :], ii[:, 128:128 + n].rearrange("p (e s) -> p e s", e=E1)).then_inc(made, 1)

        @block.gpsimd
        def _(pool):
            pool.iota(ii[:, 200:200 + SPARE // P], pattern=[[P, SPARE // P]], base=T, channel_multiplier=1).then_inc(iota_s, 1)
            pool.iota(ii[:, 1:1 + NT], pattern=[[P, NT]], base=0, channel_multiplier=1)
            pool.iota(ii[:, 8:8 + E0], pattern=[[-CAP0, E0]], base=int(NOWHERE0), channel_multiplier=0)
            pool.iota(ii[:, 40:56].rearrange("p (k e) -> p k e", k=2), pattern=[[-SLOTS, 2], [-CAP1, E1]],
                      base=int(NOWHERE1), channel_multiplier=0)
            pool.iota(ii[:, 56:64], pattern=[[1, E1]], base=0, channel_multiplier=0)
            n = CAP1 // P
            pool.iota(ii[:, 64:64 + E1 * n].rearrange("p (e s) -> p e s", e=E1),
                      pattern=[[0, E1], [P, n]], base=0, channel_multiplier=1)
            pool.iota(ii[:, 128:128 + E1 * n].rearrange("p (e s) -> p e s", e=E1),
                      pattern=[[CAP1, E1], [P, n]], base=0, channel_multiplier=1).then_inc(iota_s, 1)
            pool.memset(c.ident[:, :], 0.0)
            pool.memset(c.identb[:, :], 0.0)
            pool.memset(c.before[:, :], 1.0)
            pool.memset(c.hide_st[:, :], 0.0)
            pool.memset(c.hide_max[:, :], 0.0).then_inc(tables, 1)
            pool.wait_ge(tables, 1)
            for m in (c.ident, c.identb):
                pool.affine_select(out=m[:, :], in_=m[:, :], compare_op=ALU.not_equal, fill=1.0,
                                   base=0, pattern=[[-1, P]], channel_multiplier=1)
            pool.affine_select(out=c.before[:, :], in_=c.before[:, :], compare_op=ALU.is_gt, fill=0.0,
                               base=0, pattern=[[1, P]], channel_multiplier=-1)
            pool.affine_select(out=c.hide_st[:, :], in_=c.hide_st[:, :], compare_op=ALU.is_ge, fill=HIDDEN,
                               base=0, pattern=[[1, P]], channel_multiplier=-1)
            pool.affine_select(out=c.hide_max[:, :], in_=c.hide_max[:, :], compare_op=ALU.is_ge, fill=HIDDEN,
                               base=0, pattern=[[-1, P]], channel_multiplier=1).then_inc(tables, 1)
            pool.wait_ge(tables, 2)


def attention(c, layer, x_in, ctx_in, mask, wq, bq, wk, bk, wv, bv, wp, bp, wroute, x_out, rows,
              qk_dram, mask_dram, tot0=None):
    nc = c.nc
    causal = layer == 0
    E = E0 if layer == 0 else E1
    CAP = CAP0 if layer == 0 else CAP1
    W = W0 if layer == 0 else W1
    NSEL = 1 if layer == 0 else 2
    NSCAT = NT * (K0 if layer == 0 else K1)
    NOWHERE = NOWHERE0 if layer == 0 else NOWHERE1
    LAST_ROW = SLOTS - 1 if layer == 0 else 2 * SLOTS - 1

    ctx = ExitStack()
    with ctx:
        t_ = lambda name, shape, dt=F32: sb(c, ctx, f"{name}_{layer}", shape, dt)
        sem = lambda n: ctx.enter_context(nc.semaphore(f"{n}_{layer}"))
        wq_s, wk_s, wv_s = (t_(n, [P, NC, D]) for n in ("wq", "wk", "wv"))
        wp_s = t_("wp", [P, GROUPS, D])
        bq_s, bk_s = t_("bq", [P, NC]), t_("bk", [P, NC])
        bv_s, bp_s = t_("bv", [P, D]), t_("bp", [P, D])
        wr_s = t_("wr", [P, NC, E])
        xrow = [t_(f"xrow{i}", [P, NT, D]) for i in range(2)]
        crow = t_("crow", [P, NT, D])
        xn = t_("xn", [P, NT, D])
        xT = t_("xT", [P, NC, S])
        cT = t_("cT", [P, NC, S])
        qk = t_("qk", [P, 2, NC, S])
        parts = t_("parts", [P, 2, 3, NC, S], BF16)
        qst = [t_(f"qst{i}", [ROWS, HEADS, S], BF16) for i in range(2)]
        kst = [t_(f"kst{i}", [ROWS, HEADS, S], BF16) for i in range(2)]
        va = [t_(f"va{i}", [P, NT, HEADS, 32]) for i in range(2)]
        pt = t_("pt", [P, 8, 2 * S])
        on = t_("on", [P, GROUPS, S])
        den = t_("den", [P, S])
        nmx = t_("nmx", [P, NT, HEADS])
        m3 = t_("m3", [P, NT, 3, HEADS], BF16)
        m3T = t_("m3T", [3 * HEADS, S], BF16)
        st6, mv = t_("st6", [P, NT, 6]), t_("mv", [P, NT, 2])
        st6b, mvb = t_("st6b", [P, NT, 6]), t_("mvb", [P, NT, 2])
        rstd, rstdb = t_("rstd", [P, NT]), t_("rstdb", [P, NT])
        rowb = t_("rowb", [P, NT, W])
        lgs, ex, rep = t_("lgs", [P, NT, E]), t_("ex", [P, NT, E]), t_("rep", [P, NT, E])
        lmx, rec, tok = t_("lmx", [P, NT]), t_("rec", [P, NT]), t_("tok", [P, NT])
        v8, k8 = t_("v8", [P, NT, 8]), t_("k8", [P, NT, 8])
        i8 = t_("i8", [P, NT, 8], U32)
        i8f = t_("i8f", [P, NT, 8])
        sel = t_("sel", [P, NSEL, NT, E], BF16)
        selsum = t_("selsum", [P, NT, E])
        pos, okay = t_("pos", [P, NSEL, NT, E]), t_("okay", [P, NSEL, NT, E])
        base = t_("base", [P, NSEL, E])
        idx = t_("idx", [P, NT, 8], U32)
        maskq = [t_(f"maskq{i}", [P, S]) for i in range(2)] if layer else None
        maski = [t_(f"maski{i}", [P, S], I32) for i in range(2)] if layer else None

        work = ctx.enter_context(nc.psum_tensor(f"work_{layer}", [P, 512], F32))
        mxb = [ctx.enter_context(nc.psum_tensor(f"mxb{i}_{layer}", [P, 512], F32)) for i in range(2)]
        stb = [ctx.enter_context(nc.psum_tensor(f"stb{i}_{layer}", [P, 1024], F32)) for i in range(2)]
        ob = ctx.enter_context(nc.psum_tensor(f"ob_{layer}", [P, 512], F32))

        with ExitStack() as tmp:
            w_in, w_zero, w_t, w_put, w_scaled = (
                tmp.enter_context(nc.semaphore(f"{n}_{layer}")) for n in
                ("w_in", "w_zero", "w_t", "w_put", "w_scaled"))
            w_chain = tmp.enter_context(nc.semaphore(f"w_chain_{layer}"))
            m_out = tmp.enter_context(nc.semaphore(f"m_out_{layer}"))
            if layer == 0:
                route_nat = pt[0:E0, 0, 0:D]
                mrow = pt[0:B, 1, 0:S]
                mparts = parts[0:B, 0, 0:3, 0, :]
            else:
                nat = [pt[:, i, 0:NC * D].rearrange("p (c n) -> p c n", c=NC) for i in range(3)]
                wo_nat = pt[:, 4:6, :].rearrange("p c (g j d) -> p c g j d", g=GROUPS, j=4)[:, :, :, :, 0:32]
                wo_nat = pt[:, 4, 0:NC * GROUPS * 128].rearrange("p (c g j d) -> p c g j d", c=NC, g=GROUPS, j=4)
            block = tmp.enter_context(nc.Block())

            @block.sync
            def _(sp):
                n = 0
                for w, s in ((wq, wq_s), (wk, wk_s), (wv, wv_s)):
                    dst = s[:, :, :] if layer == 0 else nat[n // 16]
                    sp.dma_start(dst, w.rearrange("(c p) n -> p c n", p=P)).then_inc(w_in, 16)
                    n += 16
                for b_, s in ((bq, bq_s), (bk, bk_s)):
                    sp.dma_start(s[:, :], b_.rearrange("(c p) -> p c", p=P), allow_slow_non_contiguous=True).then_inc(w_in, 16)
                for b_, s in ((bv, bv_s), (bp, bp_s)):
                    sp.dma_start(s[:, :], b_.partition_broadcast(P)).then_inc(w_in, 16)
                sp.wait_ge(w_zero, 1)
                if layer == 0:
                    sp.dma_start(route_nat, wroute).then_inc(w_in, 16)
                    sp.dma_start(mrow, mask).then_inc(w_in, 16)
                    src = wp.rearrange("(g j d) n -> j d g n", g=GROUPS, j=4)
                    for j in range(4):
                        sp.dma_start(wp_s[32 * j:32 * j + DH, :, :], src[j]).then_inc(w_in, 16)
                    sp.wait_ge(w_chain, 6)
                    sp.dma_start(mask_dram.rearrange("r b s -> b r s"), mparts).then_inc(m_out, 16)
                    sp.wait_ge(m_out, 16)
                else:
                    sp.dma_start(wr_s[:, :, :], wroute.rearrange("(c p) e -> p c e", p=P)).then_inc(w_in, 16)
                    src = wp.rearrange("(c p) (g j d) -> p c g j d", p=P, g=GROUPS, j=4)
                    for cc in range(NC):
                        for g in range(GROUPS):
                            sp.dma_start(wo_nat[:, cc, g, :, 0:DH], src[:, cc, g]).then_inc(w_in, 16)

            n_in = 16 * (7 + 2 + 4) if layer == 0 else 16 * (7 + 1 + NC * GROUPS)

            @block.tensor
            def _(pe):
                pe.wait_ge(w_in, n_in)
                if layer == 0:
                    for cc in range(NC):
                        last = pe.transpose(work[:, cc * E0:(cc + 1) * E0], route_nat[:, cc * P:(cc + 1) * P], c.ident[0:E0, 0:E0])
                    last.then_inc(w_t, 1)
                else:
                    for m, bank in ((0, work), (1, mxb[0]), (2, mxb[1])):
                        for co in range(NC):
                            for ci in range(NC):
                                last = pe.transpose(bank[:, ci * D + co * P:ci * D + (co + 1) * P],
                                                    nat[m][:, co, ci * P:(ci + 1) * P], c.ident[:, :])
                        last.then_inc(w_t, 1)
                    for g in range(GROUPS):
                        for co in range(NC):
                            last = pe.transpose(stb[0][:, g * D + co * P:g * D + (co + 1) * P],
                                                wo_nat[:, co, g, :, :].rearrange("p j d -> p (j d)"), c.ident[:, :])
                    last.then_inc(w_t, 1)

            @block.vector
            def _(dve):
                if layer == 0:
                    dve.memset(wp_s[:, :, :], 0.0).then_inc(w_zero, 1)
                else:
                    dve.memset(wo_nat, 0.0).then_inc(w_zero, 1)
                for i in range(2):
                    dve.memset(va[i][:, :, :, DH:32], 1.0)
                    dve.memset(qst[i][STACK:ROWS, :, :], 1.0)
                    dve.memset(kst[i][STACK:ROWS, :, :], 1.0)
                dve.memset(base[:, :, :], 0.0)
                dve.tensor_copy(tok[:, :], c.tok0[:, :])
                dve.wait_ge(w_in, n_in)
                dve.tensor_scalar(bp_s[:, :], bp_s[:, :], c.gates[:, layer:layer + 1], None, ALU.mult)
                if layer == 0:
                    dve.tensor_scalar(mrow, mrow, 1.0 / SCALE, None, ALU.mult).then_inc(w_chain, 1)
                    for r in range(3):
                        dve.wait_ge(w_chain, 1 + 2 * r)
                        dve.tensor_copy(mparts[:, r, :], mrow).then_inc(w_chain, 1)
                        if r < 2:
                            dve.wait_ge(w_chain, 2 + 2 * r)
                            dve.tensor_tensor(mrow, mrow, mparts[:, r, :], ALU.subtract).then_inc(w_chain, 1)
                    dve.tensor_scalar(wp_s[:, :, :], wp_s[:, :, :], c.gates[:, 0:1], None, ALU.mult)
                    dve.wait_ge(w_t, 1)
                    dve.tensor_copy(wr_s[:, :, :], work[:, 0:NC * E0].rearrange("p (c e) -> p c e", c=NC)).then_inc(w_put, 1)
                else:
                    for n, (s, bank) in enumerate(((wq_s, work), (wk_s, mxb[0]), (wv_s, mxb[1]))):
                        dve.wait_ge(w_t, n + 1)
                        dve.tensor_copy(s[:, :, :], bank[:, :].rearrange("p (c n) -> p c n", c=NC))
                    dve.wait_ge(w_t, 4)
                    dve.tensor_scalar(wp_s[:, :, :], stb[0][:, :].rearrange("p (g n) -> p g n", g=GROUPS),
                                      c.gates[:, 1:2], None, ALU.mult).then_inc(w_put, 1)

        names = ("ld0", "ld1", "parts_out", "stack_in0", "stack_in1", "shift_in", "x_out", "scat",
                 "prep_full", "prep_evac", "post_full", "post_evac", "shift_full", "shift_evac",
                 "max_full", "max_free", "st_full", "st_free", "pt_free", "pv_full", "norm_done",
                 "stat_rdy", "rstd_rdy", "xn_rdy", "xres_rdy", "split_rdy", "m3_rdy", "mchain", "nchain",
                 "stat2_rdy", "rstd2_rdy", "row_rdy", "lg_rdy", "ex_rdy", "sel_rdy", "idx_rdy", "vchain",
                 "pchain", "passed", "x_rdy", "mq_rdy", "achain")
        s = {n: sem(n) for n in names}
        ld, stack_in = (s["ld0"], s["ld1"]), (s["stack_in0"], s["stack_in1"])
        N_LD = 48 if layer else 32
        N_STACK = 16 * (13 if causal else 12)

        def span(pair):
            if not causal:
                return 0, 2 * S, ((2 * pair, 0, 0), (2 * pair + 1, S, 0))
            if pair == 0:
                return 0, 2 * S - P, ((0, 0, 0), (1, S, P))
            return 2 * P, 2 * P * 2 + P, ((2, 2 * P, 2 * P), (3, S, 3 * P))

        block = ctx.enter_context(nc.Block())

        def at(per, b, extra=0):
            return count(per, b[0], b[1], extra)

        def half_of(b, per, extra=0):
            return b[0] * per + extra

        @block.sync
        def _(sp):
            def load(n):
                par = n[1]
                r0 = n[0] * (2 * S) + n[1] * S
                wait_apart(sp, s["row_rdy"], at(1, n, -1), s["passed"])
                wait_apart(sp, s["prep_evac"], at(N_PREP, n, 0), s["passed"])
                if layer:
                    wait_apart(sp, s["mq_rdy"], at(1, n, -1), s["passed"])
                wait_apart(sp, s["x_out"], at(16, n, -16), s["passed"])
                sp.dma_start(xrow[par][:, :, :], x_in[bass.ds(r0, S), :].rearrange("(t p) d -> p t d", p=P)).then_inc(ld[par], 16)
                sp.dma_start(crow[:, :, :], ctx_in[bass.ds(r0, S), :].rearrange("(t p) d -> p t d", p=P)).then_inc(ld[par], 16)
                if layer:
                    sp.dma_start(maski[par][:, :], mask[bass.ds(r0, S)].partition_broadcast(P)).then_inc(ld[par], 16)

            def stack(n):
                par = n[1]
                sp.wait_ge(s["split_rdy"], at(1, n, 1))
                sp.dma_start(qk_dram[par].rearrange("i r (c p) s -> p (i r c) s", p=P),
                             parts[:, :, :, :, :].rearrange("p i r c s -> p (i r c) s")).then_inc(s["parts_out"], 16)
                wait_apart(sp, s["parts_out"], at(16, n, 16), s["passed"])
                wait_apart(sp, s["st_free"], at(32, n, -32 + 2), s["passed"])
                for side, dst, terms in ((0, qst, Q_TERM), (1, kst, K_TERM)):
                    for r, term in enumerate(terms):
                        sp.dma_start(dst[par][DH * r:DH * r + DH, :, :],
                                     qk_dram[par][side, term].rearrange("(h d) s -> d h s", d=DH)).then_inc(stack_in[par], 16)
                if causal:
                    sp.dma_start(kst[par][ROW_MASK:ROW_MASK + 3, :, :],
                                 mask_dram[:, bass.ds(n[0] * 2 + n[1], 1), :].to_broadcast([3, HEADS, S])).then_inc(stack_in[par], 16)

            def shift(n):
                par = n[1]
                sp.wait_ge(s["shift_evac"], at(1, n, 1))
                for r in range(3):
                    sp.dma_start(qst[par][ROW_SHIFT + r:ROW_SHIFT + r + 1, :, :],
                                 m3T[HEADS * r:HEADS * (r + 1), :]).then_inc(s["shift_in"], 16)

            def store(b):
                par = b[1]
                r0 = b[0] * (2 * S) + b[1] * S
                sp.wait_ge(s["x_rdy"], at(1, b, 1))
                sp.dma_start(x_out[bass.ds(r0, S), :].rearrange("(t p) d -> p t d", p=P), xrow[par][:, :, :]).then_inc(s["x_out"], 16)

            def prologue(n):
                load(n)
                stack(n)
                shift(n)

            def iteration(cur, nxt):
                if nxt:
                    load(nxt)
                    stack(nxt)
                    shift(nxt)
                store(cur)

            pipeline(sp, B, prologue, iteration)
            sp.wait_ge(s["x_out"], 16 * B)

        @block.tensor
        def _(pe):
            def prep(n, t):
                par = n[1]
                if t == 0:
                    wait(pe, s["post_evac"], at(N_POST, n, -N_POST))
                    wait(pe, s["shift_evac"], at(1, n, 0))
                    pe.wait_ge(s["xn_rdy"], at(1, n, 1))
                elif t == 2:
                    pe.wait_ge(ld[par], half_of(n, N_LD, N_LD))
                wait(pe, s["prep_evac"], at(N_PREP, n, t))
                if t < 4:
                    src, cc = (xn, crow)[t // 2], t % 2
                    for i in range(NT):
                        last = pe.transpose(work[:, i * P:(i + 1) * P], src[:, i, cc * P:(cc + 1) * P], c.ident[:, :])
                elif t < 8:
                    w, act_, co = ((wq_s, xT), (wk_s, cT))[(t - 4) // 2] + ((t - 4) % 2,)
                    for ci in range(NC):
                        last = pe.matmul(work[:, :], w[:, ci, co * P:(co + 1) * P], act_[:, ci, :],
                                         start=ci == 0, stop=ci == NC - 1)
                else:
                    for i in range(2):
                        tt = 2 * (t - 8) + i
                        for ci in range(NC):
                            last = pe.matmul(work[:, i * D:(i + 1) * D], cT[:, ci, tt * P:(tt + 1) * P], wv_s[:, ci, :],
                                             start=ci == 0, stop=ci == NC - 1)
                last.then_inc(s["prep_full"], 1)

            def maxima(n, u0, u1):
                par = n[1]
                rows_used = STACK + 3 if causal else STACK
                for u in range(u0, u1):
                    h, qt = u // NT, u % NT
                    if u == 0:
                        pe.wait_ge(stack_in[par], half_of(n, N_STACK, N_STACK))
                    pe.wait_ge(s["max_free"], at(64, n, u + 1))
                    nk = (qt + 1) * P if causal else S
                    last = pe.matmul(mxb[u % 2][:, 0:nk], qst[par][0:rows_used, h, qt * P:(qt + 1) * P],
                                     kst[par][0:rows_used, h, 0:nk], start=True, stop=not causal)
                    if causal:
                        last = pe.matmul(mxb[u % 2][:, nk - P:nk], c.identb[:, :], c.hide_max[:, :], start=False, stop=True)
                    last.then_inc(s["max_full"], 1)

            def shift(n):
                pe.wait_ge(s["m3_rdy"], at(1, n, 1))
                wait(pe, s["post_evac"], at(N_POST, n, -N_POST))
                pe.wait_ge(s["prep_evac"], at(N_PREP, n, N_PREP))
                for qt in range(NT):
                    last = pe.matmul(work[0:3 * HEADS, qt * P:(qt + 1) * P],
                                     m3[:, qt, :, :].rearrange("p r h -> p (r h)"), c.identb[:, :], start=True, stop=True)
                last.then_inc(s["shift_full"], 1)

            def scores(b, hf):
                par, g, pair = b[1], hf // 2, hf % 2
                if hf == 0:
                    pe.wait_ge(s["shift_in"], at(48, b, 48))
                for j in range(4):
                    u, h = 4 * hf + j, 4 * g + j
                    pe.wait_ge(s["st_free"], at(32, b, u + 1))
                    for kt, col, q0 in span(pair)[2]:
                        bank = stb[u % 2]
                        last = pe.matmul(bank[:, col:col + S - q0], kst[par][0:ROWS, h, kt * P:(kt + 1) * P],
                                         qst[par][0:ROWS, h, q0:S], start=True, stop=not causal)
                        if causal:
                            last = pe.matmul(bank[:, col:col + P], c.identb[:, :], c.hide_st[:, :], start=False, stop=True)
                    last.then_inc(s["st_full"], 1)

            def values(b, hf):
                par, g, pair = b[1], hf // 2, hf % 2
                pe.wait_ge(s["st_free"], at(32, b, 4 * hf + 4 + 2))
                if pair == 0:
                    wait(pe, s["norm_done"], at(4, b, g))
                for kt, col, q0 in span(pair)[2]:
                    for j in range(4):
                        u, h = 4 * hf + j, 4 * g + j
                        last = pe.matmul(ob[32 * j:32 * j + 32, q0:S], va[par][:, kt, h, :],
                                         pt[:, u % 8, col:col + S - q0], start=kt == 0, stop=kt == NT - 1,
                                         tile_position=(0, 32 * j))
                last.then_inc(s["pt_free"], 1)

            def post(b, t, last_batch):
                if t == 0:
                    pe.wait_ge(s["norm_done"], at(4, b, 4))
                    pe.wait_ge(s["prep_evac"], at(N_PREP, b, N_PREP if last_batch else 2 * N_PREP))
                    wait(pe, s["shift_evac"], at(1, b, 1 if last_batch else 2))
                elif t == 2:
                    pe.wait_ge(s["row_rdy"], at(1, b, 1))
                elif t == 5:
                    pe.wait_ge(s["sel_rdy"], at(1, b, 1))
                wait(pe, s["post_evac"], at(N_POST, b, t))
                if t < 2:
                    for i in range(2):
                        tt = 2 * t + i
                        for g in range(GROUPS):
                            last = pe.matmul(work[:, i * D:(i + 1) * D], on[:, g, tt * P:(tt + 1) * P], wp_s[:, g, :],
                                             start=g == 0, stop=g == GROUPS - 1)
                elif t < 4:
                    for i in range(NT):
                        last = pe.transpose(work[:, i * P:(i + 1) * P], rowb[:, i, (t - 2) * P:(t - 1) * P], c.ident[:, :])
                elif t == 4:
                    for i in range(NT):
                        for ci in range(NC):
                            last = pe.matmul(work[:, i * E:(i + 1) * E], xT[:, ci, i * P:(i + 1) * P], wr_s[:, ci, :],
                                             start=ci == 0, stop=ci == NC - 1)
                else:
                    for k in range(NSEL):
                        for i in range(NT + 1):
                            o = (k * (NT + 1) + i) * E
                            if i < NT:
                                last = pe.matmul(work[:, o:o + E], c.before[:, :], sel[:, k, i, :], start=True, stop=i == 0)
                            for ii in range(i):
                                last = pe.matmul(work[:, o:o + E], c.onesb[:, :], sel[:, k, ii, :],
                                                 start=i == NT and ii == 0, stop=ii == i - 1)
                last.then_inc(s["post_full"], 1)

            def prologue(n):
                for t in range(N_PREP):
                    prep(n, t)
                maxima(n, 0, 64)
                shift(n)

            def iteration(cur, nxt):
                for hf in range(8):
                    scores(cur, hf)
                    if nxt:
                        for t in range(2 * hf, min(2 * hf + 2, N_PREP)):
                            prep(nxt, t)
                    if hf:
                        values(cur, hf - 1)
                values(cur, 7)
                if nxt:
                    maxima(nxt, 0, 64)
                    shift(nxt)
                for t in range(N_POST):
                    post(cur, t, nxt is None)

            pe.sem_inc(s["pt_free"], 2)
            pipeline(pe, B, prologue, iteration)

        @block.scalar
        def _(act):
            def prep(n, t):
                act.wait_ge(s["prep_full"], at(N_PREP, n, t + 1))
                if t < 4:
                    dst = (xT, cT)[t // 2][:, t % 2, :]
                    act.activation(dst, work[:, :], ACT.Copy).then_inc(s["prep_evac"], 1)
                elif t < 8:
                    side, cc = (t - 4) // 2, (t - 4) % 2
                    bias = (bq_s, bk_s)[side][:, cc:cc + 1]
                    if t == 4 or (layer and t == 6):
                        wait(act, s["split_rdy"], at(1, n, 0))
                    act.activation(qk[:, side, cc, :], work[:, :], ACT.Identity, bias=bias).then_inc(s["prep_evac"], 1)

            def exps(b, hf):
                pair = hf % 2
                act.wait_ge(s["pt_free"], at(8, b, hf + 1))
                lo, hi, _ = span(pair)
                for j in range(4):
                    u = 4 * hf + j
                    act.wait_ge(s["st_full"], at(32, b, u + 1))
                    act.activation(pt[:, u % 8, lo:hi], stb[u % 2][:, lo:hi], ACT.Exp, scale=SCALE).then_inc(s["st_free"], 1)

            def post(b, t):
                if t in (2, 3):
                    act.wait_ge(s["post_full"], at(N_POST, b, t + 1))
                    act.activation(xT[:, t - 2, :], work[:, :], ACT.Copy).then_inc(s["post_evac"], 1)

            def route(b):
                act.wait_ge(s["lg_rdy"], at(1, b, 1))
                act.activation(ex[:, :, :], lgs[:, :, :], ACT.Exp).then_inc(s["ex_rdy"], 1)

            n_act = (0, 1, 2, 3, 6, 7) if layer else range(8)

            def prologue(n):
                for t in n_act:
                    prep(n, t)

            def iteration(cur, nxt):
                for hf in range(8):
                    exps(cur, hf)
                    if nxt:
                        for t in range(2 * hf, 2 * hf + 2):
                            if t in n_act:
                                prep(nxt, t)
                post(cur, 2)
                post(cur, 3)
                route(cur)

            act.sem_inc(s["st_free"], 2)
            pipeline(act, B, prologue, iteration)

        @block.vector
        def _(dve):
            def stats(x, st, m, n_chain, ready):
                for i in range(NT):
                    last = dve.bn_stats(st[:, i, :], x[:, i, :])
                return last

            def norm1(n):
                par = n[1]
                dve.wait_ge(ld[par], half_of(n, N_LD, N_LD))
                for i in range(NT):
                    dve.bn_stats(st6[:, i, :], xrow[par][:, i, :]).then_inc(s["nchain"], 1)
                wait_apart(dve, s["nchain"], at(NT, n, NT), s["passed"])
                for i in range(NT):
                    dve.bn_aggr(mv[:, i, :], st6[:, i, :]).then_inc(s["stat_rdy"], 1)
                if layer:
                    dve.tensor_scalar(maskq[par][:, :], maski[par][:, :], 0.0, None, ALU.not_equal).then_inc(s["mq_rdy"], 1)

            def norm1_apply(n):
                par = n[1]
                dve.wait_ge(s["rstd_rdy"], at(1, n, 1))
                wait(dve, s["prep_evac"], at(N_PREP, n, 0))
                for i in range(NT):
                    last = dve.tensor_scalar(xn[:, i, :], xrow[par][:, i, :], mv[:, i, 0:1], rstd[:, i:i + 1],
                                             ALU.subtract, ALU.mult)
                last.then_inc(s["xn_rdy"], 1)

            def prep(n, t):
                par = n[1]
                dve.wait_ge(s["prep_full"], at(N_PREP, n, t + 1))
                if t < 8:
                    if t == 4:
                        wait(dve, s["split_rdy"], at(1, n, 0))
                        dve.wait_ge(s["mq_rdy"], at(1, n, 1))
                    dve.scalar_tensor_tensor(out=qk[:, 0, t - 4, :], in0=work[:, :], scalar=bq_s[:, t - 4:t - 3],
                                             in1=maskq[par][:, :], op0=ALU.add, op1=ALU.mult).then_inc(s["prep_evac"], 1)
                else:
                    if t == 8:
                        wait(dve, s["pt_free"], at(8, n, -8 + 2))
                    i = 2 * (t - 8)
                    dve.tensor_tensor(va[par][:, i:i + 2, :, 0:DH],
                                      work[:, :].rearrange("p (t h d) -> p t h d", t=2, h=HEADS),
                                      bv_s[:, :].rearrange("p (h d) -> p h d", h=HEADS).unsqueeze(1).to_broadcast([P, 2, HEADS, DH]),
                                      ALU.add).then_inc(s["prep_evac"], 1)

            def maxima(n, u0, u1):
                for u in range(u0, u1):
                    h, qt = u // NT, u % NT
                    nk = (qt + 1) * P if causal else S
                    dve.wait_ge(s["max_full"], at(64, n, u + 1))
                    dve.tensor_reduce(nmx[:, qt, h:h + 1], mxb[u % 2][:, 0:nk], AX.X, ALU.max, negate=True).then_inc(s["max_free"], 1)

            def shift(n):
                dve.wait_ge(s["max_free"], at(64, n, 64 + 2))
                wait(dve, s["shift_full"], at(1, n, 0))
                for r in range(3):
                    dve.tensor_copy(m3[:, :, r, :], nmx[:, :, :]).then_inc(s["mchain"], 1)
                    dve.wait_ge(s["mchain"], at(5, n, 2 * r + 1))
                    if r < 2:
                        dve.tensor_tensor(nmx[:, :, :], nmx[:, :, :], m3[:, :, r, :], ALU.subtract).then_inc(s["mchain"], 1)
                        dve.wait_ge(s["mchain"], at(5, n, 2 * r + 2))
                dve.sem_inc(s["m3_rdy"], 1)
                dve.wait_ge(s["shift_full"], at(1, n, 1))
                wait(dve, s["shift_in"], at(48, n, 0))
                dve.tensor_copy(m3T[:, :], work[0:3 * HEADS, :]).then_inc(s["shift_evac"], 1)

            def norm(b, g):
                wait_apart(dve, s["pt_free"], at(8, b, 2 * g + 2 + 2), s["passed"])
                dve.stream_shuffle(den[:, :], ob[:, :], [DH + i % DH for i in range(32)]).then_inc(s["vchain"], 1)
                dve.wait_ge(s["vchain"], at(8, b, 2 * g + 1))
                dve.reciprocal(den[:, :], den[:, :]).then_inc(s["vchain"], 1)
                dve.wait_ge(s["vchain"], at(8, b, 2 * g + 2))
                if g == 0:
                    wait(dve, s["post_evac"], at(N_POST, b, 0))
                dve.tensor_tensor(on[:, g, :], ob[:, :], den[:, :], ALU.mult).then_inc(s["norm_done"], 1)

            def post(b, t):
                par = b[1]
                dve.wait_ge(s["post_full"], at(N_POST, b, t + 1))
                if t == 0:
                    dve.wait_ge(s["xres_rdy"], at(1, b, 1))
                dve.tensor_tensor(xrow[par][:, 2 * t:2 * t + 2, :], work[:, :].rearrange("p (t d) -> p t d", t=2),
                                  xrow[par][:, 2 * t:2 * t + 2, :], ALU.add).then_inc(s["post_evac"], 1)

            def norm2(b):
                par = b[1]
                dve.wait_ge(s["post_evac"], at(N_POST, b, 2))
                dve.sem_inc(s["x_rdy"], 1)
                for i in range(NT):
                    dve.bn_stats(st6b[:, i, :], xrow[par][:, i, :]).then_inc(s["nchain2"], 1)
                wait_apart(dve, s["nchain2"], at(NT, b, NT), s["passed"])
                for i in range(NT):
                    dve.bn_aggr(mvb[:, i, :], st6b[:, i, :]).then_inc(s["stat2_rdy"], 1)
                dve.wait_ge(s["rstd2_rdy"], at(1, b, 1))
                wait(dve, s["scat"], at(16 * NSCAT, b, 0))
                for i in range(NT):
                    last = dve.tensor_scalar(rowb[:, i, 0:D], xrow[par][:, i, :], mvb[:, i, 0:1], rstdb[:, i:i + 1],
                                             ALU.subtract, ALU.mult)
                last.then_inc(s["row_rdy"], 1)

            N_CH = 40

            def route(b):
                link = [0]

                def chain(ins):
                    link[0] += 1
                    ins.then_inc(s["rchain"], 1)
                    wait_apart(dve, s["rchain"], at(N_CH, b, link[0]), s["passed"])

                bc = lambda ap: ap.unsqueeze(2).to_broadcast([P, NT, E])
                lg = work[:, 0:NT * E].rearrange("p (t e) -> p t e", t=NT)
                dve.wait_ge(s["post_full"], at(N_POST, b, 5))
                chain(dve.tensor_reduce(lmx[:, :], lg, AX.X, ALU.max))
                dve.tensor_tensor(lgs[:, :, :], lg, bc(lmx[:, :]), ALU.subtract).then_inc(s["lg_rdy"], 1)
                dve.wait_ge(s["lg_rdy"], at(1, b, 1))
                dve.sem_inc(s["post_evac"], 1)
                wait_apart(dve, s["ex_rdy"], at(1, b, 1), s["passed"])
                for i in range(NT):
                    last = dve.max(v8[:, i, :], ex[:, i, :])
                chain(last)
                if layer == 0:
                    for i in range(NT):
                        last = dve.match_replace(rep[:, i, :], v8[:, i, :], ex[:, i, :], -1.0)
                    dve.tensor_reduce(rec[:, :], v8[:, :, :], AX.X, ALU.add)
                    chain(last)
                    dve.tensor_scalar(selsum[:, :, :], rep[:, :, :], 0.0, None, ALU.is_lt)
                    chain(dve.tensor_scalar(sel[:, 0, :, :], rep[:, :, :], 0.0, None, ALU.is_lt))
                else:
                    for i in range(NT):
                        last = dve.max_index(i8[:, i, :], v8[:, i, :], ex[:, i, :])
                    chain(last)
                    chain(dve.tensor_copy(i8f[:, :, :], i8[:, :, :]))
                    dve.tensor_tensor(rec[:, :], v8[:, :, 0], v8[:, :, 1], ALU.add)
                    for k in range(2):
                        last = dve.tensor_tensor(sel[:, k, :, :], c.eid[:, :].unsqueeze(1).to_broadcast([P, NT, E]),
                                                 bc(i8f[:, :, k]), ALU.is_equal)
                    chain(last)
                    chain(dve.tensor_tensor(selsum[:, :, :], sel[:, 0, :, :], sel[:, 1, :, :], ALU.add))
                dve.sem_inc(s["sel_rdy"], 1)
                chain(dve.reciprocal(rec[:, :], rec[:, :]))
                chain(dve.tensor_tensor(ex[:, :, :], ex[:, :, :], selsum[:, :, :], ALU.mult))
                dve.tensor_tensor(rowb[:, :, D + 1:W], ex[:, :, :], bc(rec[:, :]), ALU.mult)
                chain(dve.tensor_copy(rowb[:, :, D:D + 1], tok[:, :].unsqueeze(2)))
                chain(dve.tensor_scalar(tok[:, :], tok[:, :], float(S), None, ALU.add))
                dve.wait_ge(s["post_full"], at(N_POST, b, 6))
                got = work[:, 0:NSEL * (NT + 1) * E].rearrange("p (k t e) -> p k t e", k=NSEL, t=NT + 1)
                bases = base[:, :, :].unsqueeze(2).to_broadcast([P, NSEL, NT, E])
                keys = (c.key0[:, :].unsqueeze(1) if layer == 0 else c.key1[:, :, :]).unsqueeze(2).to_broadcast([P, NSEL, NT, E])
                for k in range(NSEL):
                    last = dve.tensor_tensor(pos[:, k, :, :], got[:, k, 0:NT, :], base[:, k, :].unsqueeze(1).to_broadcast([P, NT, E]), ALU.add)
                chain(last)
                chain(dve.tensor_tensor(base[:, :, :], got[:, :, NT, :], base[:, :, :], ALU.add))
                dve.sem_inc(s["post_evac"], 1)
                chain(dve.tensor_scalar(okay[:, :, :, :], pos[:, :, :, :], float(CAP), None, ALU.is_lt))
                for k in range(NSEL):
                    key = (c.key0[:, :] if layer == 0 else c.key1[:, k, :]).unsqueeze(1).to_broadcast([P, NT, E])
                    last = dve.tensor_tensor(pos[:, k, :, :], key, pos[:, k, :, :], ALU.subtract)
                chain(last)
                chain(dve.tensor_tensor(pos[:, :, :, :], pos[:, :, :, :], okay[:, :, :, :], ALU.mult))
                chain(dve.tensor_tensor(pos[:, :, :, :], pos[:, :, :, :], sel[:, :, :, :], ALU.mult))
                if layer == 0:
                    for i in range(NT):
                        last = dve.max(k8[:, i, :], pos[:, 0, i, :])
                else:
                    for k in range(2):
                        last = dve.tensor_reduce(k8[:, :, k], pos[:, k, :, :], AX.X, ALU.max)
                chain(last)
                wait(dve, s["scat"], at(16 * NSCAT, b, 0))
                nk = 8 if layer == 0 else 2
                dve.tensor_scalar(idx[:, :, 0:nk], k8[:, :, 0:nk], -1.0, NOWHERE, ALU.mult, ALU.add).then_inc(s["idx_rdy"], 1)
                while link[0] < N_CH:
                    dve.sem_inc(s["rchain"], N_CH - link[0])
                    link[0] = N_CH

            def prologue(n):
                norm1(n)
                norm1_apply(n)
                if layer:
                    prep(n, 4)
                    prep(n, 5)
                prep(n, 8)
                prep(n, 9)
                maxima(n, 0, 64)
                shift(n)

            def iteration(cur, nxt):
                if nxt:
                    norm1(nxt)
                    norm1_apply(nxt)
                for hf in range(8):
                    if nxt:
                        for t in range(2 * hf, 2 * hf + 2):
                            if t in ((4, 5, 8, 9) if layer else (8, 9)):
                                prep(nxt, t)
                    if hf and hf % 2 == 0:
                        norm(cur, hf // 2 - 1)
                norm(cur, 3)
                if nxt:
                    maxima(nxt, 0, 64)
                    shift(nxt)
                post(cur, 0)
                post(cur, 1)
                norm2(cur)
                route(cur)

            s["nchain2"], s["rchain"] = sem("nchain2"), sem("rchain")
            dve.sem_inc(s["max_free"], 2)
            pipeline(dve, B, prologue, iteration)
            if tot0 is not None:
                dve.wait_ge(s["rchain"], N_CH * B)
                dve.tensor_copy(tot0[:, :], base[:, 0, :]).then_inc(s["vchain"], 1)

        @block.gpsimd
        def _(pool):
            def rstd_of(b, m, out, ready, done):
                pool.wait_ge(ready, at(NT, b, NT))
                pool.tensor_scalar(out[:, :], m[:, :, 1], EPS, None, ALU.add).then_inc(s["pchain"], 1)
                return done

            def norm1(n):
                pool.wait_ge(s["stat_rdy"], at(NT, n, NT))
                wait_apart(pool, s["xn_rdy"], at(1, n, 0), s["passed"])
                pool.tensor_scalar(rstd[:, :], mv[:, :, 1], EPS, None, ALU.add).then_inc(s["pchain"], 1)
                pool.wait_ge(s["pchain"], at(1, n, 1))
                pool.tensor_tensor(rstd[:, :], rstd[:, :], c.mhalf[:, :], ALU.pow).then_inc(s["rstd_rdy"], 1)

            def residual(n):
                par = n[1]
                pool.wait_ge(s["xn_rdy"], at(1, n, 1))
                pool.tensor_tensor(xrow[par][:, :, :], xrow[par][:, :, :],
                                   bp_s[:, :].unsqueeze(1).to_broadcast([P, NT, D]), ALU.add).then_inc(s["xres_rdy"], 1)

            def split(n):
                pool.wait_ge(s["prep_evac"], at(N_PREP, n, 8))
                wait_apart(pool, s["parts_out"], at(16, n, 0), s["passed"])
                k = 0
                for side in range(2):
                    for r in range(3):
                        src = qk[:, side, :, :]
                        ins = pool.tensor_copy(parts[:, side, r, :, :], src)
                        k += 1
                        if side == 1 and r == 2:
                            ins.then_inc(s["split_rdy"], 1)
                        else:
                            ins.then_inc(s["schain"], 1)
                        if r < 2:
                            pool.wait_ge(s["schain"], at(9, n, 5 * side + 2 * r + 1))
                            pool.tensor_tensor(src, src, parts[:, side, r, :, :], ALU.subtract).then_inc(s["schain"], 1)
                            wait_apart(pool, s["schain"], at(9, n, 5 * side + 2 * r + 2), s["passed"])

            def norm2(b):
                wait_apart(pool, s["stat2_rdy"], at(NT, b, NT), s["passed"])
                pool.tensor_scalar(rstdb[:, :], mvb[:, :, 1], EPS, None, ALU.add).then_inc(s["pchain2"], 1)
                pool.wait_ge(s["pchain2"], at(1, b, 1))
                pool.tensor_tensor(rstdb[:, :], rstdb[:, :], c.mhalf[:, :], ALU.pow).then_inc(s["rstd2_rdy"], 1)

            def scatter(b):
                wait_apart(pool, s["idx_rdy"], at(1, b, 1), s["passed"])
                for i in range(NT):
                    for k in range(NSCAT // NT):
                        pool.indirect_dma_start(rows, bass.IndirectOffsetOnAxis(idx[:, i, k:k + 1], 0), rowb[:, i, :], None,
                                                bounds_check=LAST_ROW, oob_is_err=False).then_inc(s["scat"], 16)

            def prologue(n):
                norm1(n)
                residual(n)
                split(n)

            def iteration(cur, nxt):
                if nxt:
                    norm1(nxt)
                    residual(nxt)
                    split(nxt)
                norm2(cur)
                scatter(cur)

            s["schain"], s["pchain2"] = sem("schain"), sem("pchain2")
            pipeline(pool, B, prologue, iteration)
            pool.wait_ge(s["scat"], 16 * NSCAT * B)

        @block.tensor
        def _(pe):
            pass


def experts0(c, rows, gate_up, down, x):
    nc = c.nc
    FC = F0 // 2
    TILES = CAP0 // P
    with ExitStack() as ctx:
        t_ = lambda name, shape, dt=F32: sb(c, ctx, f"e0_{name}", shape, dt)
        names = ("rows_in0", "rows_in1", "weights_in0", "weights_in1", "t_full", "act_evac", "dve_evac",
                 "gu_full", "silu_done", "h_done", "y_full", "y_done", "added", "w_done", "passed")
        s = {n: ctx.enter_context(nc.semaphore(f"e0_{n}")) for n in names}
        rows_in, weights_in = (s["rows_in0"], s["rows_in1"]), (s["weights_in0"], s["weights_in1"])
        two = lambda name, shape, dt=F32: [t_(f"{name}{i}", shape, dt) for i in range(2)]
        row = two("row", [P, TILES, W0])
        gu_nat = two("gu_nat", [FC, 4, D])
        dn_nat = two("dn_nat", [P, NC, F0])
        xT = two("xT", [P, NC, CAP0])
        guT = two("guT", [P, NC, 4, FC])
        dnT = two("dnT", [FC, 2, D])
        sg = t_("silu", [FC, 2, CAP0])
        h = t_("h", [FC, 2, CAP0])
        y = two("y", [P, TILES, D])
        wcol, token = two("wcol", [P, TILES]), two("token", [P, TILES], U32)
        bank = [ctx.enter_context(nc.psum_tensor(f"e0_bank{i}", [P, 512], F32)) for i in range(7)]
        x_b, gu_b, dn_b, g_b, u_b, y_b = bank[0], bank[1:3], bank[3], bank[4], bank[5], bank[6]
        at = lambda per, b, extra=0: count(per, b[0], b[1], extra)
        block = ctx.enter_context(nc.Block())

        @block.sync
        def _(sp):
            def load(n):
                par = n[1]
                e = n[0] * 2 + n[1]
                wait_apart(sp, s["t_full"], at(4, n, -4), s["passed"])
                wait_apart(sp, s["y_done"], at(1, n, -1), s["passed"])
                sp.dma_start(gu_nat[par][:, :, :], gate_up[bass.ds(e, 1)].rearrange("o (c f) h -> f (o c) h", f=FC)).then_inc(weights_in[par], 16)
                sp.dma_start(dn_nat[par][:, :, :], down[bass.ds(e, 1)].rearrange("o (c p) f -> p (o c) f", p=P)).then_inc(weights_in[par], 16)
                sp.dma_start(row[par][:, :, :], rows[bass.ds(e * CAP0, CAP0), :].rearrange("(t p) w -> p t w", p=P)).then_inc(rows_in[par], 16)

            def iteration(cur, nxt):
                if nxt:
                    load(nxt)

            pipeline(sp, E0, load, iteration)

        @block.tensor
        def _(pe):
            def turn(n):
                par = n[1]
                pe.wait_ge(rows_in[par], n[0] * 16 + 16)
                wait(pe, s["dve_evac"], at(2, n, 0))
                for cc in range(NC):
                    for i in range(TILES):
                        last = pe.transpose(x_b[:, cc * CAP0 + i * P:cc * CAP0 + (i + 1) * P],
                                            row[par][:, i, cc * P:(cc + 1) * P], c.ident[:, :])
                last.then_inc(s["t_full"], 1)
                pe.wait_ge(weights_in[par], n[0] * 32 + 32)
                wait(pe, s["act_evac"], at(2, n, 0))
                for cc in range(NC):
                    for q in range(4):
                        last = pe.transpose(gu_b[cc][:, q * FC:(q + 1) * FC], gu_nat[par][:, q, cc * P:(cc + 1) * P], c.ident[0:FC, 0:FC])
                    last.then_inc(s["t_full"], 1)
                for f in range(2):
                    for cc in range(NC):
                        last = pe.transpose(dn_b[0:FC, f * D + cc * P:f * D + (cc + 1) * P],
                                            dn_nat[par][:, cc, f * FC:(f + 1) * FC], c.ident[:, :])
                last.then_inc(s["t_full"], 1)

            def up(b):
                par = b[1]
                pe.wait_ge(s["dve_evac"], at(2, b, 2))
                pe.wait_ge(s["act_evac"], at(2, b, 2))
                wait(pe, s["h_done"], at(1, b, 0))
                for q in range(4):
                    out = (g_b, u_b)[q // 2][0:FC, (q % 2) * CAP0:(q % 2 + 1) * CAP0]
                    for ci in range(NC):
                        last = pe.matmul(out, guT[par][:, ci, q, :], xT[par][:, ci, :], start=ci == 0, stop=ci == NC - 1)
                last.then_inc(s["gu_full"], 1)

            def down_(b):
                par = b[1]
                pe.wait_ge(s["h_done"], at(1, b, 1))
                wait(pe, s["y_done"], at(1, b, 0))
                for i in range(TILES):
                    for f in range(2):
                        last = pe.matmul(y_b[:, i * D:(i + 1) * D], h[:, f, i * P:(i + 1) * P], dnT[par][:, f, :],
                                         start=f == 0, stop=f == 1)
                last.then_inc(s["y_full"], 1)

            def iteration(cur, nxt):
                up(cur)
                if nxt:
                    turn(nxt)
                down_(cur)

            pipeline(pe, E0, turn, iteration)

        @block.scalar
        def _(act):
            def evac(n):
                par = n[1]
                act.wait_ge(s["t_full"], at(4, n, 2))
                act.activation(guT[par][:, 0, :, :].rearrange("p q f -> p (q f)"), gu_b[0][:, 0:4 * FC], ACT.Copy).then_inc(s["act_evac"], 1)
                act.wait_ge(s["t_full"], at(4, n, 4))
                act.activation(dnT[par][:, :, :].rearrange("p f h -> p (f h)"), dn_b[0:FC, :], ACT.Copy).then_inc(s["act_evac"], 1)

            def silu(b):
                act.wait_ge(s["gu_full"], at(1, b, 1))
                act.activation(sg[:, :, :].rearrange("p f s -> p (f s)"), g_b[0:FC, :], ACT.Silu).then_inc(s["silu_done"], 1)

            def iteration(cur, nxt):
                silu(cur)
                if nxt:
                    evac(nxt)

            pipeline(act, E0, evac, iteration)

        @block.vector
        def _(dve):
            def evac(n):
                par = n[1]
                dve.wait_ge(s["t_full"], at(4, n, 1))
                dve.tensor_copy(xT[par][:, :, :].rearrange("p c s -> p (c s)"), x_b[:, :]).then_inc(s["dve_evac"], 1)
                dve.wait_ge(s["t_full"], at(4, n, 3))
                dve.tensor_copy(guT[par][:, 1, :, :].rearrange("p q f -> p (q f)"), gu_b[1][:, 0:4 * FC]).then_inc(s["dve_evac"], 1)

            def hidden(b):
                dve.wait_ge(s["silu_done"], at(1, b, 1))
                dve.tensor_tensor(h[:, :, :].rearrange("p f s -> p (f s)"), u_b[0:FC, :],
                                  sg[:, :, :].rearrange("p f s -> p (f s)"), ALU.mult).then_inc(s["h_done"], 1)

            def result(b):
                par = b[1]
                e = b[0] * 2 + b[1]
                dve.wait_ge(rows_in[par], b[0] * 16 + 16)
                wait(dve, s["added"], at(16 * TILES, b, -16 * TILES))
                dve.tensor_copy(token[par][:, :], row[par][:, :, D])
                dve.tensor_copy(wcol[par][:, :].unsqueeze(2), row[par][:, :, bass.ds(e + (D + 1), 1)]).then_inc(s["w_done"], 1)
                dve.wait_ge(s["w_done"], at(1, b, 1))
                dve.wait_ge(s["y_full"], at(1, b, 1))
                for i in range(TILES):
                    last = dve.tensor_scalar(y[par][:, i, :], y_b[:, i * D:(i + 1) * D], wcol[par][:, i:i + 1],
                                             c.gates[:, 2:3], ALU.mult, ALU.mult)
                last.then_inc(s["y_done"], 1)

            def iteration(cur, nxt):
                hidden(cur)
                if nxt:
                    evac(nxt)
                result(cur)

            pipeline(dve, E0, evac, iteration)

        @block.gpsimd
        def _(pool):
            def add(b):
                par = b[1]
                wait_apart(pool, s["added"], at(16 * TILES, b, 0), s["passed"])
                wait_apart(pool, s["y_done"], at(1, b, 1), s["passed"])
                for i in range(TILES):
                    pool.indirect_dma_start(x, bass.IndirectOffsetOnAxis(token[par][:, i:i + 1], 0), y[par][:, i, :], None,
                                            bounds_check=T + SPARE - 1, oob_is_err=True, compute_op=ALU.add).then_inc(s["added"], 16)

            def nothing(n):
                pass

            pipeline(pool, E0, nothing, lambda cur, nxt: add(cur))
            pool.wait_ge(s["added"], 16 * TILES * E0)


def experts1(c, rows, w1, b1, w2, b2, x, tot0, out):
    nc = c.nc
    TILES, HC = CAP1 // P, F1 // P
    HALF = CAP1 // 2
    with ExitStack() as ctx:
        t_ = lambda name, shape, dt=F32: sb(c, ctx, f"e1_{name}", shape, dt)
        two = lambda name, shape, dt=F32: [t_(f"{name}{i}", shape, dt) for i in range(2)]
        names = ("rows_in0", "rows_in1", "weights_in0", "weights_in1", "bias_in", "x_full", "x_evac",
                 "h_full", "act_h", "dve_h", "y_full", "y_evac", "y_done", "added", "picked", "small", "ichain",
                 "copied", "passed")
        s = {n: ctx.enter_context(nc.semaphore(f"e1_{n}")) for n in names}
        rows_in, weights_in = (s["rows_in0"], s["rows_in1"]), (s["weights_in0"], s["weights_in1"])
        row = two("row", [P, TILES, W1])
        w1_s, w2_s = two("w1", [P, NC, F1]), two("w2", [P, HC, D])
        xT = two("xT", [P, NC, CAP1])
        h = two("h", [P, HC, HALF])
        y = two("y", [P, TILES, D])
        b1_s, b2_s = t_("b1", [P, E1, HC]), t_("b2", [P, E1, D])
        b1_e = two("b1_e", [P, HC])
        gidx = t_("gidx", [P, E1, TILES], U32)
        gfl, late = t_("gfl", [P, E1, TILES]), t_("late", [P, E1, TILES])
        gidx_e = two("gidx_e", [P, TILES], U32)
        wcol, token = two("wcol", [P, TILES]), two("token", [P, TILES], U32)
        hb = [ctx.enter_context(nc.psum_tensor(f"e1_h_bank{i}", [P, 512], F32)) for i in range(4)]
        yb = [ctx.enter_context(nc.psum_tensor(f"e1_y_bank{i}", [P, 512], F32)) for i in range(2)]
        xb = ctx.enter_context(nc.psum_tensor("e1_x_bank", [P, 512], F32))
        at = lambda per, b, extra=0: count(per, b[0], b[1], extra)
        block = ctx.enter_context(nc.Block())

        @block.sync
        def _(sp):
            sp.dma_start(b1_s[:, :, :], b1.rearrange("e (c p) -> p e c", p=P), allow_slow_non_contiguous=True).then_inc(s["bias_in"], 16)
            sp.dma_start(b2_s[:, :, :], b2.partition_broadcast(P)).then_inc(s["bias_in"], 16)

            def load(n):
                par = n[1]
                e = n[0] * 2 + n[1]
                wait_apart(sp, s["y_full"], at(4, n, -4), s["passed"])
                sp.dma_start(w1_s[par][:, :, :], w1[bass.ds(e, 1)].rearrange("o (c p) f -> p (o c) f", p=P)).then_inc(weights_in[par], 16)
                sp.dma_start(w2_s[par][:, :, :], w2[bass.ds(e, 1)].rearrange("o (c p) d -> p (o c) d", p=P)).then_inc(weights_in[par], 16)

            def iteration(cur, nxt):
                if nxt:
                    load(nxt)

            pipeline(sp, E1, load, iteration)
            sp.wait_ge(s["added"], 16 * TILES * E1)
            sp.dma_start(out, x[0:T, :]).then_inc(s["copied"], 16)
            sp.wait_ge(s["copied"], 16)

        @block.tensor
        def _(pe):
            def turn(n, k):
                par, cc, hf = n[1], k // 2, k % 2
                if k == 0:
                    pe.wait_ge(rows_in[par], n[0] * (16 * TILES) + 16 * TILES)
                wait(pe, s["x_evac"], at(4, n, k))
                for i in range(4):
                    last = pe.transpose(xb[:, i * P:(i + 1) * P], row[par][:, 4 * hf + i, cc * P:(cc + 1) * P], c.ident[:, :])
                last.then_inc(s["x_full"], 1)

            def up(b, blk, k0, k1):
                par = b[1]
                if k0 == 0 and blk == 0:
                    pe.wait_ge(weights_in[par], b[0] * 32 + 32)
                    pe.wait_ge(s["x_evac"], at(4, b, 4))
                for k in range(k0, k1):
                    q = 8 * blk + k
                    wait(pe, s[("act_h", "dve_h")[q % 2]], at(8, b, q // 2 - 1))
                    for ci in range(NC):
                        last = pe.matmul(hb[q % 4][:, :], w1_s[par][:, ci, k * P:(k + 1) * P],
                                         xT[par][:, ci, blk * HALF:(blk + 1) * HALF], start=ci == 0, stop=ci == NC - 1)
                    last.then_inc(s["h_full"], 1)

            def down(b, blk):
                par = b[1]
                pe.wait_ge(s["act_h"], at(8, b, 4 * blk + 4))
                pe.wait_ge(s["dve_h"], at(8, b, 4 * blk + 4))
                for t in range(2):
                    trip = 2 * blk + t
                    wait(pe, s["y_evac"], at(4, b, trip - 1))
                    for i in range(2):
                        for k in range(HC):
                            last = pe.matmul(yb[t][:, i * D:(i + 1) * D], h[blk][:, k, (2 * t + i) * P:(2 * t + i + 1) * P],
                                             w2_s[par][:, k, :], start=k == 0, stop=k == HC - 1)
                    last.then_inc(s["y_full"], 1)

            def prologue(n):
                for k in range(4):
                    turn(n, k)
                up(n, 0, 0, HC)

            def iteration(cur, nxt):
                for k in range(4):
                    up(cur, 1, 2 * k, 2 * k + 2)
                    if nxt:
                        turn(nxt, k)
                down(cur, 0)
                if nxt:
                    up(nxt, 0, 0, HC)
                down(cur, 1)

            pipeline(pe, E1, prologue, iteration)

        @block.scalar
        def _(act):
            def evac(n, k):
                par, cc, hf = n[1], k // 2, k % 2
                act.wait_ge(s["x_full"], at(4, n, k + 1))
                act.activation(xT[par][:, cc, hf * HALF:(hf + 1) * HALF], xb[:, :], ACT.Copy).then_inc(s["x_evac"], 1)

            def hidden(b, blk, ks):
                par = b[1]
                if blk == 0:
                    act.wait_ge(s["small"], at(1, b, 1))
                for k in ks:
                    q = 8 * blk + k
                    act.wait_ge(s["h_full"], at(16, b, q + 1))
                    act.activation(h[blk][:, k, :], hb[q % 4][:, :], ACT.Relu, bias=b1_e[par][:, k:k + 1]).then_inc(s["act_h"], 1)

            def prologue(n):
                for k in range(4):
                    evac(n, k)
                hidden(n, 0, (0, 2, 4, 6))

            def iteration(cur, nxt):
                for k in range(4):
                    hidden(cur, 1, (2 * k,))
                    if nxt:
                        evac(nxt, k)
                if nxt:
                    hidden(nxt, 0, (0, 2, 4, 6))

            pipeline(act, E1, prologue, iteration)

        @block.vector
        def _(dve):
            full = tot0[:, :].unsqueeze(2).to_broadcast([P, E1, TILES])
            dve.tensor_tensor(late[:, :, :], c.slot_in[:, :, :], full, ALU.is_ge).then_inc(s["ichain"], 1)
            dve.tensor_scalar(gfl[:, :, :], full, -1.0, float(SLOTS), ALU.mult, ALU.add).then_inc(s["ichain"], 1)
            dve.wait_ge(s["ichain"], 2)
            dve.tensor_tensor(gfl[:, :, :], gfl[:, :, :], late[:, :, :], ALU.mult).then_inc(s["ichain"], 1)
            dve.wait_ge(s["ichain"], 3)
            dve.tensor_tensor(gidx[:, :, :], gfl[:, :, :], c.slot_at[:, :, :], ALU.add).then_inc(s["ichain"], 1)
            dve.wait_ge(s["ichain"], 4)
            dve.wait_ge(s["bias_in"], 32)

            def pick(n):
                par = n[1]
                e = n[0] * 2 + n[1]
                wait(dve, s["rows_in" + str(par)], n[0] * (16 * TILES))
                wait(dve, s["act_h"], at(8, n, -8))
                dve.tensor_copy(gidx_e[par][:, :].unsqueeze(1), gidx[:, bass.ds(e, 1), :]).then_inc(s["picked"], 1)
                dve.tensor_copy(b1_e[par][:, :].unsqueeze(1), b1_s[:, bass.ds(e, 1), :]).then_inc(s["small"], 1)

            def gates(n):
                par = n[1]
                e = n[0] * 2 + n[1]
                dve.wait_ge(rows_in[par], n[0] * (16 * TILES) + 16 * TILES)
                wait(dve, s["added"], at(16 * TILES, n, -16 * TILES))
                dve.tensor_copy(token[par][:, :], row[par][:, :, D])
                dve.tensor_scalar(wcol[par][:, :].unsqueeze(2), row[par][:, :, bass.ds(e + (D + 1), 1)],
                                  c.gates[:, 3:4], None, ALU.mult).then_inc(s["picked"], 1)

            def hidden(b, blk, ks):
                par = b[1]
                if blk == 0:
                    dve.wait_ge(s["small"], at(1, b, 1))
                for k in ks:
                    q = 8 * blk + k
                    dve.wait_ge(s["h_full"], at(16, b, q + 1))
                    dve.tensor_scalar(h[blk][:, k, :], hb[q % 4][:, :], b1_e[par][:, k:k + 1], 0.0, ALU.add, ALU.max).then_inc(s["dve_h"], 1)

            def result(b, blk):
                par = b[1]
                e = b[0] * 2 + b[1]
                if blk == 0:
                    dve.wait_ge(s["picked"], at(2, b, 2))
                for t in range(2):
                    trip = 2 * blk + t
                    dve.wait_ge(s["y_full"], at(4, b, trip + 1))
                    ys = y[par][:, 2 * trip:2 * trip + 2, :]
                    dve.tensor_tensor(ys, yb[t][:, :].rearrange("p (t d) -> p t d", t=2),
                                      b2_s[:, bass.ds(e, 1), :].to_broadcast([P, 2, D]), ALU.add).then_inc(s["y_evac"], 1)
                    dve.wait_ge(s["y_evac"], at(4, b, trip + 1))
                    for i in (2 * trip, 2 * trip + 1):
                        dve.tensor_scalar(y[par][:, i, :], y[par][:, i, :], wcol[par][:, i:i + 1], None, ALU.mult).then_inc(s["y_done"], 1)

            def prologue(n):
                pick(n)
                gates(n)
                hidden(n, 0, (1, 3, 5, 7))

            def iteration(cur, nxt):
                if nxt:
                    pick(nxt)
                hidden(cur, 1, (1, 3, 5, 7))
                result(cur, 0)
                if nxt:
                    gates(nxt)
                    hidden(nxt, 0, (1, 3, 5, 7))
                result(cur, 1)

            pipeline(dve, E1, prologue, iteration)

        @block.gpsimd
        def _(pool):
            def gather(n):
                par = n[1]
                wait_apart(pool, s["picked"], at(2, n, 1), s["passed"])
                wait_apart(pool, s["x_full"], at(4, n, -4), s["passed"])
                wait_apart(pool, s["y_done"], at(TILES, n, -TILES), s["passed"])
                for i in range(TILES):
                    pool.indirect_dma_start(row[par][:, i, :], None, rows, bass.IndirectOffsetOnAxis(gidx_e[par][:, i:i + 1], 0),
                                            bounds_check=2 * SLOTS - 1, oob_is_err=True).then_inc(rows_in[par], 16)

            def add(b):
                par = b[1]
                wait_apart(pool, s["added"], at(16 * TILES, b, 0), s["passed"])
                for i in range(TILES):
                    wait_apart(pool, s["y_done"], at(TILES, b, i + 1), s["passed"])
                    pool.indirect_dma_start(x, bass.IndirectOffsetOnAxis(token[par][:, i:i + 1], 0), y[par][:, i, :], None,
                                            bounds_check=T + SPARE - 1, oob_is_err=True, compute_op=ALU.add).then_inc(s["added"], 16)

            def iteration(cur, nxt):
                if nxt:
                    gather(nxt)
                add(cur)

            pipeline(pool, E1, gather, iteration)
            pool.wait_ge(s["added"], 16 * TILES * E1)


def program(nc, a, out, stage=4):
    with ExitStack() as ctx:
        c = Chip(nc, ctx)
        dram = lambda n, shape, dt=F32: nc.dram_tensor(n, shape, dt, kind="Internal").ap()
        x1 = dram("x_after_l0", (T + SPARE, D))
        x3 = dram("x_after_l1", (T + SPARE, D))
        rows0 = dram("rows0", (SLOTS, W0))
        rows1 = dram("rows1", (2 * SLOTS, W1))
        qk_dram = [dram(f"qk_parts{i}", (2, 3, D, S), BF16) for i in range(2)]
        mask_dram = dram("mask_parts", (3, B, S), BF16)
        flat = lambda ap: ap.rearrange("b s d -> (b s) d")
        constants(c, a["g_xattn"], a["g_ffn"], rows0, rows1, x1, x3)
        pre = "L0_xattn_"
        attention(c, 0, flat(a["x"]), flat(a["ctx_1024"]), a["mask_BxS2_ff0"],
                  *(a[pre + n] for n in ("Wq", "bq", "Wk", "bk", "Wv", "bv", "Wp", "bp")),
                  a["L0_ffn_gate_weight"], x1, rows0, qk_dram, mask_dram)
        if stage > 1:
            experts0(c, rows0, a["L0_ffn_gate_up_proj"], a["L0_ffn_down_proj"], x1)
        if stage > 2:
            pre = "L1_xattn_"
            tot0 = sb(c, ctx, "tot0", [P, E1])
            attention(c, 1, x1, flat(a["ctx_1024"]), a["mask_Bx1xS_if1"].rearrange("b o s -> (b o s)"),
                      *(a[pre + n] for n in ("Wq", "bq", "Wk", "bk", "Wv", "bv", "Wo", "bo")),
                      a["L1_ffn_wg"], x3, rows1, qk_dram, mask_dram, tot0)
        if stage > 3:
            pre = "L1_ffn_"
            experts1(c, rows1, *(a[pre + n] for n in ("w1", "b1", "w2", "b2")), x3, tot0, flat(out))
        if stage < 4:
            with nc.semaphore("dbg") as dbg, nc.Block() as block:
                @block.sync
                def _(sp):
                    sp.dma_start(flat(out), (x3 if stage == 3 else x1)[0:T, :]).then_inc(dbg, 16)
                    sp.wait_ge(dbg, 16)


STAGE = 4


def kernel(**inputs):
    import numpy as np
    import concourse.bacc as bacc
    from concourse.bass_utils import run_bass_kernel_spmd

    nc = bacc.Bacc("TRN2", target_bir_lowering=False, num_devices=1)
    arrays, args = {}, {}
    for name, value in inputs.items():
        a = np.ascontiguousarray(value)
        arrays[f"in_{name}"] = a
        args[name] = nc.dram_tensor(f"in_{name}", a.shape, mybir.dt.from_np(a.dtype), kind="ExternalInput").ap()
    out = nc.dram_tensor("out_x", (B, S, D), F32, kind="ExternalOutput").ap()
    program(nc, args, out, STAGE)
    r = run_bass_kernel_spmd(nc, [arrays], core_ids=[0])
    return r.results[0]["out_x"]
```

```python
from contextlib import ExitStack

import concourse.bass as bass
from concourse import mybir
from concourse.alu_op_type import AluOpType as ALU

F32 = mybir.dt.float32
BF16 = mybir.dt.bfloat16
U32 = mybir.dt.uint32
I32 = mybir.dt.int32
ACT = mybir.ActivationFunctionType
AX = mybir.AxisListType

P = 128
B, S, D = 8, 512, 256
T = B * S
HEADS, DH = 16, 16
NT = S // P
NC = D // P
GROUPS = HEADS // 4
EPS = 1e-5
SCALE = DH ** -0.5
HIDDEN = -float(2 ** 100)

Q_TERM = (0, 0, 1, 1, 0, 2)
K_TERM = (0, 1, 0, 1, 2, 0)
STACK = DH * len(Q_TERM)
ROW_MASK = STACK
ROW_SHIFT = STACK + 3
ROWS = STACK + 6

E0, CAP0, F0, K0 = 32, 256, 192, 8
E1, CAP1, F1, K1 = 8, 1024, 1024, 2
W0 = D + 1 + E0
W1 = D + 1 + E1
SLOTS = E0 * CAP0
SPARE = CAP1
NOWHERE0 = 16384.0
NOWHERE1 = 32768.0

N_PREP = 10
N_POST = 6


class Chip:

    def __init__(self, nc, ctx):
        self.nc, self.ctx = nc, ctx


def sb(c, ctx, name, shape, dt=F32):
    return ctx.enter_context(c.nc.sbuf_tensor(name, shape, dt))


class Semaphores:

    def __init__(self, nc):
        self.nc, self.taken = nc, []

    def __enter__(self):
        return self

    def __call__(self, name):
        self.taken.append(self.nc.alloc_semaphore(name=name))
        return self.taken[-1]

    def __exit__(self, *_):
        self.nc.clear_and_free_semaphores(self.taken)
        self.nc.all_engine_barrier()


def count(per, half, par, extra=0):
    return half * (2 * per) + (per * par + extra)


def wait(eng, sem, value):
    if isinstance(value, int) and value <= 0:
        return
    eng.wait_ge(sem, value)


def wait_apart(eng, sem, value, passed):
    wait(eng, sem, value)
    if not isinstance(value, int):
        eng.sem_inc(passed, 1)


def pipeline(eng, n_items, prologue, iteration):
    prologue((0, 0))
    iteration((0, 0), (0, 1))
    with eng.Fori(1, n_items // 2) as it:
        iteration((it - 1, 1), (it, 0))
        iteration((it, 0), (it, 1))
    iteration((n_items // 2 - 1, 1), None)


def deep_pipeline(eng, n_items, depth, iteration):
    def items(half, par):
        return [(half + (par + k) // 2, (par + k) % 2) for k in range(-1, depth + 1)]

    def single(i):
        iteration([x if 0 <= 2 * x[0] + x[1] < n_items else None for x in items(i // 2, i % 2)])

    single(0)
    looped = (n_items - depth - 1) // 2
    with eng.Fori(0, looped) as it:
        iteration(items(it, 1))
        iteration(items(it + 1, 0))
    for i in range(2 * looped + 1, n_items + 1):
        single(i)


def constants(c, g_xattn, g_ffn, rows0, rows1, x1, x3):
    nc, ctx = c.nc, c.ctx
    c.ident = sb(c, ctx, "ident", [P, P])
    c.identb = sb(c, ctx, "identb", [P, P], BF16)
    c.before = sb(c, ctx, "before", [P, P], BF16)
    c.onesb = sb(c, ctx, "onesb", [P, P], BF16)
    c.hide_st = sb(c, ctx, "hide_st", [P, P], BF16)
    c.hide_max = sb(c, ctx, "hide_max", [P, P], BF16)
    c.gates = sb(c, ctx, "gates", [P, 4])
    c.mhalf = sb(c, ctx, "mhalf", [P, NT])
    c.tok0 = sb(c, ctx, "tok0", [P, NT])
    c.key0 = sb(c, ctx, "key0", [P, E0])
    c.key1 = sb(c, ctx, "key1", [P, 2, E1])
    c.eid = sb(c, ctx, "eid", [P, E1])
    c.slot_in = sb(c, ctx, "slot_in", [P, E1, CAP1 // P])
    c.slot_at = sb(c, ctx, "slot_at", [P, E1, CAP1 // P])
    c.empty0 = ctx.enter_context(nc.semaphore("empty0"))
    with ExitStack() as tmp:
        ii = sb(c, tmp, "ii", [P, 256], I32)
        empty = sb(c, tmp, "empty", [P, SPARE // P, W0])
        sem = lambda n: tmp.enter_context(nc.semaphore(n))
        gate_in, tables, empty_set, empty_out, iota_s, made = (
            sem(n) for n in ("gate_in", "tables", "empty_set", "empty_out", "iota_s", "made"))
        block = tmp.enter_context(nc.Block())

        @block.sync
        def _(sp):
            sp.dma_start(c.gates[:, 0:2], g_xattn.partition_broadcast(P)).then_inc(gate_in, 16)
            sp.dma_start(c.gates[:, 2:4], g_ffn.partition_broadcast(P)).then_inc(gate_in, 16)
            sp.wait_ge(empty_set, 2)
            sp.dma_start(rows0[0:SPARE, :].rearrange("(t p) w -> p t w", p=P), empty[:, :, :]).then_inc(empty_out, 16)
            sp.dma_start(rows1[0:SPARE, :].rearrange("(t p) w -> p t w", p=P), empty[:, :, 0:W1]).then_inc(empty_out, 16)
            for x in (x1, x3):
                sp.dma_start(x[T:T + SPARE, :].rearrange("(t p) d -> p t d", p=P), empty[:, :, 0:D]).then_inc(empty_out, 16)
            sp.wait_ge(empty_out, 64)
            for at in range(SPARE, SLOTS, SPARE):
                sp.dma_start(rows0[at:at + SPARE, :], rows0[0:SPARE, :]).then_inc(c.empty0, 16)

        @block.scalar
        def _(act):
            act.wait_ge(gate_in, 32)
            act.activation(c.gates[:, :], c.gates[:, :], ACT.Tanh).then_inc(made, 1)

        @block.vector
        def _(dve):
            dve.memset(empty[:, :, :], 0.0).then_inc(made, 1)
            dve.wait_ge(made, 2)
            dve.wait_ge(iota_s, 1)
            dve.tensor_copy(empty[:, :, D:D + 1], ii[:, 200:200 + SPARE // P].unsqueeze(2)).then_inc(empty_set, 1)
            dve.memset(c.onesb[:, :], 1.0)
            dve.memset(c.mhalf[:, :], -0.5).then_inc(empty_set, 1)
            dve.wait_ge(iota_s, 2)
            dve.tensor_copy(c.tok0[:, :], ii[:, 1:1 + NT])
            dve.tensor_copy(c.key0[:, :], ii[:, 8:8 + E0])
            dve.tensor_copy(c.key1[:, :, :], ii[:, 40:56].rearrange("p (k e) -> p k e", k=2))
            dve.tensor_copy(c.eid[:, :], ii[:, 56:64])
            n = E1 * (CAP1 // P)
            dve.tensor_copy(c.slot_in[:, :, :], ii[:, 64:64 + n].rearrange("p (e s) -> p e s", e=E1))
            dve.tensor_copy(c.slot_at[:, :, :], ii[:, 128:128 + n].rearrange("p (e s) -> p e s", e=E1)).then_inc(made, 1)

        @block.gpsimd
        def _(pool):
            pool.iota(ii[:, 200:200 + SPARE // P], pattern=[[P, SPARE // P]], base=T, channel_multiplier=1).then_inc(iota_s, 1)
            pool.iota(ii[:, 1:1 + NT], pattern=[[P, NT]], base=0, channel_multiplier=1)
            pool.iota(ii[:, 8:8 + E0], pattern=[[-CAP0, E0]], base=int(NOWHERE0), channel_multiplier=0)
            pool.iota(ii[:, 40:56].rearrange("p (k e) -> p k e", k=2), pattern=[[-SLOTS, 2], [-CAP1, E1]],
                      base=int(NOWHERE1), channel_multiplier=0)
            pool.iota(ii[:, 56:64], pattern=[[1, E1]], base=0, channel_multiplier=0)
            n = CAP1 // P
            pool.iota(ii[:, 64:64 + E1 * n].rearrange("p (e s) -> p e s", e=E1),
                      pattern=[[0, E1], [P, n]], base=0, channel_multiplier=1)
            pool.iota(ii[:, 128:128 + E1 * n].rearrange("p (e s) -> p e s", e=E1),
                      pattern=[[CAP1, E1], [P, n]], base=0, channel_multiplier=1).then_inc(iota_s, 1)
            pool.memset(c.ident[:, :], 0.0)
            pool.memset(c.identb[:, :], 0.0)
            pool.memset(c.before[:, :], 1.0)
            pool.memset(c.hide_st[:, :], 0.0)
            pool.memset(c.hide_max[:, :], 0.0).then_inc(tables, 1)
            pool.wait_ge(tables, 1)
            for m in (c.ident, c.identb):
                pool.affine_select(out=m[:, :], in_=m[:, :], compare_op=ALU.not_equal, fill=1.0,
                                   base=0, pattern=[[-1, P]], channel_multiplier=1)
            pool.affine_select(out=c.before[:, :], in_=c.before[:, :], compare_op=ALU.is_gt, fill=0.0,
                               base=0, pattern=[[1, P]], channel_multiplier=-1)
            pool.affine_select(out=c.hide_st[:, :], in_=c.hide_st[:, :], compare_op=ALU.is_ge, fill=HIDDEN,
                               base=0, pattern=[[1, P]], channel_multiplier=-1)
            pool.affine_select(out=c.hide_max[:, :], in_=c.hide_max[:, :], compare_op=ALU.is_ge, fill=HIDDEN,
                               base=0, pattern=[[-1, P]], channel_multiplier=1).then_inc(tables, 1)
            pool.wait_ge(tables, 2)


def attention(c, layer, x_in, ctx_in, mask, wq, bq, wk, bk, wv, bv, wp, bp, wroute, x_out, rows,
              qk_dram, mask_dram, tot0=None):
    nc = c.nc
    causal = layer == 0
    E = E0 if layer == 0 else E1
    CAP = CAP0 if layer == 0 else CAP1
    W = W0 if layer == 0 else W1
    NSEL = 1 if layer == 0 else 2
    NSCAT = NT * (K0 if layer == 0 else K1)
    NOWHERE = NOWHERE0 if layer == 0 else NOWHERE1
    LAST_ROW = SLOTS - 1 if layer == 0 else 2 * SLOTS - 1

    with ExitStack() as ctx:
        t_ = lambda name, shape, dt=F32: sb(c, ctx, f"{name}_{layer}", shape, dt)
        phase_sems = ctx.enter_context(Semaphores(nc))
        sem = lambda n: phase_sems(f"{n}_{layer}")
        wq_s, wk_s, wv_s = (t_(n, [P, NC, D]) for n in ("wq", "wk", "wv"))
        wp_s = t_("wp", [P, GROUPS, D])
        bq_s, bk_s = t_("bq", [P, NC]), t_("bk", [P, NC])
        bp_s = t_("bp", [P, D])
        wr_s = t_("wr", [P, NC, E])
        xin = t_("xin", [P, NT, D])
        xres = t_("xres", [P, NT, D])
        crow = t_("crow", [P, NT, D])
        xn = t_("xn", [P, NT, D])
        xT = t_("xT", [P, NC, S])
        cT = t_("cT", [P, NC, S])
        yT = t_("yT", [P, NC, S])
        qk = t_("qk", [P, 2, NC, S])
        parts = t_("parts", [P, 2, 3, NC, S], BF16)
        qst = [t_(f"qst{i}", [ROWS, HEADS, S], BF16) for i in range(2)]
        kst = [t_(f"kst{i}", [ROWS, HEADS, S], BF16) for i in range(2)]
        va = [t_(f"va{i}", [P, NT, HEADS, 32]) for i in range(2)]
        pt = t_("pt", [P, 8, 2 * S])
        on = t_("on", [P, GROUPS, S])
        den = t_("den", [P, S])
        nmx = t_("nmx", [P, NT, HEADS])
        m3 = t_("m3", [P, NT, 3, HEADS], BF16)
        m3T = t_("m3T", [3 * HEADS, S], BF16)
        st6, mv = t_("st6", [P, NT, 6]), t_("mv", [P, NT, 2])
        st6b, mvb = t_("st6b", [P, NT, 6]), t_("mvb", [P, NT, 2])
        rstd, rstdb = t_("rstd", [P, NT]), t_("rstdb", [P, NT])
        rowb = t_("rowb", [P, NT, W])
        lgs, ex, rep = t_("lgs", [P, NT, E]), t_("ex", [P, NT, E]), t_("rep", [P, NT, E])
        lmx, rec, tok = t_("lmx", [P, NT]), t_("rec", [P, NT]), t_("tok", [P, NT])
        v8, k8 = t_("v8", [P, NT, 8]), t_("k8", [P, NT, 8])
        i8 = t_("i8", [P, NT, 8], U32)
        i8f = t_("i8f", [P, NT, 8])
        sel = t_("sel", [P, NSEL, NT, E], BF16)
        selsum = t_("selsum", [P, NT, E])
        pos, okay = t_("pos", [P, NSEL, NT, E]), t_("okay", [P, NSEL, NT, E])
        base = t_("base", [P, NSEL, E])
        bvc = t_("bvc", [P, GROUPS])
        idx = t_("idx", [P, NT, 8], U32)
        maskq = t_("maskq", [P, S]) if layer else None
        maski = t_("maski", [P, S], I32) if layer else None

        work = ctx.enter_context(nc.psum_tensor(f"work_{layer}", [P, 512], F32))
        mxb = [ctx.enter_context(nc.psum_tensor(f"mxb{i}_{layer}", [P, 512], F32)) for i in range(2)]
        stb = [ctx.enter_context(nc.psum_tensor(f"stb{i}_{layer}", [P, 1024], F32)) for i in range(2)]
        ob = ctx.enter_context(nc.psum_tensor(f"ob_{layer}", [P, 512], F32))

        with ExitStack() as tmp:
            w_in, w_zero, w_t, w_put, w_ones, bv_rdy, bv_out, bv_sum = (
                tmp.enter_context(nc.semaphore(f"{n}_{layer}")) for n in
                ("w_in", "w_zero", "w_t", "w_put", "w_ones", "bv_rdy", "bv_out", "bv_sum"))
            w_chain = tmp.enter_context(nc.semaphore(f"w_chain_{layer}"))
            m_out = tmp.enter_context(nc.semaphore(f"m_out_{layer}"))
            if layer == 0:
                route_nat = pt[0:E0, 0, 0:D]
                mrow = pt[0:B, 1, 0:S]
                mparts = parts[0:B, 0, 0:3, 0, :]
            else:
                nat = [pt[:, i, 0:NC * D].rearrange("p (c n) -> p c n", c=NC) for i in range(3)]
                wo_nat = pt[:, 4, 0:NC * GROUPS * 128].rearrange("p (c g j d) -> p c g j d", c=NC, g=GROUPS, j=4)
            block = tmp.enter_context(nc.Block())

            @block.sync
            def _(sp):
                n = 0
                for w, s in ((wq, wq_s), (wk, wk_s), (wv, wv_s)):
                    dst = s[:, :, :] if layer == 0 else nat[n // 16]
                    sp.dma_start(dst, w.rearrange("(c p) n -> p c n", p=P)).then_inc(w_in, 16)
                    n += 16
                for b_, s in ((bq, bq_s), (bk, bk_s)):
                    sp.dma_start(s[:, :], b_.rearrange("(c p) -> p c", p=P), allow_slow_non_contiguous=True).then_inc(w_in, 16)
                sp.dma_start(bp_s[:, :], bp.partition_broadcast(P)).then_inc(w_in, 16)
                sp.wait_ge(w_zero, 1)
                bv_src = bv.rearrange("(g j d) -> j d g", g=GROUPS, j=4)
                for j in range(4):
                    sp.dma_start(bvc[32 * j:32 * j + DH, :], bv_src[j], allow_slow_non_contiguous=True).then_inc(w_in, 16)
                for st in (*qst, *kst):
                    sp.dma_start(st[STACK:ROWS, :, :], m3T[0:ROWS - STACK, :].unsqueeze(1).to_broadcast([ROWS - STACK, HEADS, S])).then_inc(w_ones, 16)
                if layer == 0:
                    sp.dma_start(route_nat, wroute).then_inc(w_in, 16)
                    sp.dma_start(mrow, mask).then_inc(w_in, 16)
                    src = wp.rearrange("(g j d) n -> j d g n", g=GROUPS, j=4)
                    for j in range(4):
                        sp.dma_start(wp_s[32 * j:32 * j + DH, :, :], src[j]).then_inc(w_in, 16)
                    sp.wait_ge(w_chain, 7)
                    sp.dma_start(mask_dram.rearrange("r b s -> b r s"), mparts).then_inc(m_out, 16)
                    sp.wait_ge(m_out, 16)
                else:
                    sp.dma_start(wr_s[:, :, :], wroute.rearrange("(c p) e -> p c e", p=P)).then_inc(w_in, 16)
                    src = wp.rearrange("(c p) (g j d) -> p c g j d", p=P, g=GROUPS, j=4)
                    for cc in range(NC):
                        for g in range(GROUPS):
                            sp.dma_start(wo_nat[:, cc, g, :, 0:DH], src[:, cc, g]).then_inc(w_in, 16)

                sp.wait_ge(w_ones, 64)

            n_in = 16 * (10 + 2 + 4) if layer == 0 else 16 * (10 + 1 + NC * GROUPS)

            @block.tensor
            def _(pe):
                pe.wait_ge(w_in, n_in)
                if layer == 0:
                    for cc in range(NC):
                        last = pe.transpose(work[:, cc * E0:(cc + 1) * E0], route_nat[:, cc * P:(cc + 1) * P], c.ident[0:E0, 0:E0])
                    last.then_inc(w_t, 1)
                else:
                    for m, bank in ((0, work), (1, mxb[0]), (2, mxb[1])):
                        for co in range(NC):
                            for ci in range(NC):
                                last = pe.transpose(bank[:, ci * D + co * P:ci * D + (co + 1) * P],
                                                    nat[m][:, co, ci * P:(ci + 1) * P], c.ident[:, :])
                        last.then_inc(w_t, 1)
                    for g in range(GROUPS):
                        for co in range(NC):
                            last = pe.transpose(stb[0][:, g * D + co * P:g * D + (co + 1) * P],
                                                wo_nat[:, co, g, :, :].rearrange("p j d -> p (j d)"), c.ident[:, :])
                    last.then_inc(w_t, 1)
                pe.wait_ge(bv_rdy, 1)
                for g in range(GROUPS):
                    last = pe.matmul(stb[1][:, 0:D], den[:, g * P:(g + 1) * P], wp_s[:, g, :], start=g == 0, stop=g == GROUPS - 1)
                last.then_inc(bv_out, 1)

            @block.vector
            def _(dve):
                dve.memset(m3T[0:ROWS - STACK, :], 1.0)
                dve.memset(bvc[:, :], 0.0)
                dve.memset(wp_s[:, :, :] if layer == 0 else wo_nat, 0.0).then_inc(w_zero, 1)
                dve.memset(den[:, :], 1.0).then_inc(w_chain, 1)
                for i in range(2):
                    dve.memset(va[i][:, :, :, DH:32], 1.0)
                dve.memset(base[:, :, :], 0.0)
                dve.tensor_copy(tok[:, :], c.tok0[:, :])
                dve.wait_ge(w_in, n_in)
                dve.tensor_scalar(bp_s[:, :], bp_s[:, :], c.gates[:, layer:layer + 1], None, ALU.mult).then_inc(bv_sum, 1)
                if layer == 0:
                    dve.tensor_scalar(mrow, mrow, 1.0 / SCALE, None, ALU.mult).then_inc(w_chain, 1)
                    for r in range(3):
                        dve.wait_ge(w_chain, 2 + 2 * r)
                        dve.tensor_copy(mparts[:, r, :], mrow).then_inc(w_chain, 1)
                        if r < 2:
                            dve.wait_ge(w_chain, 3 + 2 * r)
                            dve.tensor_tensor(mrow, mrow, mparts[:, r, :], ALU.subtract).then_inc(w_chain, 1)
                    dve.tensor_scalar(wp_s[:, :, :], wp_s[:, :, :], c.gates[:, 0:1], None, ALU.mult)
                    dve.wait_ge(w_t, 1)
                    dve.tensor_copy(wr_s[:, :, :], work[:, 0:NC * E0].rearrange("p (c e) -> p c e", c=NC)).then_inc(w_put, 1)
                else:
                    for n, (s, bank) in enumerate(((wq_s, work), (wk_s, mxb[0]), (wv_s, mxb[1]))):
                        dve.wait_ge(w_t, n + 1)
                        dve.tensor_copy(s[:, :, :], bank[:, :].rearrange("p (c n) -> p c n", c=NC))
                    dve.wait_ge(w_t, 4)
                    dve.tensor_scalar(wp_s[:, :, :], stb[0][:, :].rearrange("p (g n) -> p g n", g=GROUPS),
                                      c.gates[:, 1:2], None, ALU.mult).then_inc(w_put, 1)
                dve.wait_ge(w_chain, 1)
                for g in range(GROUPS):
                    last = dve.tensor_scalar(den[:, g * P:(g + 1) * P], den[:, g * P:(g + 1) * P], bvc[:, g:g + 1], None, ALU.mult)
                dve.wait_ge(w_put, 1)
                last.then_inc(bv_rdy, 1)
                dve.wait_ge(bv_out, 1)
                dve.wait_ge(bv_sum, 1)
                dve.tensor_tensor(bp_s[:, :], bp_s[:, :], stb[1][:, 0:D], ALU.add).then_inc(bv_sum, 1)

        names = ("ld0", "ld1", "res_in", "parts_out", "shift_in", "x_out", "scat",
                 "prep_full", "prep_evac", "post_full", "post_evac", "shift_full", "shift_evac",
                 "max_full", "max_free", "st_full", "st_free", "pt_free", "norm_done",
                 "stat_rdy", "rstd_rdy", "xn_rdy", "xres_rdy", "hi_rdy", "rest_rdy", "mid_rdy", "split_rdy", "m3_rdy",
                 "mchain", "nchain", "nchain2", "stat2_rdy", "rstd2_rdy", "row_rdy", "lg_rdy", "ex_rdy", "sel_rdy",
                 "idx_rdy", "vchain", "rchain", "pchain", "pchain2", "passed", "x_rdy", "mq_rdy", "row_free")
        s = {n: sem(n) for n in names}
        ld = (s["ld0"], s["ld1"])
        stack_in = [[sem(f"stack_in{i}_{g}") for g in range(GROUPS)] for i in range(2)]
        N_LD = 48 if layer else 32
        N_STACK = 16 * (13 if causal else 12)

        def span(pair):
            if not causal:
                return 0, 2 * S, ((2 * pair, 0, 0), (2 * pair + 1, S, 0))
            if pair == 0:
                return 0, 2 * S - P, ((0, 0, 0), (1, S, P))
            return 2 * P, 2 * P * 2 + P, ((2, 2 * P, 2 * P), (3, S, 3 * P))

        block = ctx.enter_context(nc.Block())

        def at(per, b, extra=0):
            return count(per, b[0], b[1], extra)

        def half_of(b, per, extra=0):
            return b[0] * per + extra

        def rows_of(b):
            return bass.ds(b[0] * (2 * S) + b[1] * S, S) if not isinstance(b[0], int) else slice((2 * b[0] + b[1]) * S, (2 * b[0] + b[1] + 1) * S)

        TRIPS = ((("prep", 0), ("prep", 1)), (("post", 0), ("post", 1)), (("prep", 2), ("prep", 3)),
                 (("prep", 4), ("prep", 5)), (("prep", 6), ("prep", 7)), (None, ("post", 2)),
                 (("post", 3), ("post", 4)), (None, ("post", 5)))

        @block.sync
        def _(sp):
            def load(n):
                par = n[1]
                wait_apart(sp, s["xn_rdy"], at(1, n, 0), s["passed"])
                wait_apart(sp, s["prep_full"], at(N_PREP, n, -N_PREP + 6), s["passed"])
                if layer:
                    wait_apart(sp, s["mq_rdy"], at(1, n, 0), s["passed"])
                sp.dma_start(xin[:, :, :], x_in[rows_of(n), :].rearrange("(t p) d -> p t d", p=P)).then_inc(ld[par], 16)
                sp.dma_start(crow[:, :, :], ctx_in[rows_of(n), :].rearrange("(t p) d -> p t d", p=P)).then_inc(ld[par], 16)
                if layer:
                    sp.dma_start(maski[:, :], mask[rows_of(n)].partition_broadcast(P)).then_inc(ld[par], 16)

            def load_residual(b):
                wait_apart(sp, s["x_out"], at(16, b, 0), s["passed"])
                wait_apart(sp, s["row_rdy"], at(1, b, 0), s["passed"])
                sp.dma_start(xres[:, :, :], x_in[rows_of(b), :].rearrange("(t p) d -> p t d", p=P)).then_inc(s["res_in"], 16)

            def parts_store(n):
                wait_apart(sp, s["split_rdy"], at(2, n, 2), s["passed"])
                for g in range(GROUPS):
                    wait_apart(sp, stack_in[n[1]][g], half_of(n, N_STACK), s["passed"])
                sp.dma_start(qk_dram[n[1]].rearrange("i r (c p) s -> p (i r c) s", p=P),
                             parts[:, :, :, :, :].rearrange("p i r c s -> p (i r c) s")).then_inc(s["parts_out"], 16)
                wait_apart(sp, s["parts_out"], at(16, n, 16), s["passed"])

            def stack(n, g):
                par = n[1]
                wait_apart(sp, s["st_free"], at(32, n, -64 + 8 * g + 8), s["passed"])
                for side, dst, terms in ((0, qst, Q_TERM), (1, kst, K_TERM)):
                    for r, term in enumerate(terms):
                        sp.dma_start(dst[par][DH * r:DH * r + DH, 4 * g:4 * g + 4, :],
                                     qk_dram[par][side, term].rearrange("(h d) s -> d h s", d=DH)[:, 4 * g:4 * g + 4, :]).then_inc(stack_in[par][g], 16)
                if causal:
                    m = mask_dram[:, bass.ds(n[0] * 2 + n[1], 1), :] if not isinstance(n[0], int) else mask_dram[:, 2 * n[0] + n[1]:2 * n[0] + n[1] + 1, :]
                    sp.dma_start(kst[par][ROW_MASK:ROW_MASK + 3, 4 * g:4 * g + 4, :], m.to_broadcast([3, 4, S])).then_inc(stack_in[par][g], 16)

            def store(b):
                wait_apart(sp, s["x_rdy"], at(1, b, 1), s["passed"])
                sp.dma_start(x_out[rows_of(b), :].rearrange("(t p) d -> p t d", p=P), xres[:, :, :]).then_inc(s["x_out"], 16)

            for n in ((0, 0), (0, 1)):
                load(n)
                parts_store(n)
                for g in range(GROUPS):
                    stack(n, g)
            load((1, 0))

            def iteration(items):
                prev, cur, nxt, nn, n3 = items
                if n3:
                    load(n3)
                if prev:
                    store(prev)
                if cur:
                    load_residual(cur)
                if nn:
                    parts_store(nn)
                    for g in range(GROUPS):
                        stack(nn, g)

            deep_pipeline(sp, B, 3, iteration)
            sp.wait_ge(s["x_out"], 16 * B)
            if layer == 0:
                sp.wait_ge(c.empty0, 16 * (SLOTS // SPARE - 1))

        @block.tensor
        def _(pe):
            last_trip = [None]

            def bank_free(kind, b, t):
                before, last_trip[0] = last_trip[0], (kind, b, t)
                if before:
                    kind, b, t = before
                    pe.wait_ge(s[kind + "_evac"], at({"prep": N_PREP, "post": N_POST, "shift": 1}[kind], b, t + 1))

            def prep(n, t):
                par = n[1]
                bank_free("prep", n, t)
                if t == 0:
                    pe.wait_ge(s["xn_rdy"], at(1, n, 1))
                elif t == 4:
                    pe.wait_ge(ld[par], half_of(n, N_LD, N_LD))
                elif t == 8:
                    wait(pe, s["pt_free"], at(8, n, -8))
                if t in (0, 1, 4, 5):
                    src, cc = (xn, crow)[t // 4], t % 2
                    for i in range(NT):
                        last = pe.transpose(work[:, i * P:(i + 1) * P], src[:, i, cc * P:(cc + 1) * P], c.ident[:, :])
                elif t < 8:
                    w, act_, co = ((wq_s, xT), (wk_s, cT))[t // 4] + (t % 2,)
                    for ci in range(NC):
                        last = pe.matmul(work[:, :], w[:, ci, co * P:(co + 1) * P], act_[:, ci, :],
                                         start=ci == 0, stop=ci == NC - 1)
                else:
                    for i in range(2):
                        tt = 2 * (t - 8) + i
                        for ci in range(NC):
                            last = pe.matmul(work[:, i * D:(i + 1) * D], cT[:, ci, tt * P:(tt + 1) * P], wv_s[:, ci, :],
                                             start=ci == 0, stop=ci == NC - 1)
                last.then_inc(s["prep_full"], 1)

            def maxima(n, u0, u1):
                par = n[1]
                rows_used = STACK + 3 if causal else STACK
                for u in range(u0, u1):
                    h, qt = u // NT, u % NT
                    if u % 16 == 0:
                        pe.wait_ge(stack_in[par][u // 16], half_of(n, N_STACK, N_STACK))
                    wait(pe, s["max_free"], at(64, n, u - 1))
                    nk = (qt + 1) * P if causal else S
                    last = pe.matmul(mxb[u % 2][:, 0:nk], qst[par][0:rows_used, h, qt * P:(qt + 1) * P],
                                     kst[par][0:rows_used, h, 0:nk], start=True, stop=not causal)
                    if causal:
                        last = pe.matmul(mxb[u % 2][:, nk - P:nk], c.identb[:, :], c.hide_max[:, :], start=False, stop=True)
                    last.then_inc(s["max_full"], 1)

            def shift(n):
                bank_free("shift", n, 0)
                pe.wait_ge(s["m3_rdy"], at(1, n, 1))
                for qt in range(NT):
                    last = pe.matmul(work[0:3 * HEADS, qt * P:(qt + 1) * P],
                                     m3[:, qt, :, :].rearrange("p r h -> p (r h)"), c.identb[:, :], start=True, stop=True)
                last.then_inc(s["shift_full"], 1)

            def scores(b, hf, j):
                par, g, pair = b[1], hf // 2, hf % 2
                u, h = 4 * hf + j, 4 * g + j
                if u == 0:
                    pe.wait_ge(s["shift_in"], at(48, b, 48))
                wait(pe, s["st_free"], at(32, b, u - 1))
                for kt, col, q0 in span(pair)[2]:
                    bank = stb[u % 2]
                    last = pe.matmul(bank[:, col:col + S - q0], kst[par][0:ROWS, h, kt * P:(kt + 1) * P],
                                     qst[par][0:ROWS, h, q0:S], start=True, stop=not causal)
                    if causal:
                        last = pe.matmul(bank[:, col:col + P], c.identb[:, :], c.hide_st[:, :], start=False, stop=True)
                last.then_inc(s["st_full"], 1)

            def values(b, hf):
                par, g, pair = b[1], hf // 2, hf % 2
                pe.wait_ge(s["st_free"], at(32, b, 4 * hf + 4))
                if pair == 0:
                    wait(pe, s["norm_done"], at(4, b, g))
                for kt, col, q0 in span(pair)[2]:
                    for j in range(4):
                        u, h = 4 * hf + j, 4 * g + j
                        last = pe.matmul(ob[32 * j:32 * j + 32, q0:S], va[par][:, kt, h, :],
                                         pt[:, u % 8, col:col + S - q0], start=kt == 0, stop=kt == NT - 1,
                                         tile_position=(0, 32 * j))
                last.then_inc(s["pt_free"], 1)

            def post(b, t):
                bank_free("post", b, t)
                if t == 0:
                    pe.wait_ge(s["norm_done"], at(4, b, 4))
                elif t == 2:
                    pe.wait_ge(s["row_rdy"], at(1, b, 1))
                elif t == 5:
                    pe.wait_ge(s["sel_rdy"], at(1, b, 1))
                if t < 2:
                    for i in range(2):
                        tt = 2 * t + i
                        for g in range(GROUPS):
                            last = pe.matmul(work[:, i * D:(i + 1) * D], on[:, g, tt * P:(tt + 1) * P], wp_s[:, g, :],
                                             start=g == 0, stop=g == GROUPS - 1)
                elif t < 4:
                    for i in range(NT):
                        last = pe.transpose(work[:, i * P:(i + 1) * P], rowb[:, i, (t - 2) * P:(t - 1) * P], c.ident[:, :])
                elif t == 4:
                    for i in range(NT):
                        for ci in range(NC):
                            last = pe.matmul(work[:, i * E:(i + 1) * E], yT[:, ci, i * P:(i + 1) * P], wr_s[:, ci, :],
                                             start=ci == 0, stop=ci == NC - 1)
                else:
                    for k in range(NSEL):
                        for i in range(NT + 1):
                            o = (k * (NT + 1) + i) * E
                            if i < NT:
                                last = pe.matmul(work[:, o:o + E], c.before[:, :], sel[:, k, i, :], start=True, stop=i == 0)
                            for ii in range(i):
                                last = pe.matmul(work[:, o:o + E], c.onesb[:, :], sel[:, k, ii, :],
                                                 start=i == NT and ii == 0, stop=ii == i - 1)
                last.then_inc(s["post_full"], 1)

            for n in ((0, 0), (0, 1)):
                for t in range(N_PREP):
                    prep(n, t)
            maxima((0, 0), 0, 64)
            shift((0, 0))

            def iteration(items):
                prev, cur, nxt, nn, _ = items
                if prev and nxt:
                    last_trip[0] = ("prep", nxt, N_PREP - 1)

                def trip(what):
                    kind, t = what or (None, None)
                    if kind == "prep" and nn:
                        prep(nn, t)
                    if kind == "post" and prev:
                        post(prev, t)

                for hf in range(8):
                    for j in range(4):
                        if cur:
                            scores(cur, hf, j)
                        if nxt:
                            maxima(nxt, 8 * hf + 2 * j, 8 * hf + 2 * j + 2)
                    trip(TRIPS[hf][0])
                    if cur and hf:
                        values(cur, hf - 1)
                    trip(TRIPS[hf][1])
                if cur:
                    values(cur, 7)
                if nxt:
                    shift(nxt)
                if nn:
                    prep(nn, 8)
                    prep(nn, 9)

            deep_pipeline(pe, B, 3, iteration)

        @block.scalar
        def _(act):
            def prep(n, t):
                par = n[1]
                if layer and t in (2, 3):
                    if t == 3:
                        act.wait_ge(s["prep_evac"], at(N_PREP, n, 4))
                        wait(act, s["parts_out"], at(16, n, 0))
                        act.activation(parts[:, 0, 0, :, :], qk[:, 0, :, :], ACT.Copy).then_inc(s["hi_rdy"], 1)
                    return
                act.wait_ge(s["prep_full"], at(N_PREP, n, t + 1))
                if t in (0, 1, 4, 5):
                    dst = (xT, cT)[t // 4][:, t % 2, :]
                    act.activation(dst, work[:, :], ACT.Copy).then_inc(s["prep_evac"], 1)
                elif t < 8:
                    side, cc = t // 4, t % 2
                    bias = (bq_s, bk_s)[side][:, cc:cc + 1]
                    if cc == 0:
                        wait(act, s["split_rdy"], at(2, n, side - 1))
                        wait(act, s["parts_out"], at(16, n, 0))
                    hi = act.activation(parts[:, side, 0, cc, :], work[:, :], ACT.Identity, bias=bias)
                    if cc == 1:
                        hi.then_inc(s["hi_rdy"], 1)
                    act.activation(qk[:, side, cc, :], work[:, :], ACT.Identity, bias=bias).then_inc(s["prep_evac"], 1)
                else:
                    i = 2 * (t - 8)
                    act.activation(va[par][:, i:i + 2, :, 0:DH], work[:, :].rearrange("p (t h d) -> p t h d", t=2, h=HEADS),
                                   ACT.Copy).then_inc(s["prep_evac"], 1)

            def exps(b, hf, js):
                pair = hf % 2
                if js[0] == 0:
                    wait(act, s["pt_free"], at(8, b, hf - 1))
                lo, hi, _ = span(pair)
                for j in js:
                    u = 4 * hf + j
                    act.wait_ge(s["st_full"], at(32, b, u + 1))
                    act.activation(pt[:, u % 8, lo:hi], stb[u % 2][:, lo:hi], ACT.Exp, scale=SCALE).then_inc(s["st_free"], 1)

            def shift(n):
                act.wait_ge(s["shift_evac"], at(1, n, 1))
                for r in range(3):
                    act.dma_start(qst[n[1]][ROW_SHIFT + r:ROW_SHIFT + r + 1, :, :],
                                  m3T[HEADS * r:HEADS * (r + 1), :]).then_inc(s["shift_in"], 16)

            def post(b, t):
                if t in (2, 3):
                    act.wait_ge(s["post_full"], at(N_POST, b, t + 1))
                    act.activation(yT[:, t - 2, :], work[:, :], ACT.Copy).then_inc(s["post_evac"], 1)

            def route(b):
                act.wait_ge(s["lg_rdy"], at(1, b, 1))
                act.activation(ex[:, :, :], lgs[:, :, :], ACT.Exp).then_inc(s["ex_rdy"], 1)

            for n in ((0, 0), (0, 1)):
                for t in range(N_PREP):
                    prep(n, t)
            shift((0, 0))

            def iteration(items):
                prev, cur, nxt, nn, _ = items
                for hf in range(8):
                    if cur:
                        exps(cur, hf, (0, 1))
                    if prev and hf == 7:
                        route(prev)
                    if cur:
                        exps(cur, hf, (2, 3))
                    for kind, t in (x for x in TRIPS[hf] if x):
                        if kind == "prep" and nn:
                            prep(nn, t)
                        if kind == "post" and prev:
                            post(prev, t)
                if nxt:
                    shift(nxt)
                if nn:
                    prep(nn, 8)
                    prep(nn, 9)

            deep_pipeline(act, B, 3, iteration)

        @block.vector
        def _(dve):
            def norm1(n):
                par = n[1]
                dve.wait_ge(ld[par], half_of(n, N_LD, N_LD))
                for i in range(NT):
                    dve.bn_stats(st6[:, i, :], xin[:, i, :]).then_inc(s["nchain"], 1)
                wait_apart(dve, s["nchain"], at(NT, n, NT), s["passed"])
                for i in range(NT):
                    dve.bn_aggr(mv[:, i, :], st6[:, i, :]).then_inc(s["stat_rdy"], 1)
                if layer:
                    wait(dve, s["prep_evac"], at(N_PREP, n, -N_PREP + 4))
                    dve.tensor_scalar(maskq[:, :], maski[:, :], 0.0, None, ALU.not_equal).then_inc(s["mq_rdy"], 1)

            def norm1_apply(n):
                dve.wait_ge(s["rstd_rdy"], at(1, n, 1))
                wait(dve, s["prep_full"], at(N_PREP, n, -N_PREP + 2))
                for i in range(NT):
                    last = dve.tensor_scalar(xn[:, i, :], xin[:, i, :], mv[:, i, 0:1], rstd[:, i:i + 1],
                                             ALU.subtract, ALU.mult)
                last.then_inc(s["xn_rdy"], 1)

            def prep(n, t):
                dve.wait_ge(s["prep_full"], at(N_PREP, n, t + 1))
                if t == 2:
                    wait(dve, s["split_rdy"], at(2, n, -1))
                    dve.wait_ge(s["mq_rdy"], at(1, n, 1))
                dve.scalar_tensor_tensor(out=qk[:, 0, t - 2, :], in0=work[:, :], scalar=bq_s[:, t - 2:t - 1],
                                         in1=maskq[:, :], op0=ALU.add, op1=ALU.mult).then_inc(s["prep_evac"], 1)

            def split(n, side):
                dve.wait_ge(s["rest_rdy"], at(2, n, side + 1))
                wait(dve, s["parts_out"], at(16, n, 0))
                dve.tensor_copy(parts[:, side, 1, :, :], qk[:, side, :, :]).then_inc(s["mid_rdy"], 1)

            def maxima(n, u0, u1):
                for u in range(u0, u1):
                    h, qt = u // NT, u % NT
                    nk = (qt + 1) * P if causal else S
                    dve.wait_ge(s["max_full"], at(64, n, u + 1))
                    dve.tensor_reduce(nmx[:, qt, h:h + 1], mxb[u % 2][:, 0:nk], AX.X, ALU.max, negate=True).then_inc(s["max_free"], 1)

            def shift(n):
                dve.wait_ge(s["max_free"], at(64, n, 64))
                wait(dve, s["shift_full"], at(1, n, 0))
                for r in range(3):
                    dve.tensor_copy(m3[:, :, r, :], nmx[:, :, :]).then_inc(s["mchain"], 1)
                    dve.wait_ge(s["mchain"], at(5, n, 2 * r + 1))
                    if r < 2:
                        dve.tensor_tensor(nmx[:, :, :], nmx[:, :, :], m3[:, :, r, :], ALU.subtract).then_inc(s["mchain"], 1)
                        dve.wait_ge(s["mchain"], at(5, n, 2 * r + 2))
                dve.sem_inc(s["m3_rdy"], 1)
                dve.wait_ge(s["shift_full"], at(1, n, 1))
                wait(dve, s["shift_in"], at(48, n, 0))
                dve.tensor_copy(m3T[:, :], work[0:3 * HEADS, :]).then_inc(s["shift_evac"], 1)

            def norm(b, g, part):
                if part == 0:
                    wait_apart(dve, s["pt_free"], at(8, b, 2 * g + 2), s["passed"])
                    dve.stream_shuffle(den[:, :], ob[:, :], [DH + i % DH for i in range(32)]).then_inc(s["vchain"], 1)
                elif part < 3:
                    dve.wait_ge(s["vchain"], at(12, b, 3 * g + 1))
                    piece = den[:, (part - 1) * (S // 2):part * (S // 2)]
                    dve.reciprocal(piece, piece).then_inc(s["vchain"], 1)
                else:
                    dve.wait_ge(s["vchain"], at(12, b, 3 * g + 3))
                    if g == 0:
                        wait(dve, s["post_full"], at(N_POST, b, -N_POST + 2))
                    dve.tensor_tensor(on[:, g, :], ob[:, :], den[:, :], ALU.mult).then_inc(s["norm_done"], 1)

            def post(b, t):
                dve.wait_ge(s["post_full"], at(N_POST, b, t + 1))
                if t == 0:
                    dve.wait_ge(s["xres_rdy"], at(1, b, 1))
                dve.tensor_tensor(xres[:, 2 * t:2 * t + 2, :], work[:, :].rearrange("p (t d) -> p t d", t=2),
                                  xres[:, 2 * t:2 * t + 2, :], ALU.add).then_inc(s["post_evac"], 1)

            def norm2(b):
                dve.wait_ge(s["post_evac"], at(N_POST, b, 2))
                dve.sem_inc(s["x_rdy"], 1)
                for i in range(NT):
                    dve.bn_stats(st6b[:, i, :], xres[:, i, :]).then_inc(s["nchain2"], 1)
                wait_apart(dve, s["nchain2"], at(NT, b, NT), s["passed"])
                for i in range(NT):
                    dve.bn_aggr(mvb[:, i, :], st6b[:, i, :]).then_inc(s["stat2_rdy"], 1)

            def norm2_apply(b):
                dve.wait_ge(s["rstd2_rdy"], at(1, b, 1))
                dve.wait_ge(s["row_free"], at(1, b, 1))
                for i in range(NT):
                    last = dve.tensor_scalar(rowb[:, i, 0:D], xres[:, i, :], mvb[:, i, 0:1], rstdb[:, i:i + 1],
                                             ALU.subtract, ALU.mult)
                last.then_inc(s["row_rdy"], 1)

            N_CH = 40

            link = [0]

            def route(b, step):
                if step == 0:
                    link[0] = 0

                def chain(ins):
                    link[0] += 1
                    ins.then_inc(s["rchain"], 1)
                    wait_apart(dve, s["rchain"], at(N_CH, b, link[0]), s["passed"])

                bc = lambda ap: ap.unsqueeze(2).to_broadcast([P, NT, E])
                lg = work[:, 0:NT * E].rearrange("p (t e) -> p t e", t=NT)
                if step == 0:
                    dve.wait_ge(s["post_full"], at(N_POST, b, 5))
                    chain(dve.tensor_reduce(lmx[:, :], lg, AX.X, ALU.max))
                    dve.tensor_tensor(lgs[:, :, :], lg, bc(lmx[:, :]), ALU.subtract).then_inc(s["lg_rdy"], 1)
                    dve.wait_ge(s["lg_rdy"], at(1, b, 1))
                    dve.sem_inc(s["post_evac"], 1)
                elif step == 1:
                    wait_apart(dve, s["ex_rdy"], at(1, b, 1), s["passed"])
                    for i in range(NT):
                        last = dve.max(v8[:, i, :], ex[:, i, :])
                    chain(last)
                    if layer == 0:
                        for i in range(NT):
                            last = dve.match_replace(rep[:, i, :], v8[:, i, :], ex[:, i, :], -1.0)
                        dve.tensor_reduce(rec[:, :], v8[:, :, :], AX.X, ALU.add)
                        chain(last)
                        dve.tensor_scalar(selsum[:, :, :], rep[:, :, :], 0.0, None, ALU.is_lt)
                        chain(dve.tensor_scalar(sel[:, 0, :, :], rep[:, :, :], 0.0, None, ALU.is_lt))
                    else:
                        for i in range(NT):
                            last = dve.max_index(i8[:, i, :], v8[:, i, :], ex[:, i, :])
                        chain(last)
                        chain(dve.tensor_copy(i8f[:, :, :], i8[:, :, :]))
                        dve.tensor_tensor(rec[:, :], v8[:, :, 0], v8[:, :, 1], ALU.add)
                        for k in range(2):
                            last = dve.tensor_tensor(sel[:, k, :, :], c.eid[:, :].unsqueeze(1).to_broadcast([P, NT, E]),
                                                     bc(i8f[:, :, k]), ALU.is_equal)
                        chain(last)
                        chain(dve.tensor_tensor(selsum[:, :, :], sel[:, 0, :, :], sel[:, 1, :, :], ALU.add))
                    dve.sem_inc(s["sel_rdy"], 1)
                    chain(dve.reciprocal(rec[:, :], rec[:, :]))
                    chain(dve.tensor_tensor(ex[:, :, :], ex[:, :, :], selsum[:, :, :], ALU.mult))
                    dve.tensor_tensor(rowb[:, :, D + 1:W], ex[:, :, :], bc(rec[:, :]), ALU.mult)
                    chain(dve.tensor_copy(rowb[:, :, D:D + 1], tok[:, :].unsqueeze(2)))
                    chain(dve.tensor_scalar(tok[:, :], tok[:, :], float(S), None, ALU.add))
                elif step == 2:
                    dve.wait_ge(s["post_full"], at(N_POST, b, 6))
                    got = work[:, 0:NSEL * (NT + 1) * E].rearrange("p (k t e) -> p k t e", k=NSEL, t=NT + 1)
                    bases = base[:, :, :].unsqueeze(2).to_broadcast([P, NSEL, NT, E])
                    keys = (c.key0[:, :].unsqueeze(1) if layer == 0 else c.key1[:, :, :]).unsqueeze(2).to_broadcast([P, NSEL, NT, E])
                    for k in range(NSEL):
                        last = dve.tensor_tensor(pos[:, k, :, :], got[:, k, 0:NT, :], base[:, k, :].unsqueeze(1).to_broadcast([P, NT, E]), ALU.add)
                    chain(last)
                    chain(dve.tensor_tensor(base[:, :, :], got[:, :, NT, :], base[:, :, :], ALU.add))
                    dve.sem_inc(s["post_evac"], 1)
                else:
                    chain(dve.tensor_scalar(okay[:, :, :, :], pos[:, :, :, :], float(CAP), None, ALU.is_lt))
                    for k in range(NSEL):
                        key = (c.key0[:, :] if layer == 0 else c.key1[:, k, :]).unsqueeze(1).to_broadcast([P, NT, E])
                        last = dve.tensor_tensor(pos[:, k, :, :], key, pos[:, k, :, :], ALU.subtract)
                    chain(last)
                    chain(dve.tensor_tensor(pos[:, :, :, :], pos[:, :, :, :], okay[:, :, :, :], ALU.mult))
                    chain(dve.tensor_tensor(pos[:, :, :, :], pos[:, :, :, :], sel[:, :, :, :], ALU.mult))
                    if layer == 0:
                        for i in range(NT):
                            last = dve.max(k8[:, i, :], pos[:, 0, i, :])
                    else:
                        for k in range(2):
                            last = dve.tensor_reduce(k8[:, :, k], pos[:, k, :, :], AX.X, ALU.max)
                    chain(last)
                    nk = 8 if layer == 0 else 2
                    dve.tensor_scalar(idx[:, :, 0:nk], k8[:, :, 0:nk], -1.0, NOWHERE, ALU.mult, ALU.add).then_inc(s["idx_rdy"], 1)
                    while link[0] < N_CH:
                        dve.sem_inc(s["rchain"], N_CH - link[0])
                        link[0] = N_CH

            def prepare(n, ts):
                for t in ts:
                    if layer and t in (2, 3):
                        prep(n, t)

            for n in ((0, 0), (0, 1)):
                norm1(n)
                norm1_apply(n)
                prepare(n, range(8))
                split(n, 0)
                split(n, 1)
            maxima((0, 0), 0, 64)
            norm1((1, 0))
            norm1_apply((1, 0))
            shift((0, 0))

            def iteration(items):
                prev, cur, nxt, nn, n3 = items
                for hf in range(8):
                    done = {0: (prev, 3), 3: (cur, 0), 5: (cur, 1), 7: (cur, 2)}.get(hf, (None, 0))
                    for j in range(4):
                        if nxt:
                            maxima(nxt, 8 * hf + 2 * j, 8 * hf + 2 * j + 2)
                        if done[0]:
                            norm(*done, j)
                        if prev and hf == 7 and j == 1:
                            route(prev, 1)
                    for kind, t in (x for x in TRIPS[hf] if x):
                        if kind == "prep" and nn:
                            prepare(nn, (t,))
                        if kind == "post" and prev and t < 2:
                            post(prev, t)
                    if prev and hf == 1:
                        norm2(prev)
                    if prev and hf == 4:
                        norm2_apply(prev)
                    if nn and hf in (4, 5):
                        split(nn, hf - 4)
                    if n3 and hf == 4:
                        norm1(n3)
                    if n3 and hf == 6:
                        norm1_apply(n3)
                    if prev and hf == 6:
                        route(prev, 0)
                if prev:
                    route(prev, 2)
                if nxt:
                    shift(nxt)
                if prev:
                    route(prev, 3)

            dve.sem_inc(s["row_free"], 1)
            deep_pipeline(dve, B, 3, iteration)
            if tot0 is not None:
                dve.wait_ge(s["rchain"], N_CH * B)
                dve.tensor_copy(tot0[:, :], base[:, 0, :]).then_inc(s["vchain"], 1)

        @block.gpsimd
        def _(pool):
            def norm1(n):
                pool.wait_ge(s["stat_rdy"], at(NT, n, NT))
                wait_apart(pool, s["xn_rdy"], at(1, n, 0), s["passed"])
                pool.tensor_scalar(rstd[:, :], mv[:, :, 1], EPS, None, ALU.add).then_inc(s["pchain"], 1)
                pool.wait_ge(s["pchain"], at(1, n, 1))
                pool.tensor_tensor(rstd[:, :], rstd[:, :], c.mhalf[:, :], ALU.pow).then_inc(s["rstd_rdy"], 1)

            def residual(b):
                pool.wait_ge(s["res_in"], at(16, b, 16))
                pool.tensor_tensor(xres[:, :, :], xres[:, :, :],
                                   bp_s[:, :].unsqueeze(1).to_broadcast([P, NT, D]), ALU.add).then_inc(s["xres_rdy"], 1)

            def split(n, side):
                pool.wait_ge(s["prep_evac"], at(N_PREP, n, 4 + 4 * side))
                pool.wait_ge(s["hi_rdy"], at(2, n, side + 1))
                src = qk[:, side, :, :]
                pool.tensor_tensor(src, src, parts[:, side, 0, :, :], ALU.subtract).then_inc(s["rest_rdy"], 1)
                pool.wait_ge(s["mid_rdy"], at(2, n, side + 1))
                pool.tensor_tensor(parts[:, side, 2, :, :], src, parts[:, side, 1, :, :], ALU.subtract).then_inc(s["split_rdy"], 1)

            def norm2(b):
                wait_apart(pool, s["stat2_rdy"], at(NT, b, NT), s["passed"])
                pool.tensor_scalar(rstdb[:, :], mvb[:, :, 1], EPS, None, ALU.add).then_inc(s["pchain2"], 1)
                pool.wait_ge(s["pchain2"], at(1, b, 1))
                pool.tensor_tensor(rstdb[:, :], rstdb[:, :], c.mhalf[:, :], ALU.pow).then_inc(s["rstd2_rdy"], 1)

            def scatter(b):
                wait_apart(pool, s["idx_rdy"], at(1, b, 1), s["passed"])
                for i in range(NT):
                    for k in range(NSCAT // NT):
                        pool.indirect_dma_start(rows, bass.IndirectOffsetOnAxis(idx[:, i, k:k + 1], 0), rowb[:, i, :], None,
                                                bounds_check=LAST_ROW, oob_is_err=False).then_inc(s["scat"], 16)
                pool.wait_ge(s["scat"], at(16 * NSCAT, b, 16 * NSCAT))
                pool.sem_inc(s["row_free"], 1)

            for n in ((0, 0), (0, 1)):
                norm1(n)
                split(n, 0)
                split(n, 1)
            norm1((1, 0))
            if layer == 0:
                pool.wait_ge(c.empty0, 16 * (SLOTS // SPARE - 1))

            def iteration(items):
                prev, cur, nxt, nn, n3 = items
                if prev:
                    norm2(prev)
                if nn:
                    split(nn, 0)
                if cur:
                    residual(cur)
                if n3:
                    norm1(n3)
                if nn:
                    split(nn, 1)
                if prev:
                    scatter(prev)

            deep_pipeline(pool, B, 3, iteration)


def experts0(c, rows, gate_up, down, x, rows_next):
    nc = c.nc
    FC = F0 // 2
    TILES = CAP0 // P
    with ExitStack() as ctx:
        t_ = lambda name, shape, dt=F32: sb(c, ctx, f"e0_{name}", shape, dt)
        names = ("rows_in0", "rows_in1", "weights_in0", "weights_in1", "t_full", "act_evac", "dve_evac",
                 "gu_full", "silu_done", "h_done", "y_full", "y_done", "added", "w_done", "passed", "emptied")
        s = {n: ctx.enter_context(nc.semaphore(f"e0_{n}")) for n in names}
        rows_in, weights_in = (s["rows_in0"], s["rows_in1"]), (s["weights_in0"], s["weights_in1"])
        two = lambda name, shape, dt=F32: [t_(f"{name}{i}", shape, dt) for i in range(2)]
        row = two("row", [P, TILES, W0])
        gu_nat = two("gu_nat", [FC, 4, D])
        dn_nat = two("dn_nat", [P, NC, F0])
        xT = two("xT", [P, NC, CAP0])
        guT = two("guT", [P, NC, 4, FC])
        dnT = two("dnT", [FC, 2, D])
        sg = t_("silu", [FC, 2, CAP0])
        h = t_("h", [FC, 2, CAP0])
        y = two("y", [P, TILES, D])
        wcol, token = two("wcol", [P, TILES]), two("token", [P, TILES], U32)
        bank = [ctx.enter_context(nc.psum_tensor(f"e0_bank{i}", [P, 512], F32)) for i in range(7)]
        x_b, gu_b, dn_b, g_b, u_b, y_b = bank[0], bank[1:3], bank[3], bank[4], bank[5], bank[6]
        at = lambda per, b, extra=0: count(per, b[0], b[1], extra)
        block = ctx.enter_context(nc.Block())

        @block.sync
        def _(sp):
            for at_ in range(SPARE, 2 * SLOTS, SPARE):
                sp.dma_start(rows_next[at_:at_ + SPARE, :], rows_next[0:SPARE, :]).then_inc(s["emptied"], 16)

            def load(n):
                par = n[1]
                e = n[0] * 2 + n[1]
                wait_apart(sp, s["t_full"], at(4, n, -4), s["passed"])
                wait_apart(sp, s["y_done"], at(1, n, -1), s["passed"])
                sp.dma_start(gu_nat[par][:, :, :], gate_up[bass.ds(e, 1)].rearrange("o (c f) h -> f (o c) h", f=FC)).then_inc(weights_in[par], 16)
                sp.dma_start(dn_nat[par][:, :, :], down[bass.ds(e, 1)].rearrange("o (c p) f -> p (o c) f", p=P)).then_inc(weights_in[par], 16)
                sp.dma_start(row[par][:, :, :], rows[bass.ds(e * CAP0, CAP0), :].rearrange("(t p) w -> p t w", p=P)).then_inc(rows_in[par], 16)

            def iteration(cur, nxt):
                if nxt:
                    load(nxt)

            pipeline(sp, E0, load, iteration)
            sp.wait_ge(s["emptied"], 16 * (2 * SLOTS // SPARE - 1))

        @block.tensor
        def _(pe):
            def turn(n):
                par = n[1]
                pe.wait_ge(rows_in[par], n[0] * 16 + 16)
                wait(pe, s["dve_evac"], at(2, n, 0))
                for cc in range(NC):
                    for i in range(TILES):
                        last = pe.transpose(x_b[:, cc * CAP0 + i * P:cc * CAP0 + (i + 1) * P],
                                            row[par][:, i, cc * P:(cc + 1) * P], c.ident[:, :])
                last.then_inc(s["t_full"], 1)
                pe.wait_ge(weights_in[par], n[0] * 32 + 32)
                wait(pe, s["act_evac"], at(2, n, 0))
                for cc in range(NC):
                    for q in range(4):
                        last = pe.transpose(gu_b[cc][:, q * FC:(q + 1) * FC], gu_nat[par][:, q, cc * P:(cc + 1) * P], c.ident[0:FC, 0:FC])
                    last.then_inc(s["t_full"], 1)
                for f in range(2):
                    for cc in range(NC):
                        last = pe.transpose(dn_b[0:FC, f * D + cc * P:f * D + (cc + 1) * P],
                                            dn_nat[par][:, cc, f * FC:(f + 1) * FC], c.ident[:, :])
                last.then_inc(s["t_full"], 1)

            def up(b):
                par = b[1]
                pe.wait_ge(s["dve_evac"], at(2, b, 2))
                pe.wait_ge(s["act_evac"], at(2, b, 2))
                wait(pe, s["h_done"], at(1, b, 0))
                for q in range(4):
                    out = (g_b, u_b)[q // 2][0:FC, (q % 2) * CAP0:(q % 2 + 1) * CAP0]
                    for ci in range(NC):
                        last = pe.matmul(out, guT[par][:, ci, q, :], xT[par][:, ci, :], start=ci == 0, stop=ci == NC - 1)
                last.then_inc(s["gu_full"], 1)

            def down_(b):
                par = b[1]
                pe.wait_ge(s["h_done"], at(1, b, 1))
                wait(pe, s["y_done"], at(1, b, 0))
                for i in range(TILES):
                    for f in range(2):
                        last = pe.matmul(y_b[:, i * D:(i + 1) * D], h[:, f, i * P:(i + 1) * P], dnT[par][:, f, :],
                                         start=f == 0, stop=f == 1)
                last.then_inc(s["y_full"], 1)

            def iteration(cur, nxt):
                up(cur)
                if nxt:
                    turn(nxt)
                down_(cur)

            pipeline(pe, E0, turn, iteration)

        @block.scalar
        def _(act):
            def evac(n):
                par = n[1]
                act.wait_ge(s["t_full"], at(4, n, 2))
                act.activation(guT[par][:, 0, :, :].rearrange("p q f -> p (q f)"), gu_b[0][:, 0:4 * FC], ACT.Copy).then_inc(s["act_evac"], 1)
                act.wait_ge(s["t_full"], at(4, n, 4))
                act.activation(dnT[par][:, :, :].rearrange("p f h -> p (f h)"), dn_b[0:FC, :], ACT.Copy).then_inc(s["act_evac"], 1)

            def silu(b):
                act.wait_ge(s["gu_full"], at(1, b, 1))
                act.activation(sg[:, :, :].rearrange("p f s -> p (f s)"), g_b[0:FC, :], ACT.Silu).then_inc(s["silu_done"], 1)

            def iteration(cur, nxt):
                silu(cur)
                if nxt:
                    evac(nxt)

            pipeline(act, E0, evac, iteration)

        @block.vector
        def _(dve):
            def evac(n):
                par = n[1]
                dve.wait_ge(s["t_full"], at(4, n, 1))
                dve.tensor_copy(xT[par][:, :, :].rearrange("p c s -> p (c s)"), x_b[:, :]).then_inc(s["dve_evac"], 1)
                dve.wait_ge(s["t_full"], at(4, n, 3))
                dve.tensor_copy(guT[par][:, 1, :, :].rearrange("p q f -> p (q f)"), gu_b[1][:, 0:4 * FC]).then_inc(s["dve_evac"], 1)

            def hidden(b):
                dve.wait_ge(s["silu_done"], at(1, b, 1))
                dve.tensor_tensor(h[:, :, :].rearrange("p f s -> p (f s)"), u_b[0:FC, :],
                                  sg[:, :, :].rearrange("p f s -> p (f s)"), ALU.mult).then_inc(s["h_done"], 1)

            def result(b):
                par = b[1]
                e = b[0] * 2 + b[1]
                dve.wait_ge(rows_in[par], b[0] * 16 + 16)
                wait(dve, s["added"], at(16 * TILES, b, -16 * TILES))
                dve.tensor_copy(token[par][:, :], row[par][:, :, D])
                dve.tensor_copy(wcol[par][:, :].unsqueeze(2), row[par][:, :, bass.ds(e + (D + 1), 1)]).then_inc(s["w_done"], 1)
                dve.wait_ge(s["w_done"], at(1, b, 1))
                dve.wait_ge(s["y_full"], at(1, b, 1))
                for i in range(TILES):
                    last = dve.tensor_scalar(y[par][:, i, :], y_b[:, i * D:(i + 1) * D], wcol[par][:, i:i + 1],
                                             c.gates[:, 2:3], ALU.mult, ALU.mult)
                last.then_inc(s["y_done"], 1)

            def iteration(cur, nxt):
                hidden(cur)
                if nxt:
                    evac(nxt)
                result(cur)

            pipeline(dve, E0, evac, iteration)

        @block.gpsimd
        def _(pool):
            def add(b):
                par = b[1]
                wait_apart(pool, s["added"], at(16 * TILES, b, 0), s["passed"])
                wait_apart(pool, s["y_done"], at(1, b, 1), s["passed"])
                for i in range(TILES):
                    pool.indirect_dma_start(x, bass.IndirectOffsetOnAxis(token[par][:, i:i + 1], 0), y[par][:, i, :], None,
                                            bounds_check=T + SPARE - 1, oob_is_err=True, compute_op=ALU.add).then_inc(s["added"], 16)

            def nothing(n):
                pass

            pipeline(pool, E0, nothing, lambda cur, nxt: add(cur))
            pool.wait_ge(s["added"], 16 * TILES * E0)


def experts1(c, rows, w1, b1, w2, b2, x, tot0, out):
    nc = c.nc
    TILES, HC = CAP1 // P, F1 // P
    HALF = CAP1 // 2
    with ExitStack() as ctx:
        t_ = lambda name, shape, dt=F32: sb(c, ctx, f"e1_{name}", shape, dt)
        two = lambda name, shape, dt=F32: [t_(f"{name}{i}", shape, dt) for i in range(2)]
        names = ("rows_in0", "rows_in1", "weights_in0", "weights_in1", "bias_in", "x_full", "x_evac",
                 "h_full", "act_h", "dve_h", "y_full", "y_evac", "y_done", "added", "picked", "small", "ichain",
                 "copied", "passed")
        s = {n: ctx.enter_context(nc.semaphore(f"e1_{n}")) for n in names}
        rows_in, weights_in = (s["rows_in0"], s["rows_in1"]), (s["weights_in0"], s["weights_in1"])
        row = two("row", [P, TILES, W1])
        w1_s, w2_s = two("w1", [P, NC, F1]), two("w2", [P, HC, D])
        xT = two("xT", [P, NC, CAP1])
        h = two("h", [P, HC, HALF])
        y = two("y", [P, TILES, D])
        b1_s, b2_s = t_("b1", [P, E1, HC]), t_("b2", [P, E1, D])
        b1_e = two("b1_e", [P, HC])
        gidx = t_("gidx", [P, E1, TILES], U32)
        gfl, late = t_("gfl", [P, E1, TILES]), t_("late", [P, E1, TILES])
        gidx_e = two("gidx_e", [P, TILES], U32)
        wcol, token = two("wcol", [P, TILES]), two("token", [P, TILES], U32)
        hb = [ctx.enter_context(nc.psum_tensor(f"e1_h_bank{i}", [P, 512], F32)) for i in range(4)]
        yb = [ctx.enter_context(nc.psum_tensor(f"e1_y_bank{i}", [P, 512], F32)) for i in range(2)]
        xb = ctx.enter_context(nc.psum_tensor("e1_x_bank", [P, 512], F32))
        at = lambda per, b, extra=0: count(per, b[0], b[1], extra)
        block = ctx.enter_context(nc.Block())

        @block.sync
        def _(sp):
            sp.dma_start(b1_s[:, :, :], b1.rearrange("e (c p) -> p e c", p=P), allow_slow_non_contiguous=True).then_inc(s["bias_in"], 16)
            sp.dma_start(b2_s[:, :, :], b2.partition_broadcast(P)).then_inc(s["bias_in"], 16)

            def load(n):
                par = n[1]
                e = n[0] * 2 + n[1]
                wait_apart(sp, s["y_full"], at(4, n, -4), s["passed"])
                sp.dma_start(w1_s[par][:, :, :], w1[bass.ds(e, 1)].rearrange("o (c p) f -> p (o c) f", p=P)).then_inc(weights_in[par], 16)
                sp.dma_start(w2_s[par][:, :, :], w2[bass.ds(e, 1)].rearrange("o (c p) d -> p (o c) d", p=P)).then_inc(weights_in[par], 16)

            def iteration(cur, nxt):
                if nxt:
                    load(nxt)

            pipeline(sp, E1, load, iteration)
            sp.wait_ge(s["added"], 16 * TILES * E1)
            sp.dma_start(out, x[0:T, :]).then_inc(s["copied"], 16)
            sp.wait_ge(s["copied"], 16)

        @block.tensor
        def _(pe):
            def turn(n, k):
                par, cc, hf = n[1], k // 2, k % 2
                if k == 0:
                    pe.wait_ge(rows_in[par], n[0] * (16 * TILES) + 16 * TILES)
                wait(pe, s["x_evac"], at(4, n, k))
                for i in range(4):
                    last = pe.transpose(xb[:, i * P:(i + 1) * P], row[par][:, 4 * hf + i, cc * P:(cc + 1) * P], c.ident[:, :])
                last.then_inc(s["x_full"], 1)

            def up(b, blk, k0, k1):
                par = b[1]
                if k0 == 0 and blk == 0:
                    pe.wait_ge(weights_in[par], b[0] * 32 + 32)
                    pe.wait_ge(s["x_evac"], at(4, b, 4))
                for k in range(k0, k1):
                    q = 8 * blk + k
                    wait(pe, s[("act_h", "dve_h")[q % 2]], at(8, b, q // 2 - 1))
                    for ci in range(NC):
                        last = pe.matmul(hb[q % 4][:, :], w1_s[par][:, ci, k * P:(k + 1) * P],
                                         xT[par][:, ci, blk * HALF:(blk + 1) * HALF], start=ci == 0, stop=ci == NC - 1)
                    last.then_inc(s["h_full"], 1)

            def down(b, blk):
                par = b[1]
                pe.wait_ge(s["act_h"], at(8, b, 4 * blk + 4))
                pe.wait_ge(s["dve_h"], at(8, b, 4 * blk + 4))
                for t in range(2):
                    trip = 2 * blk + t
                    wait(pe, s["y_evac"], at(4, b, trip - 1))
                    for i in range(2):
                        for k in range(HC):
                            last = pe.matmul(yb[t][:, i * D:(i + 1) * D], h[blk][:, k, (2 * t + i) * P:(2 * t + i + 1) * P],
                                             w2_s[par][:, k, :], start=k == 0, stop=k == HC - 1)
                    last.then_inc(s["y_full"], 1)

            def prologue(n):
                for k in range(4):
                    turn(n, k)
                up(n, 0, 0, HC)

            def iteration(cur, nxt):
                for k in range(4):
                    up(cur, 1, 2 * k, 2 * k + 2)
                    if nxt:
                        turn(nxt, k)
                down(cur, 0)
                if nxt:
                    up(nxt, 0, 0, HC)
                down(cur, 1)

            pipeline(pe, E1, prologue, iteration)

        @block.scalar
        def _(act):
            def evac(n, k):
                par, cc, hf = n[1], k // 2, k % 2
                act.wait_ge(s["x_full"], at(4, n, k + 1))
                act.activation(xT[par][:, cc, hf * HALF:(hf + 1) * HALF], xb[:, :], ACT.Copy).then_inc(s["x_evac"], 1)

            def hidden(b, blk, ks):
                par = b[1]
                if blk == 0:
                    act.wait_ge(s["small"], at(1, b, 1))
                for k in ks:
                    q = 8 * blk + k
                    act.wait_ge(s["h_full"], at(16, b, q + 1))
                    act.activation(h[blk][:, k, :], hb[q % 4][:, :], ACT.Relu, bias=b1_e[par][:, k:k + 1]).then_inc(s["act_h"], 1)

            def prologue(n):
                for k in range(4):
                    evac(n, k)
                hidden(n, 0, (0, 2, 4, 6))

            def iteration(cur, nxt):
                for k in range(4):
                    hidden(cur, 1, (2 * k,))
                    if nxt:
                        evac(nxt, k)
                if nxt:
                    hidden(nxt, 0, (0, 2, 4, 6))

            pipeline(act, E1, prologue, iteration)

        @block.vector
        def _(dve):
            full = tot0[:, :].unsqueeze(2).to_broadcast([P, E1, TILES])
            dve.tensor_tensor(late[:, :, :], c.slot_in[:, :, :], full, ALU.is_ge).then_inc(s["ichain"], 1)
            dve.tensor_scalar(gfl[:, :, :], full, -1.0, float(SLOTS), ALU.mult, ALU.add).then_inc(s["ichain"], 1)
            dve.wait_ge(s["ichain"], 2)
            dve.tensor_tensor(gfl[:, :, :], gfl[:, :, :], late[:, :, :], ALU.mult).then_inc(s["ichain"], 1)
            dve.wait_ge(s["ichain"], 3)
            dve.tensor_tensor(gidx[:, :, :], gfl[:, :, :], c.slot_at[:, :, :], ALU.add).then_inc(s["ichain"], 1)
            dve.wait_ge(s["ichain"], 4)
            dve.wait_ge(s["bias_in"], 32)

            def pick(n):
                par = n[1]
                e = n[0] * 2 + n[1]
                wait(dve, s["rows_in" + str(par)], n[0] * (16 * TILES))
                wait(dve, s["act_h"], at(8, n, -8))
                dve.tensor_copy(gidx_e[par][:, :].unsqueeze(1), gidx[:, bass.ds(e, 1), :]).then_inc(s["picked"], 1)
                dve.tensor_copy(b1_e[par][:, :].unsqueeze(1), b1_s[:, bass.ds(e, 1), :]).then_inc(s["small"], 1)

            def gates(n):
                par = n[1]
                e = n[0] * 2 + n[1]
                dve.wait_ge(rows_in[par], n[0] * (16 * TILES) + 16 * TILES)
                wait(dve, s["added"], at(16 * TILES, n, -16 * TILES))
                dve.tensor_copy(token[par][:, :], row[par][:, :, D])
                dve.tensor_scalar(wcol[par][:, :].unsqueeze(2), row[par][:, :, bass.ds(e + (D + 1), 1)],
                                  c.gates[:, 3:4], None, ALU.mult).then_inc(s["picked"], 1)

            def hidden(b, blk, ks):
                par = b[1]
                if blk == 0:
                    dve.wait_ge(s["small"], at(1, b, 1))
                for k in ks:
                    q = 8 * blk + k
                    dve.wait_ge(s["h_full"], at(16, b, q + 1))
                    dve.tensor_scalar(h[blk][:, k, :], hb[q % 4][:, :], b1_e[par][:, k:k + 1], 0.0, ALU.add, ALU.max).then_inc(s["dve_h"], 1)

            def result(b, blk):
                par = b[1]
                e = b[0] * 2 + b[1]
                if blk == 0:
                    dve.wait_ge(s["picked"], at(2, b, 2))
                for t in range(2):
                    trip = 2 * blk + t
                    dve.wait_ge(s["y_full"], at(4, b, trip + 1))
                    ys = y[par][:, 2 * trip:2 * trip + 2, :]
                    dve.tensor_tensor(ys, yb[t][:, :].rearrange("p (t d) -> p t d", t=2),
                                      b2_s[:, bass.ds(e, 1), :].to_broadcast([P, 2, D]), ALU.add).then_inc(s["y_evac"], 1)
                    dve.wait_ge(s["y_evac"], at(4, b, trip + 1))
                    for i in (2 * trip, 2 * trip + 1):
                        dve.tensor_scalar(y[par][:, i, :], y[par][:, i, :], wcol[par][:, i:i + 1], None, ALU.mult).then_inc(s["y_done"], 1)

            def prologue(n):
                pick(n)
                gates(n)
                hidden(n, 0, (1, 3, 5, 7))

            def iteration(cur, nxt):
                if nxt:
                    pick(nxt)
                hidden(cur, 1, (1, 3, 5, 7))
                result(cur, 0)
                if nxt:
                    gates(nxt)
                    hidden(nxt, 0, (1, 3, 5, 7))
                result(cur, 1)

            pipeline(dve, E1, prologue, iteration)

        @block.gpsimd
        def _(pool):
            def gather(n):
                par = n[1]
                wait_apart(pool, s["picked"], at(2, n, 1), s["passed"])
                wait_apart(pool, s["x_full"], at(4, n, -4), s["passed"])
                wait_apart(pool, s["y_done"], at(TILES, n, -TILES), s["passed"])
                for i in range(TILES):
                    pool.indirect_dma_start(row[par][:, i, :], None, rows, bass.IndirectOffsetOnAxis(gidx_e[par][:, i:i + 1], 0),
                                            bounds_check=2 * SLOTS - 1, oob_is_err=True).then_inc(rows_in[par], 16)

            def add(b):
                par = b[1]
                wait_apart(pool, s["added"], at(16 * TILES, b, 0), s["passed"])
                for i in range(TILES):
                    wait_apart(pool, s["y_done"], at(TILES, b, i + 1), s["passed"])
                    pool.indirect_dma_start(x, bass.IndirectOffsetOnAxis(token[par][:, i:i + 1], 0), y[par][:, i, :], None,
                                            bounds_check=T + SPARE - 1, oob_is_err=True, compute_op=ALU.add).then_inc(s["added"], 16)

            def iteration(cur, nxt):
                if nxt:
                    gather(nxt)
                add(cur)

            pipeline(pool, E1, gather, iteration)
            pool.wait_ge(s["added"], 16 * TILES * E1)


def program(nc, a, out, stage=4):
    with ExitStack() as ctx:
        c = Chip(nc, ctx)
        dram = lambda n, shape, dt=F32: nc.dram_tensor(n, shape, dt, kind="Internal").ap()
        x1 = dram("x_after_l0", (T + SPARE, D))
        x3 = dram("x_after_l1", (T + SPARE, D))
        rows0 = dram("rows0", (SLOTS, W0))
        rows1 = dram("rows1", (2 * SLOTS, W1))
        qk_dram = [dram(f"qk_parts{i}", (2, 3, D, S), BF16) for i in range(2)]
        mask_dram = dram("mask_parts", (3, B, S), BF16)
        flat = lambda ap: ap.rearrange("b s d -> (b s) d")
        constants(c, a["g_xattn"], a["g_ffn"], rows0, rows1, x1, x3)
        pre = "L0_xattn_"
        attention(c, 0, flat(a["x"]), flat(a["ctx_1024"]), a["mask_BxS2_ff0"],
                  *(a[pre + n] for n in ("Wq", "bq", "Wk", "bk", "Wv", "bv", "Wp", "bp")),
                  a["L0_ffn_gate_weight"], x1, rows0, qk_dram, mask_dram)
        if stage > 1:
            experts0(c, rows0, a["L0_ffn_gate_up_proj"], a["L0_ffn_down_proj"], x1, rows1)
        if stage > 2:
            pre = "L1_xattn_"
            tot0 = sb(c, ctx, "tot0", [P, E1])
            attention(c, 1, x1, flat(a["ctx_1024"]), a["mask_Bx1xS_if1"].rearrange("b o s -> (b o s)"),
                      *(a[pre + n] for n in ("Wq", "bq", "Wk", "bk", "Wv", "bv", "Wo", "bo")),
                      a["L1_ffn_wg"], x3, rows1, qk_dram, mask_dram, tot0)
        if stage > 3:
            pre = "L1_ffn_"
            experts1(c, rows1, *(a[pre + n] for n in ("w1", "b1", "w2", "b2")), x3, tot0, flat(out))
        if stage < 4:
            with nc.semaphore("dbg") as dbg, nc.Block() as block:
                @block.sync
                def _(sp):
                    sp.dma_start(flat(out), (x3 if stage == 3 else x1)[0:T, :]).then_inc(dbg, 16)
                    sp.wait_ge(dbg, 16)


STAGE = 4


def kernel(**inputs):
    import numpy as np
    import concourse.bacc as bacc
    from concourse.bass_utils import run_bass_kernel_spmd

    nc = bacc.Bacc("TRN2", target_bir_lowering=False, num_devices=1)
    arrays, args = {}, {}
    for name, value in inputs.items():
        a = np.ascontiguousarray(value)
        arrays[f"in_{name}"] = a
        args[name] = nc.dram_tensor(f"in_{name}", a.shape, mybir.dt.from_np(a.dtype), kind="ExternalInput").ap()
    out = nc.dram_tensor("out_x", (B, S, D), F32, kind="ExternalOutput").ap()
    program(nc, args, out, STAGE)
    r = run_bass_kernel_spmd(nc, [arrays], core_ids=[0])
    return r.results[0]["out_x"]
```

```python
from contextlib import ExitStack

import concourse.bass as bass
from concourse import mybir
from concourse.alu_op_type import AluOpType as ALU

F32 = mybir.dt.float32
BF16 = mybir.dt.bfloat16
U32 = mybir.dt.uint32
I32 = mybir.dt.int32
ACT = mybir.ActivationFunctionType
AX = mybir.AxisListType

P = 128
B, S, D = 8, 512, 256
T = B * S
HEADS, DH = 16, 16
NT = S // P
NC = D // P
GROUPS = HEADS // 4
PAIRS = GROUPS // 2
EPS = 1e-5
SCALE = DH ** -0.5
HIDDEN = -float(2 ** 100)

Q_TERM = (0, 0, 1, 1, 0, 2)
K_TERM = (0, 1, 0, 1, 2, 0)
STACK = DH * len(Q_TERM)
ROW_MASK = STACK
ROW_SHIFT = STACK + 3
ROWS = STACK + 6

E0, CAP0, F0, K0 = 32, 256, 192, 8
E1, CAP1, F1, K1 = 8, 1024, 1024, 2
W0 = D + 1 + E0
W1 = D + 1 + E1
SLOTS = E0 * CAP0
SPARE = CAP1
NOWHERE0 = 16384.0
NOWHERE1 = 32768.0

N_PREP = 10
N_POST = 6


class Chip:

    def __init__(self, nc, ctx):
        self.nc, self.ctx = nc, ctx


def sb(c, ctx, name, shape, dt=F32):
    return ctx.enter_context(c.nc.sbuf_tensor(name, shape, dt))


class Semaphores:

    def __init__(self, nc):
        self.nc, self.taken = nc, []

    def __enter__(self):
        return self

    def __call__(self, name):
        self.taken.append(self.nc.alloc_semaphore(name=name))
        return self.taken[-1]

    def __exit__(self, *_):
        self.nc.clear_and_free_semaphores(self.taken)
        self.nc.all_engine_barrier()


def count(per, half, par, extra=0):
    return half * (2 * per) + (per * par + extra)


def wait(eng, sem, value):
    if isinstance(value, int) and value <= 0:
        return
    eng.wait_ge(sem, value)


def wait_apart(eng, sem, value, passed):
    wait(eng, sem, value)
    if not isinstance(value, int):
        eng.sem_inc(passed, 1)


def pipeline(eng, n_items, prologue, iteration):
    prologue((0, 0))
    iteration((0, 0), (0, 1))
    with eng.Fori(1, n_items // 2) as it:
        iteration((it - 1, 1), (it, 0))
        iteration((it, 0), (it, 1))
    iteration((n_items // 2 - 1, 1), None)


def deep_pipeline(eng, n_items, depth, iteration):
    def items(half, par):
        return [(half + (par + k) // 2, (par + k) % 2) for k in range(-1, depth + 1)]

    def single(i):
        iteration([x if 0 <= 2 * x[0] + x[1] < n_items else None for x in items(i // 2, i % 2)])

    single(0)
    looped = (n_items - depth - 1) // 2
    with eng.Fori(0, looped) as it:
        iteration(items(it, 1))
        iteration(items(it + 1, 0))
    for i in range(2 * looped + 1, n_items + 1):
        single(i)


def constants(c, g_xattn, g_ffn, rows0, rows1, x1, x3):
    nc, ctx = c.nc, c.ctx
    c.ident = sb(c, ctx, "ident", [P, P])
    c.identb = sb(c, ctx, "identb", [P, P], BF16)
    c.before = sb(c, ctx, "before", [P, P], BF16)
    c.onesb = sb(c, ctx, "onesb", [P, P], BF16)
    c.hide_st = sb(c, ctx, "hide_st", [P, P], BF16)
    c.hide_max = sb(c, ctx, "hide_max", [P, P], BF16)
    c.gates = sb(c, ctx, "gates", [P, 4])
    c.mhalf = sb(c, ctx, "mhalf", [P, NT])
    c.tok0 = sb(c, ctx, "tok0", [P, NT])
    c.key0 = sb(c, ctx, "key0", [P, E0])
    c.key1 = sb(c, ctx, "key1", [P, 2, E1])
    c.eid = sb(c, ctx, "eid", [P, E1])
    c.slot_in = sb(c, ctx, "slot_in", [P, E1, CAP1 // P])
    c.slot_at = sb(c, ctx, "slot_at", [P, E1, CAP1 // P])
    c.empty0 = ctx.enter_context(nc.semaphore("empty0"))
    c.spares = (rows1[0:SPARE, :], x1[T:T + SPARE, :], x3[T:T + SPARE, :])
    with ExitStack() as tmp:
        ii = sb(c, tmp, "ii", [P, 256], I32)
        empty = sb(c, tmp, "empty", [P, SPARE // P, W0])
        sem = lambda n: tmp.enter_context(nc.semaphore(n))
        gate_in, tables, empty_set, empty_out, iota_s, made = (
            sem(n) for n in ("gate_in", "tables", "empty_set", "empty_out", "iota_s", "made"))
        block = tmp.enter_context(nc.Block())

        @block.sync
        def _(sp):
            sp.dma_start(c.gates[:, 0:2], g_xattn.partition_broadcast(P)).then_inc(gate_in, 16)
            sp.dma_start(c.gates[:, 2:4], g_ffn.partition_broadcast(P)).then_inc(gate_in, 16)
            sp.wait_ge(empty_set, 2)
            sp.dma_start(rows0[0:SPARE, :].rearrange("(t p) w -> p t w", p=P), empty[:, :, :]).then_inc(empty_out, 16)
            sp.wait_ge(empty_out, 16)

        @block.scalar
        def _(act):
            act.wait_ge(gate_in, 32)
            act.activation(c.gates[:, :], c.gates[:, :], ACT.Tanh).then_inc(made, 1)

        @block.vector
        def _(dve):
            dve.memset(empty[:, :, :], 0.0).then_inc(made, 1)
            dve.wait_ge(made, 2)
            dve.wait_ge(iota_s, 1)
            dve.tensor_copy(empty[:, :, D:D + 1], ii[:, 200:200 + SPARE // P].unsqueeze(2)).then_inc(empty_set, 1)
            dve.memset(c.onesb[:, :], 1.0)
            dve.memset(c.mhalf[:, :], -0.5).then_inc(empty_set, 1)
            dve.wait_ge(iota_s, 2)
            dve.tensor_copy(c.tok0[:, :], ii[:, 1:1 + NT])
            dve.tensor_copy(c.key0[:, :], ii[:, 8:8 + E0])
            dve.tensor_copy(c.key1[:, :, :], ii[:, 40:56].rearrange("p (k e) -> p k e", k=2))
            dve.tensor_copy(c.eid[:, :], ii[:, 56:64])
            n = E1 * (CAP1 // P)
            dve.tensor_copy(c.slot_in[:, :, :], ii[:, 64:64 + n].rearrange("p (e s) -> p e s", e=E1))
            dve.tensor_copy(c.slot_at[:, :, :], ii[:, 128:128 + n].rearrange("p (e s) -> p e s", e=E1)).then_inc(made, 1)

        @block.gpsimd
        def _(pool):
            pool.iota(ii[:, 200:200 + SPARE // P], pattern=[[P, SPARE // P]], base=T, channel_multiplier=1).then_inc(iota_s, 1)
            pool.iota(ii[:, 1:1 + NT], pattern=[[P, NT]], base=0, channel_multiplier=1)
            pool.iota(ii[:, 8:8 + E0], pattern=[[-CAP0, E0]], base=int(NOWHERE0), channel_multiplier=0)
            pool.iota(ii[:, 40:56].rearrange("p (k e) -> p k e", k=2), pattern=[[-SLOTS, 2], [-CAP1, E1]],
                      base=int(NOWHERE1), channel_multiplier=0)
            pool.iota(ii[:, 56:64], pattern=[[1, E1]], base=0, channel_multiplier=0)
            n = CAP1 // P
            pool.iota(ii[:, 64:64 + E1 * n].rearrange("p (e s) -> p e s", e=E1),
                      pattern=[[0, E1], [P, n]], base=0, channel_multiplier=1)
            pool.iota(ii[:, 128:128 + E1 * n].rearrange("p (e s) -> p e s", e=E1),
                      pattern=[[CAP1, E1], [P, n]], base=0, channel_multiplier=1).then_inc(iota_s, 1)
            pool.memset(c.ident[:, :], 0.0)
            pool.memset(c.identb[:, :], 0.0)
            pool.memset(c.before[:, :], 1.0)
            pool.memset(c.hide_st[:, :], 0.0)
            pool.memset(c.hide_max[:, :], 0.0).then_inc(tables, 1)
            pool.wait_ge(tables, 1)
            for m in (c.ident, c.identb):
                pool.affine_select(out=m[:, :], in_=m[:, :], compare_op=ALU.not_equal, fill=1.0,
                                   base=0, pattern=[[-1, P]], channel_multiplier=1)
            pool.affine_select(out=c.before[:, :], in_=c.before[:, :], compare_op=ALU.is_gt, fill=0.0,
                               base=0, pattern=[[1, P]], channel_multiplier=-1)
            pool.affine_select(out=c.hide_st[:, :], in_=c.hide_st[:, :], compare_op=ALU.is_ge, fill=HIDDEN,
                               base=0, pattern=[[1, P]], channel_multiplier=-1)
            pool.affine_select(out=c.hide_max[:, :], in_=c.hide_max[:, :], compare_op=ALU.is_ge, fill=HIDDEN,
                               base=0, pattern=[[-1, P]], channel_multiplier=1).then_inc(tables, 1)
            pool.wait_ge(tables, 2)


def attention(c, layer, x_in, ctx_in, mask, wq, bq, wk, bk, wv, bv, wp, bp, wroute, x_out, rows,
              qk_dram, mask_dram, tot0=None):
    nc = c.nc
    causal = layer == 0
    E = E0 if layer == 0 else E1
    CAP = CAP0 if layer == 0 else CAP1
    W = W0 if layer == 0 else W1
    NSEL = 1 if layer == 0 else 2
    NSCAT = NT * (K0 if layer == 0 else K1)
    NOWHERE = NOWHERE0 if layer == 0 else NOWHERE1
    LAST_ROW = SLOTS - 1 if layer == 0 else 2 * SLOTS - 1

    with ExitStack() as ctx:
        t_ = lambda name, shape, dt=F32: sb(c, ctx, f"{name}_{layer}", shape, dt)
        phase_sems = ctx.enter_context(Semaphores(nc))
        sem = lambda n: phase_sems(f"{n}_{layer}")
        wq_s, wk_s, wv_s = (t_(n, [P, NC, D]) for n in ("wq", "wk", "wv"))
        wp_s = t_("wp", [P, PAIRS, D])
        bq_s, bk_s = t_("bq", [P, NC]), t_("bk", [P, NC])
        bp_s = t_("bp", [P, D])
        wr_s = t_("wr", [P, NC, E])
        xin = t_("xin", [P, NT, D])
        xres = t_("xres", [P, NT, D])
        crow = t_("crow", [P, NT, D])
        xn = t_("xn", [P, NT, D])
        xT = t_("xT", [P, NC, S])
        cT = t_("cT", [P, NC, S])
        yT = t_("yT", [P, NC, S])
        qk = t_("qk", [P, 2, NC, S])
        parts = t_("parts", [P, 2, 3, NC, S], BF16)
        qst = [t_(f"qst{i}", [ROWS, HEADS, S], BF16) for i in range(2)]
        kst = [t_(f"kst{i}", [ROWS, HEADS, S], BF16) for i in range(2)]
        va = [t_(f"va{i}", [P, NT, HEADS, 32]) for i in range(2)]
        pt = t_("pt", [P, 8, 2 * S])
        vals = t_("vals", [P, S])
        sums = t_("sums", [P, PAIRS, S])
        odd_sums = t_("odd_sums", [P, S])
        on = t_("on", [P, PAIRS, S])
        den = t_("den", [P, S])
        nmx = t_("nmx", [P, NT, HEADS])
        m3 = t_("m3", [P, NT, 3, HEADS], BF16)
        m3T = t_("m3T", [3 * HEADS, S], BF16)
        st6, mv = t_("st6", [P, NT, 6]), t_("mv", [P, NT, 2])
        st6b, mvb = t_("st6b", [P, NT, 6]), t_("mvb", [P, NT, 2])
        rstd, rstdb = t_("rstd", [P, NT]), t_("rstdb", [P, NT])
        rowb = t_("rowb", [P, NT, W])
        lgs, ex, rep = t_("lgs", [P, NT, E]), t_("ex", [P, NT, E]), t_("rep", [P, NT, E])
        lmx, rec, tok = t_("lmx", [P, NT]), t_("rec", [P, NT]), t_("tok", [P, NT])
        v8, k8 = t_("v8", [P, NT, 8]), t_("k8", [P, NT, 8])
        i8 = t_("i8", [P, NT, 8], U32)
        i8f = t_("i8f", [P, NT, 8])
        sel = t_("sel", [P, NSEL, NT, E], BF16)
        selsum = t_("selsum", [P, NT, E])
        pos, okay = t_("pos", [P, NSEL, NT, E]), t_("okay", [P, NSEL, NT, E])
        base = t_("base", [P, NSEL, E])
        bvc = t_("bvc", [P, PAIRS])
        idx = t_("idx", [P, NT, 8], U32)
        maskq = t_("maskq", [P, S]) if layer else None
        maski = t_("maski", [P, S], I32) if layer else None

        work = ctx.enter_context(nc.psum_tensor(f"work_{layer}", [P, 512], F32))
        mxb = [ctx.enter_context(nc.psum_tensor(f"mxb{i}_{layer}", [P, 512], F32)) for i in range(2)]
        stb = [ctx.enter_context(nc.psum_tensor(f"stb{i}_{layer}", [P, 1024], F32)) for i in range(2)]
        ob = ctx.enter_context(nc.psum_tensor(f"ob_{layer}", [P, 512], F32))

        with ExitStack() as tmp:
            w_in, stack_ones, w_t, w_put, w_ones, bv_rdy, bv_out, bv_sum = (
                tmp.enter_context(nc.semaphore(f"{n}_{layer}")) for n in
                ("w_in", "stack_ones", "w_t", "w_put", "w_ones", "bv_rdy", "bv_out", "bv_sum"))
            w_chain = tmp.enter_context(nc.semaphore(f"w_chain_{layer}"))
            m_out = tmp.enter_context(nc.semaphore(f"m_out_{layer}"))
            if layer == 0:
                route_nat = pt[0:E0, 0, 0:D]
                mrow = pt[0:B, 1, 0:S]
                mparts = parts[0:B, 0, 0:3, 0, :]
            else:
                nat = [pt[:, i, 0:NC * D].rearrange("p (c n) -> p c n", c=NC) for i in range(3)]
                wo_nat = pt[:, 4, 0:NC * D].rearrange("p (c q j r d) -> p c q j r d", c=NC, q=PAIRS, j=4, r=2)
            block = tmp.enter_context(nc.Block())

            @block.sync
            def _(sp):
                n = 0
                for w, s in ((wq, wq_s), (wk, wk_s), (wv, wv_s)):
                    dst = s[:, :, :] if layer == 0 else nat[n // 16]
                    sp.dma_start(dst, w.rearrange("(c p) n -> p c n", p=P)).then_inc(w_in, 16)
                    n += 16
                for b_, s in ((bq, bq_s), (bk, bk_s)):
                    sp.dma_start(s[:, :], b_.rearrange("(c p) -> p c", p=P), allow_slow_non_contiguous=True).then_inc(w_in, 16)
                sp.dma_start(bp_s[:, :], bp.partition_broadcast(P)).then_inc(w_in, 16)
                sp.wait_ge(stack_ones, 1)
                bv_src = bv.rearrange("(q r j d) -> r j d q", q=PAIRS, r=2, j=4)
                for j in range(4):
                    for odd in range(2):
                        at_ = 32 * j + DH * odd
                        sp.dma_start(bvc[at_:at_ + DH, :], bv_src[odd, j], allow_slow_non_contiguous=True).then_inc(w_in, 16)
                for st in (*qst, *kst):
                    sp.dma_start(st[STACK:ROWS, :, :], m3T[0:ROWS - STACK, :].unsqueeze(1).to_broadcast([ROWS - STACK, HEADS, S])).then_inc(w_ones, 16)
                if layer == 0:
                    sp.dma_start(route_nat, wroute).then_inc(w_in, 16)
                    sp.dma_start(mrow, mask).then_inc(w_in, 16)
                    src = wp.rearrange("(q r j d) n -> r j d q n", q=PAIRS, r=2, j=4)
                    for j in range(4):
                        for odd in range(2):
                            at_ = 32 * j + DH * odd
                            sp.dma_start(wp_s[at_:at_ + DH, :, :], src[odd, j]).then_inc(w_in, 16)
                    sp.wait_ge(w_chain, 7)
                    sp.dma_start(mask_dram.rearrange("r b s -> b r s"), mparts).then_inc(m_out, 16)
                    sp.wait_ge(m_out, 16)
                else:
                    sp.dma_start(wr_s[:, :, :], wroute.rearrange("(c p) e -> p c e", p=P)).then_inc(w_in, 16)
                    src = wp.rearrange("(c p) (q r j d) -> p c q r j d", p=P, q=PAIRS, r=2, j=4)
                    for cc in range(NC):
                        for q in range(PAIRS):
                            for odd in range(2):
                                sp.dma_start(wo_nat[:, cc, q, :, odd, :], src[:, cc, q, odd]).then_inc(w_in, 16)

                sp.wait_ge(w_ones, 64)

            n_in = 16 * (6 + 8 + 2 + 8) if layer == 0 else 16 * (6 + 8 + 1 + NC * GROUPS)

            @block.tensor
            def _(pe):
                pe.wait_ge(w_in, n_in)
                if layer == 0:
                    for cc in range(NC):
                        last = pe.transpose(work[:, cc * E0:(cc + 1) * E0], route_nat[:, cc * P:(cc + 1) * P], c.ident[0:E0, 0:E0])
                    last.then_inc(w_t, 1)
                else:
                    for m, bank in ((0, work), (1, mxb[0]), (2, mxb[1])):
                        for co in range(NC):
                            for ci in range(NC):
                                last = pe.transpose(bank[:, ci * D + co * P:ci * D + (co + 1) * P],
                                                    nat[m][:, co, ci * P:(ci + 1) * P], c.ident[:, :])
                        last.then_inc(w_t, 1)
                    for q in range(PAIRS):
                        for co in range(NC):
                            last = pe.transpose(stb[0][:, q * D + co * P:q * D + (co + 1) * P],
                                                wo_nat[:, co, q, :, :, :].rearrange("p j r d -> p (j r d)"), c.ident[:, :])
                    last.then_inc(w_t, 1)
                pe.wait_ge(bv_rdy, 1)
                for q in range(PAIRS):
                    last = pe.matmul(stb[1][:, 0:D], den[:, q * P:(q + 1) * P], wp_s[:, q, :], start=q == 0, stop=q == PAIRS - 1)
                last.then_inc(bv_out, 1)

            @block.vector
            def _(dve):
                dve.memset(m3T[0:ROWS - STACK, :], 1.0).then_inc(stack_ones, 1)
                dve.memset(den[:, :], 1.0).then_inc(w_chain, 1)
                for i in range(2):
                    dve.memset(va[i][:, :, :, :], 1.0)
                dve.memset(base[:, :, :], 0.0)
                dve.tensor_copy(tok[:, :], c.tok0[:, :])
                dve.wait_ge(w_in, n_in)
                dve.tensor_scalar(bp_s[:, :], bp_s[:, :], c.gates[:, layer:layer + 1], None, ALU.mult).then_inc(bv_sum, 1)
                if layer == 0:
                    dve.tensor_scalar(mrow, mrow, 1.0 / SCALE, None, ALU.mult).then_inc(w_chain, 1)
                    for r in range(3):
                        dve.wait_ge(w_chain, 2 + 2 * r)
                        dve.tensor_copy(mparts[:, r, :], mrow).then_inc(w_chain, 1)
                        if r < 2:
                            dve.wait_ge(w_chain, 3 + 2 * r)
                            dve.tensor_tensor(mrow, mrow, mparts[:, r, :], ALU.subtract).then_inc(w_chain, 1)
                    dve.tensor_scalar(wp_s[:, :, :], wp_s[:, :, :], c.gates[:, 0:1], None, ALU.mult)
                    dve.wait_ge(w_t, 1)
                    dve.tensor_copy(wr_s[:, :, :], work[:, 0:NC * E0].rearrange("p (c e) -> p c e", c=NC)).then_inc(w_put, 1)
                else:
                    for n, (s, bank) in enumerate(((wq_s, work), (wk_s, mxb[0]), (wv_s, mxb[1]))):
                        dve.wait_ge(w_t, n + 1)
                        dve.tensor_copy(s[:, :, :], bank[:, :].rearrange("p (c n) -> p c n", c=NC))
                    dve.wait_ge(w_t, 4)
                    dve.tensor_scalar(wp_s[:, :, :], stb[0][:, 0:PAIRS * D].rearrange("p (q n) -> p q n", q=PAIRS),
                                      c.gates[:, 1:2], None, ALU.mult).then_inc(w_put, 1)
                dve.wait_ge(w_chain, 1)
                for q in range(PAIRS):
                    last = dve.tensor_scalar(den[:, q * P:(q + 1) * P], den[:, q * P:(q + 1) * P], bvc[:, q:q + 1], None, ALU.mult)
                dve.wait_ge(w_put, 1)
                last.then_inc(bv_rdy, 1)
                dve.wait_ge(bv_out, 1)
                dve.wait_ge(bv_sum, 1)
                dve.tensor_tensor(bp_s[:, :], bp_s[:, :], stb[1][:, 0:D], ALU.add).then_inc(bv_sum, 1)

        names = ("ld0", "ld1", "res_in", "parts_out", "shift_in", "x_out", "scat",
                 "prep_full", "prep_evac", "post_full", "post_evac", "shift_full", "shift_evac",
                 "max_full", "max_free", "st_full", "st_free", "pt_free", "norm_done",
                 "stat_rdy", "rstd_rdy", "xn_rdy", "xres_rdy", "hi_rdy", "rest_rdy", "mid_rdy", "split_rdy", "m3_rdy",
                 "mchain", "nchain", "nchain2", "stat2_rdy", "rstd2_rdy", "row_rdy", "lg_rdy", "ex_rdy", "sel_rdy",
                 "idx_rdy", "vchain", "rchain", "pchain", "pchain2", "passed", "x_rdy", "mq_rdy", "row_free", "raw_rdy", "ochain", "pair_rdy")
        s = {n: sem(n) for n in names}
        ld = (s["ld0"], s["ld1"])
        stack_in = [[sem(f"stack_in{i}_{g}") for g in range(GROUPS)] for i in range(2)]
        N_LD = 48 if layer else 32
        N_STACK = 16 * (13 if causal else 12)

        def span(pair):
            if not causal:
                return 0, 2 * S, ((2 * pair, 0, 0), (2 * pair + 1, S, 0))
            if pair == 0:
                return 0, 2 * S - P, ((0, 0, 0), (1, S, P))
            return 2 * P, 2 * P * 2 + P, ((2, 2 * P, 2 * P), (3, S, 3 * P))

        block = ctx.enter_context(nc.Block())

        def at(per, b, extra=0):
            return count(per, b[0], b[1], extra)

        def half_of(b, per, extra=0):
            return b[0] * per + extra

        def rows_of(b):
            return bass.ds(b[0] * (2 * S) + b[1] * S, S) if not isinstance(b[0], int) else slice((2 * b[0] + b[1]) * S, (2 * b[0] + b[1] + 1) * S)

        FIRST_TRIPS = ((4, 5), (6, 7), (8, 9), ())
        DONE_AT = {0: (0, 3), 3: (1, 0), 5: (1, 1), 7: (1, 2)}
        TRIPS = ((("prep", 0), ("prep", 1)), (("prep", 2), ("prep", 3)), (("prep", 4), ("post", 0)),
                 (("post", 1), ("prep", 5)), (("prep", 6), ("prep", 7)), (("post", 2), ("post", 3)),
                 (("post", 4), None), (None, ("post", 5)))
        LAST_TRIPS = ((None, None), (None, None), (("post", 0), ("post", 1)), (None, None),
                      (("post", 2), ("post", 3)), (("post", 4), None), (None, ("post", 5)), (None, None))

        @block.sync
        def _(sp):
            def load(n):
                par = n[1]
                wait_apart(sp, s["xn_rdy"], at(1, n, 0), s["passed"])
                wait_apart(sp, s["prep_full"], at(N_PREP, n, -N_PREP + 6), s["passed"])
                if layer:
                    wait_apart(sp, s["mq_rdy"], at(1, n, 0), s["passed"])
                sp.dma_start(xin[:, :, :], x_in[rows_of(n), :].rearrange("(t p) d -> p t d", p=P)).then_inc(ld[par], 16)
                sp.dma_start(crow[:, :, :], ctx_in[rows_of(n), :].rearrange("(t p) d -> p t d", p=P)).then_inc(ld[par], 16)
                if layer:
                    sp.dma_start(maski[:, :], mask[rows_of(n)].partition_broadcast(P)).then_inc(ld[par], 16)

            def load_residual(b):
                wait_apart(sp, s["x_out"], at(16, b, 0), s["passed"])
                wait_apart(sp, s["row_rdy"], at(1, b, 0), s["passed"])
                sp.dma_start(xres[:, :, :], x_in[rows_of(b), :].rearrange("(t p) d -> p t d", p=P)).then_inc(s["res_in"], 16)

            def parts_store(n):
                wait_apart(sp, s["split_rdy"], at(2, n, 2), s["passed"])
                for g in range(GROUPS):
                    wait_apart(sp, stack_in[n[1]][g], half_of(n, N_STACK), s["passed"])
                sp.dma_start(qk_dram[n[1]].rearrange("i r (c p) s -> p (i r c) s", p=P),
                             parts[:, :, :, :, :].rearrange("p i r c s -> p (i r c) s")).then_inc(s["parts_out"], 16)
                wait_apart(sp, s["parts_out"], at(16, n, 16), s["passed"])

            def stack(n, g):
                par = n[1]
                wait_apart(sp, s["st_free"], at(32, n, -64 + 8 * g + 8), s["passed"])
                for side, dst, terms in ((0, qst, Q_TERM), (1, kst, K_TERM)):
                    for r, term in enumerate(terms):
                        sp.dma_start(dst[par][DH * r:DH * r + DH, 4 * g:4 * g + 4, :],
                                     qk_dram[par][side, term].rearrange("(h d) s -> d h s", d=DH)[:, 4 * g:4 * g + 4, :]).then_inc(stack_in[par][g], 16)
                if causal:
                    m = mask_dram[:, bass.ds(n[0] * 2 + n[1], 1), :] if not isinstance(n[0], int) else mask_dram[:, 2 * n[0] + n[1]:2 * n[0] + n[1] + 1, :]
                    sp.dma_start(kst[par][ROW_MASK:ROW_MASK + 3, 4 * g:4 * g + 4, :], m.to_broadcast([3, 4, S])).then_inc(stack_in[par][g], 16)

            def store(b):
                wait_apart(sp, s["x_rdy"], at(1, b, 1), s["passed"])
                sp.dma_start(x_out[rows_of(b), :].rearrange("(t p) d -> p t d", p=P), xres[:, :, :]).then_inc(s["x_out"], 16)

            load((0, 0))
            load((0, 1))
            for n in ((0, 0), (0, 1)):
                parts_store(n)
                if n[1]:
                    load((1, 0))
                for g in range(GROUPS):
                    stack(n, g)
            def iteration(items):
                prev, cur, nxt, nn, n3 = items
                if n3:
                    load(n3)
                if prev:
                    store(prev)
                if cur:
                    load_residual(cur)
                if nn:
                    parts_store(nn)
                    for g in range(GROUPS):
                        stack(nn, g)
                if layer == 0 and not prev:
                    for at_ in range(SPARE, SLOTS, SPARE):
                        sp.dma_start(rows[at_:at_ + SPARE, :], rows[0:SPARE, :]).then_inc(c.empty0, 16)
                    for x in c.spares:
                        sp.dma_start(x, rows[0:SPARE, 0:x.shape[1]]).then_inc(c.empty0, 16)

            deep_pipeline(sp, B, 3, iteration)
            sp.wait_ge(s["x_out"], 16 * B)
            if layer == 0:
                sp.wait_ge(c.empty0, 16 * (SLOTS // SPARE - 1 + len(c.spares)))

        @block.tensor
        def _(pe):
            last_trip = [None]

            def bank_free(kind, b, t):
                before, last_trip[0] = last_trip[0], (kind, b, t)
                if before:
                    kind, b, t = before
                    pe.wait_ge(s[kind + "_evac"], at({"prep": N_PREP, "post": N_POST, "shift": 1}[kind], b, t + 1))

            def prep(n, t):
                par = n[1]
                bank_free("prep", n, t)
                if t == 0:
                    pe.wait_ge(s["xn_rdy"], at(1, n, 1))
                elif t == 4:
                    pe.wait_ge(ld[par], half_of(n, N_LD, N_LD))
                if t in (0, 1, 4, 5):
                    src, cc = (xn, crow)[t // 4], t % 2
                    for i in range(NT):
                        last = pe.transpose(work[:, i * P:(i + 1) * P], src[:, i, cc * P:(cc + 1) * P], c.ident[:, :])
                elif t < 8:
                    w, act_, co = ((wq_s, xT), (wk_s, cT))[t // 4] + (t % 2,)
                    for ci in range(NC):
                        last = pe.matmul(work[:, :], w[:, ci, co * P:(co + 1) * P], act_[:, ci, :],
                                         start=ci == 0, stop=ci == NC - 1)
                else:
                    for i in range(2):
                        tt = 2 * (t - 8) + i
                        for ci in range(NC):
                            last = pe.matmul(work[:, i * D:(i + 1) * D], cT[:, ci, tt * P:(tt + 1) * P], wv_s[:, ci, :],
                                             start=ci == 0, stop=ci == NC - 1)
                last.then_inc(s["prep_full"], 1)

            def maxima(n, u0, u1):
                par = n[1]
                rows_used = STACK + 3 if causal else STACK
                for u in range(u0, u1):
                    h, qt = u // NT, u % NT
                    if u % 16 == 0:
                        pe.wait_ge(stack_in[par][u // 16], half_of(n, N_STACK, N_STACK))
                    wait(pe, s["max_free"], at(64, n, u - 1))
                    nk = (qt + 1) * P if causal else S
                    last = pe.matmul(mxb[u % 2][:, 0:nk], qst[par][0:rows_used, h, qt * P:(qt + 1) * P],
                                     kst[par][0:rows_used, h, 0:nk], start=True, stop=not causal)
                    if causal:
                        last = pe.matmul(mxb[u % 2][:, nk - P:nk], c.identb[:, :], c.hide_max[:, :], start=False, stop=True)
                    last.then_inc(s["max_full"], 1)

            def shift(n):
                bank_free("shift", n, 0)
                pe.wait_ge(s["m3_rdy"], at(1, n, 1))
                for qt in range(NT):
                    last = pe.matmul(work[0:3 * HEADS, qt * P:(qt + 1) * P],
                                     m3[:, qt, :, :].rearrange("p r h -> p (r h)"), c.identb[:, :], start=True, stop=True)
                last.then_inc(s["shift_full"], 1)

            def scores(b, hf, j):
                par, g, pair = b[1], hf // 2, hf % 2
                u, h = 4 * hf + j, 4 * g + j
                if u == 0:
                    pe.wait_ge(s["shift_in"], at(48, b, 48))
                wait(pe, s["st_free"], at(32, b, u - 1))
                for kt, col, q0 in span(pair)[2]:
                    bank = stb[u % 2]
                    last = pe.matmul(bank[:, col:col + S - q0], kst[par][0:ROWS, h, kt * P:(kt + 1) * P],
                                     qst[par][0:ROWS, h, q0:S], start=True, stop=not causal)
                    if causal:
                        last = pe.matmul(bank[:, col:col + P], c.identb[:, :], c.hide_st[:, :], start=False, stop=True)
                last.then_inc(s["st_full"], 1)

            def values(b, hf, part):
                par, g, pair = b[1], hf // 2, hf % 2
                if part == 0:
                    pe.wait_ge(s["st_free"], at(32, b, 4 * hf + 4))
                    if pair == 0:
                        wait(pe, s["raw_rdy"], at(4, b, g))
                kt, col, q0 = span(pair)[2][part]
                for j in range(4):
                    u, h = 4 * hf + j, 4 * g + j
                    last = pe.matmul(ob[32 * j:32 * j + 32, q0:S], va[par][:, kt, h, :],
                                     pt[:, u % 8, col:col + S - q0], start=kt == 0, stop=kt == NT - 1,
                                     tile_position=(0, 32 * j))
                if part == 1:
                    last.then_inc(s["pt_free"], 1)

            def post(b, t):
                bank_free("post", b, t)
                if t == 0:
                    pe.wait_ge(s["norm_done"], at(PAIRS, b, PAIRS))
                elif t == 2:
                    pe.wait_ge(s["row_rdy"], at(1, b, 1))
                elif t == 5:
                    pe.wait_ge(s["sel_rdy"], at(1, b, 1))
                if t < 2:
                    for i in range(2):
                        tt = 2 * t + i
                        for q in range(PAIRS):
                            last = pe.matmul(work[:, i * D:(i + 1) * D], on[:, q, tt * P:(tt + 1) * P], wp_s[:, q, :],
                                             start=q == 0, stop=q == PAIRS - 1)
                elif t < 4:
                    for i in range(NT):
                        last = pe.transpose(work[:, i * P:(i + 1) * P], rowb[:, i, (t - 2) * P:(t - 1) * P], c.ident[:, :])
                elif t == 4:
                    for i in range(NT):
                        for ci in range(NC):
                            last = pe.matmul(work[:, i * E:(i + 1) * E], yT[:, ci, i * P:(i + 1) * P], wr_s[:, ci, :],
                                             start=ci == 0, stop=ci == NC - 1)
                else:
                    for k in range(NSEL):
                        for i in range(NT + 1):
                            o = (k * (NT + 1) + i) * E
                            if i < NT:
                                last = pe.matmul(work[:, o:o + E], c.before[:, :], sel[:, k, i, :], start=True, stop=i == 0)
                            for ii in range(i):
                                last = pe.matmul(work[:, o:o + E], c.onesb[:, :], sel[:, k, ii, :],
                                                 start=i == NT and ii == 0, stop=ii == i - 1)
                last.then_inc(s["post_full"], 1)

            for t in range(N_PREP):
                prep((0, 0), t)
            for t in range(4):
                prep((0, 1), t)
            for g in range(GROUPS):
                maxima((0, 0), 16 * g, 16 * g + 16)
                for t in FIRST_TRIPS[g]:
                    prep((0, 1), t)
            shift((0, 0))

            def iteration(items):
                prev, cur, nxt, nn, _ = items
                trips = TRIPS if nxt or not cur else LAST_TRIPS
                if prev and nxt:
                    last_trip[0] = ("prep", nxt, N_PREP - 1)

                def trip(what):
                    kind, t = what or (None, None)
                    if kind == "prep" and nn:
                        prep(nn, t)
                    if kind == "post" and prev:
                        post(prev, t)

                def unit(hf, k):
                    if nxt:
                        maxima(nxt, 8 * hf + 2 * k, 8 * hf + 2 * k + 2)

                for hf in range(8):
                    if hf == 0:
                        unit(0, 0)
                        trip(trips[0][0])
                    for j in range(4):
                        if cur:
                            scores(cur, hf, j)
                        if j == 1 and hf > 0:
                            unit(hf, 0)
                            trip(trips[hf][0])
                        elif j > 1:
                            unit(hf, j - 1)
                    if cur and hf:
                        values(cur, hf - 1, 0)
                    unit(hf, 3)
                    if cur and hf:
                        values(cur, hf - 1, 1)
                    trip(trips[hf][1])
                if cur:
                    values(cur, 7, 0)
                    values(cur, 7, 1)
                if nn:
                    prep(nn, 8)
                if nxt:
                    shift(nxt)
                if nn:
                    prep(nn, 9)

            deep_pipeline(pe, B, 3, iteration)

        @block.scalar
        def _(act):
            def prep(n, t):
                par = n[1]
                if layer and t in (2, 3):
                    if t == 3:
                        act.wait_ge(s["prep_evac"], at(N_PREP, n, 4))
                        wait(act, s["parts_out"], at(16, n, 0))
                        act.activation(parts[:, 0, 0, :, :], qk[:, 0, :, :], ACT.Copy).then_inc(s["hi_rdy"], 1)
                    return
                act.wait_ge(s["prep_full"], at(N_PREP, n, t + 1))
                if t in (0, 1, 4, 5):
                    dst = (xT, cT)[t // 4][:, t % 2, :]
                    act.activation(dst, work[:, :], ACT.Copy).then_inc(s["prep_evac"], 1)
                elif t < 8:
                    side, cc = t // 4, t % 2
                    bias = (bq_s, bk_s)[side][:, cc:cc + 1]
                    if cc == 0:
                        wait(act, s["split_rdy"], at(2, n, side - 1))
                        wait(act, s["parts_out"], at(16, n, 0))
                    hi = act.activation(parts[:, side, 0, cc, :], work[:, :], ACT.Identity, bias=bias)
                    if cc == 1:
                        hi.then_inc(s["hi_rdy"], 1)
                    act.activation(qk[:, side, cc, :], work[:, :], ACT.Identity, bias=bias).then_inc(s["prep_evac"], 1)
                else:
                    i = 2 * (t - 8)
                    if t == 8:
                        wait(act, s["pt_free"], at(8, n, -8))
                    for odd in range(2):
                        for k in range(2):
                            last = act.activation(
                                va[par][:, i + k, :, DH * odd:DH * odd + DH].rearrange("p (q r j) d -> p q r j d", q=PAIRS, r=2)[:, :, odd],
                                work[:, k * D:(k + 1) * D].rearrange("p (q r j d) -> p q r j d", q=PAIRS, r=2, j=4)[:, :, odd], ACT.Copy)
                    last.then_inc(s["prep_evac"], 1)

            def exps(b, hf, js):
                pair = hf % 2
                if js[0] == 0:
                    wait(act, s["pt_free"], at(8, b, hf - 1))
                lo, hi, _ = span(pair)
                for j in js:
                    u = 4 * hf + j
                    act.wait_ge(s["st_full"], at(32, b, u + 1))
                    act.activation(pt[:, u % 8, lo:hi], stb[u % 2][:, lo:hi], ACT.Exp, scale=SCALE).then_inc(s["st_free"], 1)

            def outputs(b, g):
                q = g // 2
                act.wait_ge(s["pt_free"], at(8, b, 2 * g + 2))
                if g % 2 == 0:
                    wait(act, s["norm_done"], at(PAIRS, b, q - 1))
                    act.activation(sums[:, q, :], ob[:, :], ACT.Copy).then_inc(s["raw_rdy"], 1)
                    return
                wait(act, s["norm_done"], at(PAIRS, b, q))
                act.activation(vals[:, :], ob[:, :], ACT.Copy).then_inc(s["ochain"], 1)
                act.activation(odd_sums[:, :], ob[:, :], ACT.Copy).then_inc(s["raw_rdy"], 1)

            def join(b, g, step):
                q = g // 2
                if step == 0:
                    act.wait_ge(s["ochain"], at(2 * PAIRS, b, 2 * q + 1))
                    for j in range(4):
                        last = act.activation(vals[32 * j:32 * j + DH, :], sums[32 * j:32 * j + DH, q, :], ACT.Copy)
                    last.then_inc(s["ochain"], 1)
                else:
                    act.wait_ge(s["ochain"], at(2 * PAIRS, b, 2 * q + 2))
                    act.wait_ge(s["raw_rdy"], at(GROUPS, b, g + 1))
                    for j in range(4):
                        last = act.activation(sums[32 * j:32 * j + DH, q, :], odd_sums[32 * j:32 * j + DH, :], ACT.Copy)
                    last.then_inc(s["pair_rdy"], 1)

            def shift(n):
                act.wait_ge(s["shift_evac"], at(1, n, 1))
                for r in range(3):
                    act.dma_start(qst[n[1]][ROW_SHIFT + r:ROW_SHIFT + r + 1, :, :],
                                  m3T[HEADS * r:HEADS * (r + 1), :]).then_inc(s["shift_in"], 16)

            def post(b, t):
                if t in (2, 3):
                    act.wait_ge(s["post_full"], at(N_POST, b, t + 1))
                    act.activation(yT[:, t - 2, :], work[:, :], ACT.Copy).then_inc(s["post_evac"], 1)

            def route(b):
                act.wait_ge(s["lg_rdy"], at(1, b, 1))
                act.activation(ex[:, :, :], lgs[:, :, :], ACT.Exp).then_inc(s["ex_rdy"], 1)

            for n in ((0, 0), (0, 1)):
                for t in range(N_PREP):
                    prep(n, t)
            shift((0, 0))

            def iteration(items):
                prev, cur, nxt, nn, _ = items
                trips = TRIPS if nxt or not cur else LAST_TRIPS

                def together(hf, step):
                    item, g = DONE_AT.get(hf, (0, 0))
                    if g % 2 and items[item]:
                        join(items[item], g, step)

                def evac(trip):
                    kind, t = trip or (None, None)
                    if kind == "prep" and nn:
                        prep(nn, t)
                    if kind == "post" and prev:
                        post(prev, t)

                for hf in range(8):
                    if hf == 0:
                        evac(trips[0][0])
                    if cur:
                        exps(cur, hf, (0, 1))
                    if prev and ("post", 5) in trips[hf]:
                        route(prev)
                    together(hf - 1, 1)
                    if hf in DONE_AT and items[DONE_AT[hf][0]]:
                        outputs(items[DONE_AT[hf][0]], DONE_AT[hf][1])
                    if hf > 0:
                        evac(trips[hf][0])
                    if cur:
                        exps(cur, hf, (2, 3))
                    evac(trips[hf][1])
                    together(hf, 0)
                if nn:
                    prep(nn, 8)
                if nxt:
                    shift(nxt)
                if nn:
                    prep(nn, 9)

            deep_pipeline(act, B, 3, iteration)

        @block.vector
        def _(dve):
            def norm1(n):
                par = n[1]
                dve.wait_ge(ld[par], half_of(n, N_LD, N_LD))
                for i in range(NT):
                    dve.bn_stats(st6[:, i, :], xin[:, i, :]).then_inc(s["nchain"], 1)
                wait_apart(dve, s["nchain"], at(NT, n, NT), s["passed"])
                for i in range(NT):
                    dve.bn_aggr(mv[:, i, :], st6[:, i, :]).then_inc(s["stat_rdy"], 1)
                if layer:
                    wait(dve, s["prep_evac"], at(N_PREP, n, -N_PREP + 4))
                    dve.tensor_scalar(maskq[:, :], maski[:, :], 0.0, None, ALU.not_equal).then_inc(s["mq_rdy"], 1)

            def norm1_apply(n):
                dve.wait_ge(s["rstd_rdy"], at(1, n, 1))
                wait(dve, s["prep_full"], at(N_PREP, n, -N_PREP + 2))
                for i in range(NT):
                    last = dve.tensor_scalar(xn[:, i, :], xin[:, i, :], mv[:, i, 0:1], rstd[:, i:i + 1],
                                             ALU.subtract, ALU.mult)
                last.then_inc(s["xn_rdy"], 1)

            def prep(n, t):
                dve.wait_ge(s["prep_full"], at(N_PREP, n, t + 1))
                if t == 2:
                    wait(dve, s["split_rdy"], at(2, n, -1))
                    dve.wait_ge(s["mq_rdy"], at(1, n, 1))
                dve.scalar_tensor_tensor(out=qk[:, 0, t - 2, :], in0=work[:, :], scalar=bq_s[:, t - 2:t - 1],
                                         in1=maskq[:, :], op0=ALU.add, op1=ALU.mult).then_inc(s["prep_evac"], 1)

            def split(n, side):
                dve.wait_ge(s["rest_rdy"], at(2, n, side + 1))
                wait(dve, s["parts_out"], at(16, n, 0))
                dve.tensor_copy(parts[:, side, 1, :, :], qk[:, side, :, :]).then_inc(s["mid_rdy"], 1)

            def maxima(n, u0, u1):
                for u in range(u0, u1):
                    h, qt = u // NT, u % NT
                    nk = (qt + 1) * P if causal else S
                    dve.wait_ge(s["max_full"], at(64, n, u + 1))
                    dve.tensor_reduce(nmx[:, qt, h:h + 1], mxb[u % 2][:, 0:nk], AX.X, ALU.max, negate=True).then_inc(s["max_free"], 1)

            def shift(n):
                dve.wait_ge(s["max_free"], at(64, n, 64))
                wait(dve, s["shift_full"], at(1, n, 0))
                for r in range(3):
                    dve.tensor_copy(m3[:, :, r, :], nmx[:, :, :]).then_inc(s["mchain"], 1)
                    dve.wait_ge(s["mchain"], at(5, n, 2 * r + 1))
                    if r < 2:
                        dve.tensor_tensor(nmx[:, :, :], nmx[:, :, :], m3[:, :, r, :], ALU.subtract).then_inc(s["mchain"], 1)
                        dve.wait_ge(s["mchain"], at(5, n, 2 * r + 2))
                dve.sem_inc(s["m3_rdy"], 1)
                dve.wait_ge(s["shift_full"], at(1, n, 1))
                wait(dve, s["shift_in"], at(48, n, 0))
                dve.tensor_copy(m3T[:, :], work[0:3 * HEADS, :]).then_inc(s["shift_evac"], 1)

            def norm(b, q):
                wait(dve, s["norm_done"], at(PAIRS, b, q))
                wait_apart(dve, s["pair_rdy"], at(PAIRS, b, q + 1), s["passed"])
                dve.stream_shuffle(den[:, :], sums[:, q, :], [(DH + i) % 32 for i in range(32)]).then_inc(s["vchain"], 1)
                dve.wait_ge(s["vchain"], at(2 * PAIRS, b, 2 * q + 1))
                dve.reciprocal(den[:, :], den[:, :]).then_inc(s["vchain"], 1)
                dve.wait_ge(s["vchain"], at(2 * PAIRS, b, 2 * q + 2))
                if q == 0:
                    wait(dve, s["post_full"], at(N_POST, b, -N_POST + 2))
                dve.tensor_tensor(on[:, q, :], vals[:, :], den[:, :], ALU.mult).then_inc(s["norm_done"], 1)

            def post(b, t):
                dve.wait_ge(s["post_full"], at(N_POST, b, t + 1))
                if t == 0:
                    dve.wait_ge(s["xres_rdy"], at(1, b, 1))
                dve.tensor_tensor(xres[:, 2 * t:2 * t + 2, :], work[:, :].rearrange("p (t d) -> p t d", t=2),
                                  xres[:, 2 * t:2 * t + 2, :], ALU.add).then_inc(s["post_evac"], 1)

            def norm2(b):
                dve.wait_ge(s["post_evac"], at(N_POST, b, 2))
                dve.sem_inc(s["x_rdy"], 1)
                for i in range(NT):
                    dve.bn_stats(st6b[:, i, :], xres[:, i, :]).then_inc(s["nchain2"], 1)
                wait_apart(dve, s["nchain2"], at(NT, b, NT), s["passed"])
                for i in range(NT):
                    dve.bn_aggr(mvb[:, i, :], st6b[:, i, :]).then_inc(s["stat2_rdy"], 1)

            def norm2_apply(b):
                dve.wait_ge(s["rstd2_rdy"], at(1, b, 1))
                dve.wait_ge(s["row_free"], at(1, b, 1))
                for i in range(NT):
                    last = dve.tensor_scalar(rowb[:, i, 0:D], xres[:, i, :], mvb[:, i, 0:1], rstdb[:, i:i + 1],
                                             ALU.subtract, ALU.mult)
                last.then_inc(s["row_rdy"], 1)

            N_CH = 40

            link = [0]

            def route(b, step):
                if step == 0:
                    link[0] = 0

                def chain(ins):
                    link[0] += 1
                    ins.then_inc(s["rchain"], 1)
                    wait_apart(dve, s["rchain"], at(N_CH, b, link[0]), s["passed"])

                bc = lambda ap: ap.unsqueeze(2).to_broadcast([P, NT, E])
                lg = work[:, 0:NT * E].rearrange("p (t e) -> p t e", t=NT)
                if step == 0:
                    dve.wait_ge(s["post_full"], at(N_POST, b, 5))
                    chain(dve.tensor_reduce(lmx[:, :], lg, AX.X, ALU.max))
                    dve.tensor_tensor(lgs[:, :, :], lg, bc(lmx[:, :]), ALU.subtract).then_inc(s["lg_rdy"], 1)
                    dve.wait_ge(s["lg_rdy"], at(1, b, 1))
                    dve.sem_inc(s["post_evac"], 1)
                elif step == 1:
                    wait_apart(dve, s["ex_rdy"], at(1, b, 1), s["passed"])
                    for i in range(NT):
                        last = dve.max(v8[:, i, :], ex[:, i, :])
                    chain(last)
                    if layer == 0:
                        for i in range(NT):
                            last = dve.match_replace(rep[:, i, :], v8[:, i, :], ex[:, i, :], -1.0)
                        dve.tensor_reduce(rec[:, :], v8[:, :, :], AX.X, ALU.add)
                        chain(last)
                        dve.tensor_scalar(selsum[:, :, :], rep[:, :, :], 0.0, None, ALU.is_lt)
                        chain(dve.tensor_scalar(sel[:, 0, :, :], rep[:, :, :], 0.0, None, ALU.is_lt))
                    else:
                        for i in range(NT):
                            last = dve.max_index(i8[:, i, :], v8[:, i, :], ex[:, i, :])
                        chain(last)
                        chain(dve.tensor_copy(i8f[:, :, :], i8[:, :, :]))
                        dve.tensor_tensor(rec[:, :], v8[:, :, 0], v8[:, :, 1], ALU.add)
                        for k in range(2):
                            last = dve.tensor_tensor(sel[:, k, :, :], c.eid[:, :].unsqueeze(1).to_broadcast([P, NT, E]),
                                                     bc(i8f[:, :, k]), ALU.is_equal)
                        chain(last)
                        chain(dve.tensor_tensor(selsum[:, :, :], sel[:, 0, :, :], sel[:, 1, :, :], ALU.add))
                    dve.sem_inc(s["sel_rdy"], 1)
                    chain(dve.reciprocal(rec[:, :], rec[:, :]))
                    chain(dve.tensor_tensor(ex[:, :, :], ex[:, :, :], selsum[:, :, :], ALU.mult))
                    dve.tensor_tensor(rowb[:, :, D + 1:W], ex[:, :, :], bc(rec[:, :]), ALU.mult)
                    chain(dve.tensor_copy(rowb[:, :, D:D + 1], tok[:, :].unsqueeze(2)))
                    chain(dve.tensor_scalar(tok[:, :], tok[:, :], float(S), None, ALU.add))
                elif step == 2:
                    dve.wait_ge(s["post_full"], at(N_POST, b, 6))
                    got = work[:, 0:NSEL * (NT + 1) * E].rearrange("p (k t e) -> p k t e", k=NSEL, t=NT + 1)
                    bases = base[:, :, :].unsqueeze(2).to_broadcast([P, NSEL, NT, E])
                    keys = (c.key0[:, :].unsqueeze(1) if layer == 0 else c.key1[:, :, :]).unsqueeze(2).to_broadcast([P, NSEL, NT, E])
                    for k in range(NSEL):
                        last = dve.tensor_tensor(pos[:, k, :, :], got[:, k, 0:NT, :], base[:, k, :].unsqueeze(1).to_broadcast([P, NT, E]), ALU.add)
                    chain(last)
                    chain(dve.tensor_tensor(base[:, :, :], got[:, :, NT, :], base[:, :, :], ALU.add))
                    dve.sem_inc(s["post_evac"], 1)
                else:
                    chain(dve.tensor_scalar(okay[:, :, :, :], pos[:, :, :, :], float(CAP), None, ALU.is_lt))
                    for k in range(NSEL):
                        key = (c.key0[:, :] if layer == 0 else c.key1[:, k, :]).unsqueeze(1).to_broadcast([P, NT, E])
                        last = dve.tensor_tensor(pos[:, k, :, :], key, pos[:, k, :, :], ALU.subtract)
                    chain(last)
                    chain(dve.tensor_tensor(pos[:, :, :, :], pos[:, :, :, :], okay[:, :, :, :], ALU.mult))
                    chain(dve.tensor_tensor(pos[:, :, :, :], pos[:, :, :, :], sel[:, :, :, :], ALU.mult))
                    if layer == 0:
                        for i in range(NT):
                            last = dve.max(k8[:, i, :], pos[:, 0, i, :])
                    else:
                        for k in range(2):
                            last = dve.tensor_reduce(k8[:, :, k], pos[:, k, :, :], AX.X, ALU.max)
                    chain(last)
                    nk = 8 if layer == 0 else 2
                    dve.tensor_scalar(idx[:, :, 0:nk], k8[:, :, 0:nk], -1.0, NOWHERE, ALU.mult, ALU.add).then_inc(s["idx_rdy"], 1)
                    while link[0] < N_CH:
                        dve.sem_inc(s["rchain"], N_CH - link[0])
                        link[0] = N_CH

            def prepare(n, ts):
                for t in ts:
                    if layer and t in (2, 3):
                        prep(n, t)

            norm1((0, 0))
            norm1_apply((0, 0))
            prepare((0, 0), range(8))
            if not layer:
                norm1((0, 1))
            split((0, 0), 0)
            if layer:
                norm1((0, 1))
            norm1_apply((0, 1))
            split((0, 0), 1)
            prepare((0, 1), range(8))
            for g in range(GROUPS):
                maxima((0, 0), 16 * g, 16 * g + 16)
                if g in (0, 2):
                    split((0, 1), g // 2)
            shift((0, 0))
            norm1((1, 0))
            norm1_apply((1, 0))

            def iteration(items):
                prev, cur, nxt, nn, n3 = items

                trips = TRIPS if nxt or not cur else LAST_TRIPS

                def evac(trip):
                    kind, t = trip or (None, None)
                    if kind == "prep" and nn:
                        prepare(nn, (t,))
                    if kind == "post" and prev and t < 2:
                        post(prev, t)

                def normalise(hf):
                    item, g = DONE_AT.get(hf, (0, 0))
                    if g % 2 and items[item]:
                        norm(items[item], g // 2)

                for hf in range(8):
                    if nxt:
                        maxima(nxt, 8 * hf, 8 * hf + 2)
                    evac(trips[hf][0])
                    if nxt:
                        maxima(nxt, 8 * hf + 2, 8 * hf + 4)
                    if prev and ("post", 5) in trips[hf]:
                        route(prev, 1)
                    if nxt:
                        maxima(nxt, 8 * hf + 4, 8 * hf + 8)
                    evac(trips[hf][1])
                    if prev and ("post", 4) in trips[hf]:
                        route(prev, 0)
                    if hf == 1:
                        normalise(0)
                    if prev and hf == (3 if trips is TRIPS else 2):
                        norm2(prev)
                    if prev and hf == (4 if trips is TRIPS else 3):
                        norm2_apply(prev)
                    if nn and hf in (4, 5):
                        split(nn, hf - 4)
                    if n3 and hf == 5:
                        norm1(n3)
                    if n3 and hf == 6:
                        norm1_apply(n3)
                    if prev and ("post", 5) in trips[hf]:
                        route(prev, 2)
                    if prev and ("post", 5) in trips[hf] and hf < 7:
                        route(prev, 3)
                if nxt:
                    shift(nxt)
                normalise(5)
                if prev and ("post", 5) in trips[7]:
                    route(prev, 3)

            dve.sem_inc(s["row_free"], 1)
            deep_pipeline(dve, B, 3, iteration)
            if tot0 is not None:
                dve.wait_ge(s["rchain"], N_CH * B)
                dve.tensor_copy(tot0[:, :], base[:, 0, :]).then_inc(s["vchain"], 1)

        @block.gpsimd
        def _(pool):
            def norm1(n):
                pool.wait_ge(s["stat_rdy"], at(NT, n, NT))
                wait_apart(pool, s["xn_rdy"], at(1, n, 0), s["passed"])
                pool.tensor_scalar(rstd[:, :], mv[:, :, 1], EPS, None, ALU.add).then_inc(s["pchain"], 1)
                pool.wait_ge(s["pchain"], at(1, n, 1))
                pool.tensor_tensor(rstd[:, :], rstd[:, :], c.mhalf[:, :], ALU.pow).then_inc(s["rstd_rdy"], 1)

            def residual(b):
                pool.wait_ge(s["res_in"], at(16, b, 16))
                pool.tensor_tensor(xres[:, :, :], xres[:, :, :],
                                   bp_s[:, :].unsqueeze(1).to_broadcast([P, NT, D]), ALU.add).then_inc(s["xres_rdy"], 1)

            def split(n, side):
                pool.wait_ge(s["prep_evac"], at(N_PREP, n, 4 + 4 * side))
                pool.wait_ge(s["hi_rdy"], at(2, n, side + 1))
                src = qk[:, side, :, :]
                pool.tensor_tensor(src, src, parts[:, side, 0, :, :], ALU.subtract).then_inc(s["rest_rdy"], 1)
                pool.wait_ge(s["mid_rdy"], at(2, n, side + 1))
                pool.tensor_tensor(parts[:, side, 2, :, :], src, parts[:, side, 1, :, :], ALU.subtract).then_inc(s["split_rdy"], 1)

            def norm2(b):
                wait_apart(pool, s["stat2_rdy"], at(NT, b, NT), s["passed"])
                pool.tensor_scalar(rstdb[:, :], mvb[:, :, 1], EPS, None, ALU.add).then_inc(s["pchain2"], 1)
                pool.wait_ge(s["pchain2"], at(1, b, 1))
                pool.tensor_tensor(rstdb[:, :], rstdb[:, :], c.mhalf[:, :], ALU.pow).then_inc(s["rstd2_rdy"], 1)

            def scatter(b):
                wait_apart(pool, s["idx_rdy"], at(1, b, 1), s["passed"])
                for i in range(NT):
                    for k in range(NSCAT // NT):
                        pool.indirect_dma_start(rows, bass.IndirectOffsetOnAxis(idx[:, i, k:k + 1], 0), rowb[:, i, :], None,
                                                bounds_check=LAST_ROW, oob_is_err=False).then_inc(s["scat"], 16)
                pool.wait_ge(s["scat"], at(16 * NSCAT, b, 16 * NSCAT))
                pool.sem_inc(s["row_free"], 1)

            norm1((0, 0))
            if not layer:
                norm1((0, 1))
            split((0, 0), 0)
            if layer:
                norm1((0, 1))
            split((0, 0), 1)
            split((0, 1), 0)
            split((0, 1), 1)
            norm1((1, 0))
            def iteration(items):
                prev, cur, nxt, nn, n3 = items
                if prev:
                    norm2(prev)
                if nn:
                    split(nn, 0)
                if cur:
                    residual(cur)
                if nn:
                    split(nn, 1)
                if n3:
                    norm1(n3)
                if prev:
                    scatter(prev)
                elif layer == 0:
                    pool.wait_ge(c.empty0, 16 * (SLOTS // SPARE - 1 + len(c.spares)))

            deep_pipeline(pool, B, 3, iteration)


def experts0(c, rows, gate_up, down, x, rows_next):
    nc = c.nc
    FC = F0 // 2
    TILES = CAP0 // P
    with ExitStack() as ctx:
        t_ = lambda name, shape, dt=F32: sb(c, ctx, f"e0_{name}", shape, dt)
        names = ("rows_in0", "rows_in1", "weights_in0", "weights_in1", "t_full", "act_evac", "dve_evac",
                 "gu_full", "silu_done", "h_done", "y_full", "y_done", "added", "w_done", "passed", "emptied")
        s = {n: ctx.enter_context(nc.semaphore(f"e0_{n}")) for n in names}
        rows_in, weights_in = (s["rows_in0"], s["rows_in1"]), (s["weights_in0"], s["weights_in1"])
        two = lambda name, shape, dt=F32: [t_(f"{name}{i}", shape, dt) for i in range(2)]
        row = two("row", [P, TILES, W0])
        gu_nat = two("gu_nat", [FC, 4, D])
        dn_nat = two("dn_nat", [P, NC, F0])
        xT = two("xT", [P, NC, CAP0])
        guT = two("guT", [P, NC, 4, FC])
        dnT = two("dnT", [FC, 2, D])
        sg = t_("silu", [FC, 2, CAP0])
        h = t_("h", [FC, 2, CAP0])
        y = two("y", [P, TILES, D])
        wcol, token = two("wcol", [P, TILES]), two("token", [P, TILES], U32)
        bank = [ctx.enter_context(nc.psum_tensor(f"e0_bank{i}", [P, 512], F32)) for i in range(7)]
        x_b, gu_b, dn_b, g_b, u_b, y_b = bank[0], bank[1:3], bank[3], bank[4], bank[5], bank[6]
        at = lambda per, b, extra=0: count(per, b[0], b[1], extra)
        block = ctx.enter_context(nc.Block())

        @block.sync
        def _(sp):
            def load(n):
                par = n[1]
                e = n[0] * 2 + n[1]
                wait_apart(sp, s["t_full"], at(4, n, -4), s["passed"])
                wait_apart(sp, s["w_done"], at(1, n, -1), s["passed"])
                sp.dma_start(gu_nat[par][:, :, :], gate_up[bass.ds(e, 1)].rearrange("o (c f) h -> f (o c) h", f=FC)).then_inc(weights_in[par], 16)
                sp.dma_start(dn_nat[par][:, :, :], down[bass.ds(e, 1)].rearrange("o (c p) f -> p (o c) f", p=P)).then_inc(weights_in[par], 16)
                sp.dma_start(row[par][:, :, :], rows[bass.ds(e * CAP0, CAP0), :].rearrange("(t p) w -> p t w", p=P)).then_inc(rows_in[par], 16)

            def iteration(cur, nxt):
                if nxt:
                    load(nxt)
                if nxt and not isinstance(nxt[0], int) and nxt[1] == 0:
                    sp.dma_start(rows_next[bass.ds(nxt[0] * SPARE, SPARE), :], rows_next[0:SPARE, :]).then_inc(s["emptied"], 16)

            assert E0 // 2 == 2 * SLOTS // SPARE
            pipeline(sp, E0, load, iteration)
            sp.wait_ge(s["emptied"], 16 * (2 * SLOTS // SPARE - 1))

        @block.tensor
        def _(pe):
            def turn(n):
                par = n[1]
                pe.wait_ge(rows_in[par], n[0] * 16 + 16)
                wait(pe, s["dve_evac"], at(2, n, 0))
                for cc in range(NC):
                    for i in range(TILES):
                        last = pe.transpose(x_b[:, cc * CAP0 + i * P:cc * CAP0 + (i + 1) * P],
                                            row[par][:, i, cc * P:(cc + 1) * P], c.ident[:, :])
                last.then_inc(s["t_full"], 1)
                pe.wait_ge(weights_in[par], n[0] * 32 + 32)
                wait(pe, s["act_evac"], at(2, n, 0))
                for cc in range(NC):
                    for q in range(4):
                        last = pe.transpose(gu_b[cc][:, q * FC:(q + 1) * FC], gu_nat[par][:, q, cc * P:(cc + 1) * P], c.ident[0:FC, 0:FC])
                    last.then_inc(s["t_full"], 1)
                for f in range(2):
                    for cc in range(NC):
                        last = pe.transpose(dn_b[0:FC, f * D + cc * P:f * D + (cc + 1) * P],
                                            dn_nat[par][:, cc, f * FC:(f + 1) * FC], c.ident[:, :])
                last.then_inc(s["t_full"], 1)

            def up(b):
                par = b[1]
                pe.wait_ge(s["dve_evac"], at(2, b, 2))
                pe.wait_ge(s["act_evac"], at(2, b, 2))
                wait(pe, s["h_done"], at(1, b, 0))
                for q in range(4):
                    out = (g_b, u_b)[q // 2][0:FC, (q % 2) * CAP0:(q % 2 + 1) * CAP0]
                    for ci in range(NC):
                        last = pe.matmul(out, guT[par][:, ci, q, :], xT[par][:, ci, :], start=ci == 0, stop=ci == NC - 1)
                    if q % 2:
                        last.then_inc(s["gu_full"], 1)

            def down_(b):
                par = b[1]
                pe.wait_ge(s["h_done"], at(1, b, 1))
                wait(pe, s["y_done"], at(1, b, 0))
                for i in range(TILES):
                    for f in range(2):
                        last = pe.matmul(y_b[:, i * D:(i + 1) * D], h[:, f, i * P:(i + 1) * P], dnT[par][:, f, :],
                                         start=f == 0, stop=f == 1)
                last.then_inc(s["y_full"], 1)

            def iteration(cur, nxt):
                up(cur)
                if nxt:
                    turn(nxt)
                down_(cur)

            pipeline(pe, E0, turn, iteration)

        @block.scalar
        def _(act):
            def evac(n):
                par = n[1]
                act.wait_ge(s["t_full"], at(4, n, 2))
                act.activation(guT[par][:, 0, :, :].rearrange("p q f -> p (q f)"), gu_b[0][:, 0:4 * FC], ACT.Copy).then_inc(s["act_evac"], 1)
                act.wait_ge(s["t_full"], at(4, n, 4))
                act.activation(dnT[par][:, :, :].rearrange("p f h -> p (f h)"), dn_b[0:FC, :], ACT.Copy).then_inc(s["act_evac"], 1)

            def silu(b):
                act.wait_ge(s["gu_full"], at(2, b, 1))
                act.activation(sg[:, :, :].rearrange("p f s -> p (f s)"), g_b[0:FC, :], ACT.Silu).then_inc(s["silu_done"], 1)

            def iteration(cur, nxt):
                silu(cur)
                if nxt:
                    evac(nxt)

            pipeline(act, E0, evac, iteration)

        @block.vector
        def _(dve):
            def evac(n):
                par = n[1]
                dve.wait_ge(s["t_full"], at(4, n, 1))
                dve.tensor_copy(xT[par][:, :, :].rearrange("p c s -> p (c s)"), x_b[:, :]).then_inc(s["dve_evac"], 1)
                dve.wait_ge(s["t_full"], at(4, n, 3))
                dve.tensor_copy(guT[par][:, 1, :, :].rearrange("p q f -> p (q f)"), gu_b[1][:, 0:4 * FC]).then_inc(s["dve_evac"], 1)

            def gates(n):
                par = n[1]
                e = n[0] * 2 + n[1]
                dve.wait_ge(rows_in[par], n[0] * 16 + 16)
                wait(dve, s["added"], at(16 * TILES, n, -16 * TILES))
                dve.tensor_copy(token[par][:, :], row[par][:, :, D])
                dve.tensor_copy(wcol[par][:, :].unsqueeze(2), row[par][:, :, bass.ds(e + (D + 1), 1)]).then_inc(s["w_done"], 1)

            def hidden(b):
                dve.wait_ge(s["silu_done"], at(1, b, 1))
                dve.wait_ge(s["gu_full"], at(2, b, 2))
                dve.tensor_tensor(h[:, :, :].rearrange("p f s -> p (f s)"), u_b[0:FC, :],
                                  sg[:, :, :].rearrange("p f s -> p (f s)"), ALU.mult).then_inc(s["h_done"], 1)

            def result(b):
                par = b[1]
                dve.wait_ge(s["w_done"], at(1, b, 1))
                dve.wait_ge(s["y_full"], at(1, b, 1))
                for i in range(TILES):
                    last = dve.tensor_scalar(y[par][:, i, :], y_b[:, i * D:(i + 1) * D], wcol[par][:, i:i + 1],
                                             c.gates[:, 2:3], ALU.mult, ALU.mult)
                last.then_inc(s["y_done"], 1)

            def iteration(cur, nxt):
                hidden(cur)
                if nxt:
                    evac(nxt)
                result(cur)
                if nxt:
                    gates(nxt)

            def prologue(n):
                evac(n)
                gates(n)

            pipeline(dve, E0, prologue, iteration)

        @block.gpsimd
        def _(pool):
            def add(b):
                par = b[1]
                wait_apart(pool, s["added"], at(16 * TILES, b, 0), s["passed"])
                wait_apart(pool, s["y_done"], at(1, b, 1), s["passed"])
                for i in range(TILES):
                    pool.indirect_dma_start(x, bass.IndirectOffsetOnAxis(token[par][:, i:i + 1], 0), y[par][:, i, :], None,
                                            bounds_check=T + SPARE - 1, oob_is_err=True, compute_op=ALU.add).then_inc(s["added"], 16)

            def nothing(n):
                pass

            pipeline(pool, E0, nothing, lambda cur, nxt: add(cur))
            pool.wait_ge(s["added"], 16 * TILES * E0)


def experts1(c, rows, w1, b1, w2, b2, x, tot0, out):
    nc = c.nc
    TILES, HC = CAP1 // P, F1 // P
    HALF = CAP1 // 2
    with ExitStack() as ctx:
        t_ = lambda name, shape, dt=F32: sb(c, ctx, f"e1_{name}", shape, dt)
        two = lambda name, shape, dt=F32: [t_(f"{name}{i}", shape, dt) for i in range(2)]
        names = ("rows_in0", "rows_in1", "weights_in0", "weights_in1", "bias_in", "x_full", "x_evac",
                 "h_full", "act_h", "dve_h", "y_full", "y_evac", "y_done", "added", "picked", "small", "ichain",
                 "copied", "passed")
        s = {n: ctx.enter_context(nc.semaphore(f"e1_{n}")) for n in names}
        rows_in, weights_in = (s["rows_in0"], s["rows_in1"]), (s["weights_in0"], s["weights_in1"])
        row = two("row", [P, TILES, W1])
        w1_s, w2_s = two("w1", [P, NC, F1]), two("w2", [P, HC, D])
        xT = two("xT", [P, NC, CAP1])
        h = two("h", [P, HC, HALF])
        y = two("y", [P, TILES, D])
        b1_s, b2_s = t_("b1", [P, E1, HC]), t_("b2", [P, E1, D])
        b1_e = two("b1_e", [P, HC])
        gidx = t_("gidx", [P, E1, TILES], U32)
        gfl, late = t_("gfl", [P, E1, TILES]), t_("late", [P, E1, TILES])
        gidx_e = two("gidx_e", [P, TILES], U32)
        wcol, token = two("wcol", [P, TILES]), two("token", [P, TILES], U32)
        hb = [ctx.enter_context(nc.psum_tensor(f"e1_h_bank{i}", [P, 512], F32)) for i in range(4)]
        yb = [ctx.enter_context(nc.psum_tensor(f"e1_y_bank{i}", [P, 512], F32)) for i in range(2)]
        xb = ctx.enter_context(nc.psum_tensor("e1_x_bank", [P, 512], F32))
        at = lambda per, b, extra=0: count(per, b[0], b[1], extra)
        block = ctx.enter_context(nc.Block())

        @block.sync
        def _(sp):
            sp.dma_start(b1_s[:, :, :], b1.rearrange("e (c p) -> p e c", p=P), allow_slow_non_contiguous=True).then_inc(s["bias_in"], 16)
            sp.dma_start(b2_s[:, :, :], b2.partition_broadcast(P)).then_inc(s["bias_in"], 16)

            def load(n):
                par = n[1]
                e = n[0] * 2 + n[1]
                wait_apart(sp, s["y_full"], at(4, n, -4), s["passed"])
                sp.dma_start(w1_s[par][:, :, :], w1[bass.ds(e, 1)].rearrange("o (c p) f -> p (o c) f", p=P)).then_inc(weights_in[par], 16)
                sp.dma_start(w2_s[par][:, :, :], w2[bass.ds(e, 1)].rearrange("o (c p) d -> p (o c) d", p=P)).then_inc(weights_in[par], 16)

            def iteration(cur, nxt):
                if nxt:
                    load(nxt)

            pipeline(sp, E1, load, iteration)
            sp.wait_ge(s["added"], 16 * TILES * E1)
            sp.dma_start(out, x[0:T, :]).then_inc(s["copied"], 16)
            sp.wait_ge(s["copied"], 16)

        @block.tensor
        def _(pe):
            def turn(n, k):
                par, cc, hf = n[1], k // 2, k % 2
                if k == 0:
                    pe.wait_ge(rows_in[par], n[0] * (16 * TILES) + 16 * TILES)
                wait(pe, s["x_evac"], at(4, n, k))
                for i in range(4):
                    last = pe.transpose(xb[:, i * P:(i + 1) * P], row[par][:, 4 * hf + i, cc * P:(cc + 1) * P], c.ident[:, :])
                last.then_inc(s["x_full"], 1)

            def up(b, blk, k0, k1):
                par = b[1]
                if k0 == 0 and blk == 0:
                    pe.wait_ge(weights_in[par], b[0] * 32 + 32)
                    pe.wait_ge(s["x_evac"], at(4, b, 4))
                for k in range(k0, k1):
                    q = 8 * blk + k
                    wait(pe, s[("act_h", "dve_h")[q % 2]], at(8, b, q // 2 - 1))
                    for ci in range(NC):
                        last = pe.matmul(hb[q % 4][:, :], w1_s[par][:, ci, k * P:(k + 1) * P],
                                         xT[par][:, ci, blk * HALF:(blk + 1) * HALF], start=ci == 0, stop=ci == NC - 1)
                    last.then_inc(s["h_full"], 1)

            def down(b, blk, nxt=None):
                par = b[1]
                pe.wait_ge(s["act_h"], at(8, b, 4 * blk + 4))
                pe.wait_ge(s["dve_h"], at(8, b, 4 * blk + 4))
                for t in range(2):
                    trip = 2 * blk + t
                    wait(pe, s["y_evac"], at(4, b, trip - 1))
                    for i in range(2):
                        for k in range(HC):
                            last = pe.matmul(yb[t][:, i * D:(i + 1) * D], h[blk][:, k, (2 * t + i) * P:(2 * t + i + 1) * P],
                                             w2_s[par][:, k, :], start=k == 0, stop=k == HC - 1)
                        if i == 1:
                            last.then_inc(s["y_full"], 1)
                        if nxt:
                            turn(nxt, 2 * t + i)

            def prologue(n):
                for k in range(4):
                    turn(n, k)
                up(n, 0, 0, HC)

            def iteration(cur, nxt):
                up(cur, 1, 0, HC)
                down(cur, 0, nxt)
                if nxt:
                    up(nxt, 0, 0, HC)
                down(cur, 1)

            pipeline(pe, E1, prologue, iteration)

        @block.scalar
        def _(act):
            def evac(n, k):
                par, cc, hf = n[1], k // 2, k % 2
                act.wait_ge(s["x_full"], at(4, n, k + 1))
                act.activation(xT[par][:, cc, hf * HALF:(hf + 1) * HALF], xb[:, :], ACT.Copy).then_inc(s["x_evac"], 1)

            def hidden(b, blk, ks):
                par = b[1]
                if blk == 0:
                    act.wait_ge(s["small"], at(1, b, 1))
                for k in ks:
                    q = 8 * blk + k
                    act.wait_ge(s["h_full"], at(16, b, q + 1))
                    act.activation(h[blk][:, k, :], hb[q % 4][:, :], ACT.Relu, bias=b1_e[par][:, k:k + 1]).then_inc(s["act_h"], 1)

            def prologue(n):
                for k in range(4):
                    evac(n, k)
                hidden(n, 0, (0, 2, 4, 6))

            def iteration(cur, nxt):
                hidden(cur, 1, (0, 2, 4, 6))
                if nxt:
                    for k in range(4):
                        evac(nxt, k)
                    hidden(nxt, 0, (0, 2, 4, 6))

            pipeline(act, E1, prologue, iteration)

        @block.vector
        def _(dve):
            full = tot0[:, :].unsqueeze(2).to_broadcast([P, E1, TILES])
            dve.tensor_tensor(late[:, :, :], c.slot_in[:, :, :], full, ALU.is_ge).then_inc(s["ichain"], 1)
            dve.tensor_scalar(gfl[:, :, :], full, -1.0, float(SLOTS), ALU.mult, ALU.add).then_inc(s["ichain"], 1)
            dve.wait_ge(s["ichain"], 2)
            dve.tensor_tensor(gfl[:, :, :], gfl[:, :, :], late[:, :, :], ALU.mult).then_inc(s["ichain"], 1)
            dve.wait_ge(s["ichain"], 3)
            dve.tensor_tensor(gidx[:, :, :], gfl[:, :, :], c.slot_at[:, :, :], ALU.add).then_inc(s["ichain"], 1)
            dve.wait_ge(s["ichain"], 4)
            dve.wait_ge(s["bias_in"], 32)

            def pick(n):
                par = n[1]
                e = n[0] * 2 + n[1]
                wait(dve, s["rows_in" + str(par)], n[0] * (16 * TILES))
                wait(dve, s["act_h"], at(8, n, -8))
                dve.tensor_copy(gidx_e[par][:, :].unsqueeze(1), gidx[:, bass.ds(e, 1), :]).then_inc(s["picked"], 1)
                dve.tensor_copy(b1_e[par][:, :].unsqueeze(1), b1_s[:, bass.ds(e, 1), :]).then_inc(s["small"], 1)

            def gates(n):
                par = n[1]
                e = n[0] * 2 + n[1]
                dve.wait_ge(rows_in[par], n[0] * (16 * TILES) + 16 * TILES)
                wait(dve, s["added"], at(16 * TILES, n, -16 * TILES))
                dve.tensor_copy(token[par][:, :], row[par][:, :, D])
                dve.tensor_scalar(wcol[par][:, :].unsqueeze(2), row[par][:, :, bass.ds(e + (D + 1), 1)],
                                  c.gates[:, 3:4], None, ALU.mult).then_inc(s["picked"], 1)

            def hidden(b, blk, ks):
                par = b[1]
                if blk == 0:
                    dve.wait_ge(s["small"], at(1, b, 1))
                for k in ks:
                    q = 8 * blk + k
                    dve.wait_ge(s["h_full"], at(16, b, q + 1))
                    dve.tensor_scalar(h[blk][:, k, :], hb[q % 4][:, :], b1_e[par][:, k:k + 1], 0.0, ALU.add, ALU.max).then_inc(s["dve_h"], 1)

            def result(b, blk):
                par = b[1]
                e = b[0] * 2 + b[1]
                if blk == 0:
                    dve.wait_ge(s["picked"], at(2, b, 2))
                for t in range(2):
                    trip = 2 * blk + t
                    dve.wait_ge(s["y_full"], at(4, b, trip + 1))
                    ys = y[par][:, 2 * trip:2 * trip + 2, :]
                    dve.tensor_tensor(ys, yb[t][:, :].rearrange("p (t d) -> p t d", t=2),
                                      b2_s[:, bass.ds(e, 1), :].to_broadcast([P, 2, D]), ALU.add).then_inc(s["y_evac"], 1)
                    dve.wait_ge(s["y_evac"], at(4, b, trip + 1))
                    for i in (2 * trip, 2 * trip + 1):
                        dve.tensor_scalar(y[par][:, i, :], y[par][:, i, :], wcol[par][:, i:i + 1], None, ALU.mult).then_inc(s["y_done"], 1)

            def prologue(n):
                pick(n)
                gates(n)
                hidden(n, 0, (1, 3, 5, 7))

            def iteration(cur, nxt):
                if nxt:
                    pick(nxt)
                hidden(cur, 1, (1, 3, 5, 7))
                result(cur, 0)
                if nxt:
                    gates(nxt)
                    hidden(nxt, 0, (1, 3, 5, 7))
                result(cur, 1)

            pipeline(dve, E1, prologue, iteration)

        @block.gpsimd
        def _(pool):
            def gather(n):
                par = n[1]
                wait_apart(pool, s["picked"], at(2, n, 1), s["passed"])
                wait_apart(pool, s["x_full"], at(4, n, -4), s["passed"])
                wait_apart(pool, s["y_done"], at(TILES, n, -TILES), s["passed"])
                for i in range(TILES):
                    pool.indirect_dma_start(row[par][:, i, :], None, rows, bass.IndirectOffsetOnAxis(gidx_e[par][:, i:i + 1], 0),
                                            bounds_check=2 * SLOTS - 1, oob_is_err=True).then_inc(rows_in[par], 16)

            def add(b):
                par = b[1]
                wait_apart(pool, s["added"], at(16 * TILES, b, 0), s["passed"])
                for i in range(TILES):
                    wait_apart(pool, s["y_done"], at(TILES, b, i + 1), s["passed"])
                    pool.indirect_dma_start(x, bass.IndirectOffsetOnAxis(token[par][:, i:i + 1], 0), y[par][:, i, :], None,
                                            bounds_check=T + SPARE - 1, oob_is_err=True, compute_op=ALU.add).then_inc(s["added"], 16)

            def iteration(cur, nxt):
                if nxt:
                    gather(nxt)
                add(cur)

            pipeline(pool, E1, gather, iteration)
            pool.wait_ge(s["added"], 16 * TILES * E1)


def program(nc, a, out, stage=4):
    with ExitStack() as ctx:
        c = Chip(nc, ctx)
        dram = lambda n, shape, dt=F32: nc.dram_tensor(n, shape, dt, kind="Internal").ap()
        x1 = dram("x_after_l0", (T + SPARE, D))
        x3 = dram("x_after_l1", (T + SPARE, D))
        rows0 = dram("rows0", (SLOTS, W0))
        rows1 = dram("rows1", (2 * SLOTS, W1))
        qk_dram = [dram(f"qk_parts{i}", (2, 3, D, S), BF16) for i in range(2)]
        mask_dram = dram("mask_parts", (3, B, S), BF16)
        flat = lambda ap: ap.rearrange("b s d -> (b s) d")
        constants(c, a["g_xattn"], a["g_ffn"], rows0, rows1, x1, x3)
        pre = "L0_xattn_"
        attention(c, 0, flat(a["x"]), flat(a["ctx_1024"]), a["mask_BxS2_ff0"],
                  *(a[pre + n] for n in ("Wq", "bq", "Wk", "bk", "Wv", "bv", "Wp", "bp")),
                  a["L0_ffn_gate_weight"], x1, rows0, qk_dram, mask_dram)
        if stage > 1:
            experts0(c, rows0, a["L0_ffn_gate_up_proj"], a["L0_ffn_down_proj"], x1, rows1)
        if stage > 2:
            pre = "L1_xattn_"
            tot0 = sb(c, ctx, "tot0", [P, E1])
            attention(c, 1, x1, flat(a["ctx_1024"]), a["mask_Bx1xS_if1"].rearrange("b o s -> (b o s)"),
                      *(a[pre + n] for n in ("Wq", "bq", "Wk", "bk", "Wv", "bv", "Wo", "bo")),
                      a["L1_ffn_wg"], x3, rows1, qk_dram, mask_dram, tot0)
        if stage > 3:
            pre = "L1_ffn_"
            experts1(c, rows1, *(a[pre + n] for n in ("w1", "b1", "w2", "b2")), x3, tot0, flat(out))
        if stage < 4:
            with nc.semaphore("dbg") as dbg, nc.Block() as block:
                @block.sync
                def _(sp):
                    sp.dma_start(flat(out), (x3 if stage == 3 else x1)[0:T, :]).then_inc(dbg, 16)
                    sp.wait_ge(dbg, 16)


STAGE = 4


def kernel(**inputs):
    import numpy as np
    import concourse.bacc as bacc
    from concourse.bass_utils import run_bass_kernel_spmd

    nc = bacc.Bacc("TRN2", target_bir_lowering=False, num_devices=1)
    arrays, args = {}, {}
    for name, value in inputs.items():
        a = np.ascontiguousarray(value)
        arrays[f"in_{name}"] = a
        args[name] = nc.dram_tensor(f"in_{name}", a.shape, mybir.dt.from_np(a.dtype), kind="ExternalInput").ap()
    out = nc.dram_tensor("out_x", (B, S, D), F32, kind="ExternalOutput").ap()
    program(nc, args, out, STAGE)
    r = run_bass_kernel_spmd(nc, [arrays], core_ids=[0])
    return r.results[0]["out_x"]
```
